# Optimizing a Trainium2 kernel written in Bass

```python
import numpy as np
import jax
import jax.numpy as jnp

def _softmax(x, axis=-1):
    return jax.nn.softmax(x, axis=axis)

def _gelu(x):
    return jax.nn.gelu(x, approximate=True)

def _silu(x):
    return jax.nn.silu(x)

def _sigmoid(x):
    return jax.nn.sigmoid(x)

def _layernorm(x, axis=-1, eps=1e-05):
    m = jnp.mean(x, axis=axis, keepdims=True)
    v = jnp.var(x, axis=axis, keepdims=True)
    return (x - m) / jnp.sqrt(v + eps)

def _scatter_add(tgt, idx, src, axis=0):
    return tgt.at[idx].add(src)

def _segment_sum(src, seg, n):
    return jax.ops.segment_sum(src, seg, n)
kernel_name = 'mk_flamingo_gated_d1_seqx_r4_5d6da5'

def setup_inputs(seed: int=0):
    np.random.seed(seed)
    _w = jnp.asarray

    def _rec_inputs():
        import jax
        import jax.numpy as jnp
        _rk = jax.random.key(seed)
        x = -0.0002928 + 1 * jax.random.normal(jax.random.fold_in(_rk, 1), (4, 1024, 256), jnp.float32)
        _lenS = 1024 - jax.random.randint(jax.random.fold_in(_rk, 7), (4,), 0, max(1, 1024 // 4) + 1, jnp.int32)
        _lenS2 = 154 - jax.random.randint(jax.random.fold_in(_rk, 8), (4,), 0, max(1, 154 // 4) + 1, jnp.int32)
        _ctx_1024P = jax.random.normal(jax.random.fold_in(_rk, 11), (4, 16, 256), jnp.float32)
        _ctx_1024c = jax.random.dirichlet(jax.random.fold_in(_rk, 511), 0.3 * jnp.ones((16,), jnp.float32), (4, 154))
        _ctx_1024t = jnp.einsum('bsk,bkd->bsd', _ctx_1024c, _ctx_1024P)
        _ctx_1024t = _ctx_1024t * jax.lax.rsqrt(jnp.mean(jnp.square(_ctx_1024t)) + 1e-12) * 0.953939
        ctx_1024 = -0.000292821 + 1.00034 * (_ctx_1024t + 0.3 * jax.random.normal(jax.random.fold_in(_rk, 611), (4, 154, 256), jnp.float32))
        _g = jax.random.normal(jax.random.fold_in(_rk, 9001), (2, 1), jnp.float32)
        _g = jnp.sign(_g) * jnp.maximum(jnp.abs(_g), 1.0) + (_g == 0) * 1.0
        g_xattn = _g[0]
        g_ffn = _g[1]
        return (x, ctx_1024, g_xattn, g_ffn)
    x, ctx_1024, g_xattn, g_ffn = _rec_inputs()

    def _L0_xattn_setup():
        import jax, jax.numpy as jnp
        import numpy as np
        NUM_HEADS = 16
        EMBED = 256
        HEAD = EMBED // NUM_HEADS
        MAX_DIST = 4
        NEG_INF = -1e+30
        key = jax.random.key(seed)
        ks = jax.random.split(key, 8)
        B, S = (2, 512)
        x = jax.random.normal(ks[0], (B, S, EMBED), dtype=jnp.float32)
        return {'k': x, 'v': x, 'q': x, 'Wk': jax.random.normal(ks[1], (EMBED, EMBED), dtype=jnp.float32) * 0.02, 'Wv': jax.random.normal(ks[2], (EMBED, EMBED), dtype=jnp.float32) * 0.02, 'Wq': jax.random.normal(ks[3], (EMBED, EMBED), dtype=jnp.float32) * 0.02, 'Wo': jax.random.normal(ks[4], (EMBED, EMBED), dtype=jnp.float32) * 0.02, 'p_params': jax.random.normal(ks[5], (HEAD, 2 * MAX_DIST + 1), dtype=jnp.float32) * 0.02}
    _L0_xattn_all = _L0_xattn_setup()
    _L0_xattn_in = {k: v for k, v in _L0_xattn_all.items() if k in ('Wk', 'Wv', 'Wq', 'Wo', 'p_params')}
    del _L0_xattn_all

    def _L0_ffn_setup():
        import jax, jax.numpy as jnp
        import numpy as np
        E, H, I = (8, 256, 128)
        NG, TKG, TOPK = (4, 2, 4)
        SCALE = 2.5

        def _mlp(x, wg, wu, wd):
            return jax.nn.silu(x @ wg) * (x @ wu) @ wd
        key = jax.random.key(seed)
        ks = jax.random.split(key, 8)
        s = 0.02
        return {'hidden_states': jax.random.normal(ks[0], (32, 64, H), jnp.float32), 'gate_w': jax.random.normal(ks[1], (E, H), jnp.float32) * np.float32(np.sqrt(2.0 / H)), 'correction_bias': jnp.zeros((E,), jnp.float32), 'Wg': jax.random.normal(ks[2], (E, H, I), jnp.float32) * s, 'Wu': jax.random.normal(ks[3], (E, H, I), jnp.float32) * s, 'Wd': jax.random.normal(ks[4], (E, I, H), jnp.float32) * s, 'Wg_s': jax.random.normal(ks[5], (H, I), jnp.float32) * s, 'Wu_s': jax.random.normal(ks[6], (H, I), jnp.float32) * s, 'Wd_s': jax.random.normal(ks[7], (I, H), jnp.float32) * s}
    _L0_ffn_all = _L0_ffn_setup()
    _L0_ffn_in = {k: v for k, v in _L0_ffn_all.items() if k in ('gate_w', 'correction_bias', 'Wg', 'Wu', 'Wd', 'Wg_s', 'Wu_s', 'Wd_s')}
    del _L0_ffn_all
    return {'x': x, 'ctx_1024': ctx_1024, 'g_xattn': g_xattn, 'g_ffn': g_ffn, 'L0_xattn_Wk': _L0_xattn_in['Wk'], 'L0_xattn_Wv': _L0_xattn_in['Wv'], 'L0_xattn_Wq': _L0_xattn_in['Wq'], 'L0_xattn_Wo': _L0_xattn_in['Wo'], 'L0_xattn_p_params': _L0_xattn_in['p_params'], 'L0_ffn_gate_w': _L0_ffn_in['gate_w'], 'L0_ffn_correction_bias': _L0_ffn_in['correction_bias'], 'L0_ffn_Wg': _L0_ffn_in['Wg'], 'L0_ffn_Wu': _L0_ffn_in['Wu'], 'L0_ffn_Wd': _L0_ffn_in['Wd'], 'L0_ffn_Wg_s': _L0_ffn_in['Wg_s'], 'L0_ffn_Wu_s': _L0_ffn_in['Wu_s'], 'L0_ffn_Wd_s': _L0_ffn_in['Wd_s']}

def reference(x, ctx_1024, g_xattn, g_ffn, L0_xattn_Wk, L0_xattn_Wv, L0_xattn_Wq, L0_xattn_Wo, L0_xattn_p_params, L0_ffn_gate_w, L0_ffn_correction_bias, L0_ffn_Wg, L0_ffn_Wu, L0_ffn_Wd, L0_ffn_Wg_s, L0_ffn_Wu_s, L0_ffn_Wd_s):
    import jax
    import jax.numpy as jnp

    def _L0_xattn_ref(k, v, q, Wk, Wv, Wq, Wo, p_params):
        import jax, jax.numpy as jnp
        import numpy as np
        NUM_HEADS = 16
        EMBED = 256
        HEAD = EMBED // NUM_HEADS
        MAX_DIST = 4
        NEG_INF = -1e+30
        B, Kl, _ = k.shape
        Ql = q.shape[1]
        kh = (k @ Wk.T).reshape(B, Kl, NUM_HEADS, HEAD).transpose(0, 2, 1, 3)
        vh = (v @ Wv.T).reshape(B, Kl, NUM_HEADS, HEAD).transpose(0, 2, 1, 3)
        qh = (q @ Wq.T).reshape(B, Ql, NUM_HEADS, HEAD).transpose(0, 2, 1, 3)
        qh = qh / jnp.sqrt(jnp.float32(HEAD))
        scores0 = jnp.einsum('bhqd,bhkd->bhqk', qh, kh)
        bias = jnp.einsum('bhqd,dr->bhqr', qh, p_params)
        d = jnp.clip(jnp.arange(Ql)[:, None] - jnp.arange(Kl)[None, :], -MAX_DIST, MAX_DIST) + MAX_DIST
        rel = bias[:, :, jnp.arange(Ql)[:, None], d]
        scores = scores0 + rel
        causal = jnp.arange(Ql)[:, None] >= jnp.arange(Kl)[None, :]
        scores = jnp.where(causal[None, None], scores, NEG_INF)
        attn = jax.nn.softmax(scores, axis=-1)
        out = jnp.einsum('bhqk,bhkd->bhqd', attn, vh)
        out = out.transpose(0, 2, 1, 3).reshape(B, Ql, EMBED)
        return out @ Wo.T

    def _L0_ffn_ref(hidden_states, gate_w, correction_bias, Wg, Wu, Wd, Wg_s, Wu_s, Wd_s):
        import jax, jax.numpy as jnp
        import numpy as np
        E, H, I = (8, 256, 128)
        NG, TKG, TOPK = (4, 2, 4)
        SCALE = 2.5

        def _mlp(x, wg, wu, wd):
            return jax.nn.silu(x @ wg) * (x @ wu) @ wd
        B, T, _ = hidden_states.shape
        x = hidden_states.reshape(-1, H)
        N = x.shape[0]
        logits = x @ gate_w.T
        scores = jax.nn.sigmoid(logits)
        scores_c = scores + correction_bias
        grp = scores_c.reshape(N, NG, E // NG)
        group_scores = jnp.sum(jax.lax.top_k(grp, 2)[0], axis=-1)
        grp_idx = jax.lax.top_k(group_scores, TKG)[1]
        group_mask = jnp.zeros_like(group_scores).at[jnp.arange(N)[:, None], grp_idx].set(1.0)
        score_mask = jnp.repeat(group_mask, E // NG, axis=-1) > 0.5
        scores_for_choice = jnp.where(score_mask, scores_c, 0.0)
        topk_idx = jax.lax.top_k(scores_for_choice, TOPK)[1]
        topk_w = jnp.take_along_axis(scores, topk_idx, axis=-1)
        topk_w = topk_w / (jnp.sum(topk_w, axis=-1, keepdims=True) + 1e-20)
        topk_w = topk_w * SCALE
        cw = jnp.sum(jax.nn.one_hot(topk_idx, E, dtype=topk_w.dtype) * topk_w[..., None], axis=1)
        g = jnp.einsum('nh,ehi->eni', x, Wg)
        u = jnp.einsum('nh,ehi->eni', x, Wu)
        y = jnp.einsum('eni,eih->enh', jax.nn.silu(g) * u, Wd)
        routed = jnp.einsum('enh,ne->nh', y, cw)
        out = routed + _mlp(x, Wg_s, Wu_s, Wd_s)
        return out.reshape(B, T, H)
    x = x + jnp.tanh(g_xattn[0]) * _L0_xattn_ref(ctx_1024, ctx_1024, _layernorm(x, axis=-1), L0_xattn_Wk, L0_xattn_Wv, L0_xattn_Wq, L0_xattn_Wo, L0_xattn_p_params)
    x = x + jnp.tanh(g_ffn[0]) * _L0_ffn_ref(_layernorm(x, axis=-1), L0_ffn_gate_w, L0_ffn_correction_bias, L0_ffn_Wg, L0_ffn_Wu, L0_ffn_Wd, L0_ffn_Wg_s, L0_ffn_Wu_s, L0_ffn_Wd_s)
    return x

_drawn_inputs = setup_inputs


def setup_inputs(seed=0):
    import zlib

    import numpy as np

    out = dict(_drawn_inputs(seed))
    spreads = {'L0_ffn_correction_bias': (0.0, 0.8)}
    factors = {'L0_xattn_Wk': 8.0,
     'L0_xattn_Wq': 8.0,
     'L0_xattn_p_params': 182.311,
     'L0_ffn_gate_w': 5.189,
     'L0_ffn_Wg': 3.804,
     'L0_ffn_Wu': 3.768,
     'L0_ffn_Wd': 3.77,
     'L0_ffn_Wg_s': 5.138,
     'L0_ffn_Wu_s': 5.026,
     'L0_ffn_Wd_s': 5.05}
    for name, (base, spread) in spreads.items():
        noise = np.random.default_rng([zlib.crc32(name.encode()), seed]).standard_normal(out[name].shape)
        drawn = base * np.exp(spread * noise) if base else spread * noise
        out[name] = jnp.asarray(drawn.astype(out[name].dtype))
    for name, factor in factors.items():
        out[name] = (out[name] * factor).astype(out[name].dtype)
    return out
```

```python
from contextlib import ExitStack

import concourse.bass as bass
import numpy as np
from concourse import mybir

F32 = mybir.dt.float32
F32R = mybir.dt.float32r
ALU = mybir.AluOpType
ACT = mybir.ActivationFunctionType
AX_X = mybir.AxisListType.X

P = 128
B, S, D = 4, 1024, 256
KL = 154
K1 = KL - P
KPAD = 160
H, HD = 16, 16
DIST = 4
E, I = 8, 128
NT = S // P
C = D // P
HALF = 512
NSTK = H // 2
PAIR = 2 * KL
SW = PAIR + 2 * DIST
NG = H // 4
SCALE = HD ** -0.5
EPS = 1e-5
NEG = -1e30
NE1 = E + 1
ROUTE_SCALE = 2.5

CONST = {}
_at = 0
for _name, _width in (("ident", P), ("odd", 2), ("rot", 16), ("band0", P), ("causal0", P), ("band1", 32),
                      ("causal1", 32), ("head", H), ("mhalf", 8), ("eps", 8), ("expert", E + 1),
                      ("lower4", 16), ("lower8", E * E), ("two", 4), ("four", 8), ("zero", 8)):
    CONST[_name] = (_at, _at + _width)
    _at += _width
NCONST = _at


def constants():
    c = np.zeros((P, NCONST), np.float32)
    p = np.arange(P)[:, None]

    def put(name, value):
        lo, hi = CONST[name]
        c[:, lo:hi] = value

    put("ident", np.eye(P))
    put("odd", (p // HD) % 2 == np.arange(2)[None])
    r, j = np.divmod(np.arange(16)[None], 4)
    put("rot", (p - r) % 4 == j)
    k = np.arange(P)[None]
    put("band0", (p - k >= 0) & (p - k < DIST))
    put("causal0", np.where(k > p, NEG, 0))
    k = np.arange(32)[None] - DIST
    put("band1", (p - k >= 0) & (p - k < DIST))
    put("causal1", np.where(k > p, NEG, 0))
    put("head", p % H == np.arange(H)[None])
    put("mhalf", -0.5)
    put("eps", EPS)
    e = np.arange(E + 1)[None]
    put("expert", ((p % E == e) & (p < 2 * E)) | ((e == E) & (p == 2 * E)))
    for name, n in (("lower4", 4), ("lower8", E)):
        a, b = np.divmod(np.arange(n * n)[None], n)
        put(name, b < a)
    put("two", 2)
    put("four", 4)
    return c


def attention(nc, ctx, x1, tg, t):
    def sb(name, shape, dt=F32):
        return ctx.enter_context(nc.sbuf_tensor(name, shape, dt))

    def sem(name):
        return ctx.enter_context(nc.semaphore(name))

    cst = sb("cst", [P, NCONST])

    def con(name, p0=0, p1=P):
        lo, hi = CONST[name]
        return cst[p0:p1, lo:hi]

    gates = sb("gates", [P, 2])
    wqh, wql = sb("wqh", [P, C, D], F32R), sb("wql", [P, C, D], F32R)
    wk, wv = sb("wk", [P, C, D]), sb("wv", [P, C, D])
    wo = sb("wo", [P, NG, D])
    rel = sb("rel", [P, 2 * DIST + 1])
    reld = sb("reld", [P, DIST])
    relm = sb("relm", [P, 2, DIST])
    relh, rell = sb("relh", [P, 2, DIST], F32R), sb("rell", [P, 2, DIST], F32R)
    ctxb = sb("ctxb", [P, C, KPAD])
    stats, mv = sb("stats", [P, NT, 6]), sb("mv", [P, NT, 2])
    veps, rstd = sb("veps", [P, NT]), sb("rstd", [P, NT])
    xn = sb("xn", [P, NT // 2, D])
    xth, xtl = sb("xth", [P, C, S], F32R), sb("xtl", [P, C, S], F32R)
    qh, ql = sb("qh", [P, C, S], F32R), sb("ql", [P, C, S], F32R)
    kp = sb("kp", [P, C, KL])
    kh, kl = sb("kh", [P, C, 2, KL], F32R), sb("kl", [P, C, 2, KL], F32R)
    km = sb("km", [P, NSTK, SW], F32R)
    k2 = sb("k2", [P, NSTK, P], F32R)
    qs = sb("qs", [P, NSTK, S], F32R)
    va = sb("va", [P, H, 32])
    vb = sb("vb", [P, NG, 4, 32])
    sx = sb("sx", [P, 2, NSTK, SW])
    relc, rotc, relr = sb("relc", [P, H, DIST]), sb("rotc", [P, H, 4, DIST]), sb("relr", [P, H, 4])
    d0, d1 = sb("d0", [P, H, P]), sb("d1", [P, H, 32])
    tp = sb("tp", [P, H, 32])
    mx, nm = sb("mx", [P, NT, H]), sb("nm", [P, NT, 2 * H])
    mt = sb("mt", [2 * H, HALF], F32R)
    NEB = 10
    ex = sb("ex", [P, NEB, HALF])
    den = sb("den", [P, HALF])
    at = sb("at", [P, NG, HALF])
    wq = at[:, 0, :].rearrange("p (c d) -> p c d", c=C)

    W = [ctx.enter_context(nc.psum_tensor(f"work{i}", [P, HALF], F32)) for i in range(2)]
    SM = [ctx.enter_context(nc.psum_tensor(f"smax{i}", [P, HALF], F32)) for i in range(2)]
    ST = [ctx.enter_context(nc.psum_tensor(f"sT{i}", [P, HALF], F32)) for i in range(2)]
    OT = [ctx.enter_context(nc.psum_tensor(f"oT{i}", [P, HALF], F32)) for i in range(2)]

    x_in, w_in, c_in = sem("x_in"), sem("w_in"), sem("ctx_in")
    const_set, pool_set, wq_set, rel_step = sem("const_set"), sem("pool_set"), sem("wq_set"), sem("rel_step")
    rel_set = sem("rel_set")
    waited = sem("waited")
    g_set = sem("g_set")
    stat_s, mv_s, veps_s, rstd_s, xn_s = sem("stat"), sem("mv"), sem("veps"), sem("rstd"), sem("xn")
    xT_ps, xT_hi, work_free = sem("xT_ps"), sem("xT_hi"), sem("work_free")
    k_ps, kp_s, kh_s, v_ps = sem("k_ps"), sem("kp"), sem("kh"), sem("v_ps")
    kl_s = sem("kl")
    q_ps, q_hi = sem("q_ps"), sem("q_hi")
    ks_in, k2_s = sem("kstack_in"), sem("k2")
    qs_in = [sem("qstack0_in"), sem("qstack1_in")]
    ms_in = [sem("mstack0_in"), sem("mstack1_in")]
    sm_ps, sx_s, mx_s = sem("scores_ps"), sem("sx"), sem("mx")
    relc_s, d_s, sadd_s, sub_s = sem("relc"), sem("d"), sem("sadd"), sem("sub")
    nmh_s, nm_s, mT_ps, mT_s = sem("nm_hi"), sem("nm"), sem("mT_ps"), sem("mT")
    st_ps, exp_s, pv_ps = sem("sT_ps"), sem("exp"), sem("pv_ps")
    den_s, rden_s, at_s, y_ps = sem("den"), sem("rden"), sem("at"), sem("y_ps")

    NWORK = 16
    NITEM = 40
    NK_DMA = NQ_DMA = 6
    from_one = {"pe": (st_ps, q_ps, xT_ps, pv_ps, y_ps, sm_ps), "act": (exp_s,), "pool": (d_s, k2_s),
                "dve": (work_free, at_s, mx_s, sadd_s)}
    block = ctx.enter_context(nc.Block())

    @block.sync
    def _(sp):
        sp.dma_start(x1[:, 0:NT, :], t["x"][0]).then_inc(x_in, 16)
        for dst, src in ((cst[:], t["cst"]), (rel[:], t["rel"]), (gates[:], t["gates"]), (at[:, 0, :], t["wq"].rearrange("p c d -> p (c d)")), (wk[:], t["wk"]),
                         (wv[:], t["wv"]), (wo[:], t["wo"])):
            sp.dma_start(dst, src).then_inc(w_in, 16)
        sp.dma_start(ctxb[:], t["ctx"][0]).then_inc(c_in, 16)

        def stacks(b):
            sp.wait_ge(kh_s, 2 * (b + 1))
            sp.wait_ge(kl_s, 2 * (b + 1))
            sp.nop().then_inc(waited, 1)
            sp.wait_ge(st_ps, 1 + NITEM * b)
            for r, src in enumerate((kh, kh, kl)):
                for c in range(C):
                    for i in range(4):
                        sp.dma_start(km[32 * r:32 * r + 32, 4 * c + i, 0:PAIR].bitcast(F32),
                                     src[32 * i:32 * i + 32, c, :, :].rearrange("p j k -> p (j k)").bitcast(F32)).then_inc(ks_in, 16)
            for half in range(2):
                n = slice(half * HALF, (half + 1) * HALF)
                sp.wait_ge(work_free, 1 + NWORK * b + 8 + 2 * half)
                for r, src in enumerate((qh, ql, qh)):
                    for c in range(C):
                        for i in range(4):
                            sp.dma_start(qs[32 * r:32 * r + 32, 4 * c + i, n].bitcast(F32),
                                         src[32 * i:32 * i + 32, c, n].bitcast(F32)).then_inc(qs_in[half], 16)
            for half in range(2):
                n = slice(HALF // 2 if half == 0 else HALF, (half + 1) * HALF)
                sp.wait_ge(mT_s, 2 * b + half + 1)
                for i in range(NSTK):
                    sp.dma_start(qs[96:128, i, n].bitcast(F32), mt[:, n.start - half * HALF:HALF].bitcast(F32)).then_inc(ms_in[half], 16)

        with sp.Fori(0, B - 1) as b:
            sp.wait_ge(x_in, 16 * (b + 1))
            sp.nop().then_inc(waited, 1)
            sp.dma_start(x1[:, bass.ds((b + 1) * NT, NT), :], t["x"][b + 1]).then_inc(x_in, 16)
            sp.wait_ge(v_ps, b + 1)
            sp.nop().then_inc(waited, 1)
            sp.dma_start(ctxb[:], t["ctx"][b + 1]).then_inc(c_in, 16)
            stacks(b)
        stacks(B - 1)

    @block.gpsimd
    def _(pool):
        for s in from_one["pool"]:
            pool.sem_inc(s, 1)
        nc.gpsimd.memset(va[:], 0.0).then_inc(pool_set, 1)
        nc.gpsimd.memset(vb[:], 0.0).then_inc(pool_set, 1)
        nc.gpsimd.memset(tp[:], 0.0).then_inc(pool_set, 1)
        nc.gpsimd.memset(k2[:].bitcast(F32), 0.0).then_inc(pool_set, 1)
        pool.wait_ge(w_in, 7 * 16)
        with pool.Fori(0, B) as b:
            pool.wait_ge(mv_s, NT * (b + 1))
            nc.gpsimd.tensor_tensor(veps[:], mv[:, :, 1], con("eps"), ALU.add).then_inc(veps_s, 1)
            pool.wait_ge(veps_s, b + 1)
            nc.gpsimd.tensor_tensor(rstd[:], veps[:], con("mhalf"), ALU.pow).then_inc(rstd_s, 1)
            pool.wait_ge(ks_in, 16 * 24 * (b + 1))
            pool.nop().then_inc(waited, 1)
            for par in range(2):
                src = km[:, par::2, 0:PAIR].rearrange("p s (j k) -> p s j k", j=2)[:, :, :, P:KL]
                dst = k2[:, par::2, :].rearrange("p s (q k) -> p s q k", q=4)[:, :, 2 * par:2 * par + 2, 0:K1]
                nc.gpsimd.tensor_copy(dst, src).then_inc(k2_s, 1)
            for i, (dt, band, causal, width) in enumerate(((d0, "band0", "causal0", P), (d1, "band1", "causal1", 32))):
                n = 6 * b + 3 * i
                pool.wait_ge(sx_s, 16 * b + 8 * (i + 1))
                if i == 0:
                    pool.wait_ge(sadd_s, 1 + 4 * b)
                pool.wait_ge(d_s, 1 + 4 * b + 2 * i)
                pool.nop().then_inc(waited, 1)
                src = sx[:, i, :, PAIR:SW].rearrange("p s (j d) -> p s j d", j=2)
                nc.gpsimd.tensor_copy(relc[:].rearrange("p (s j) d -> p s j d", j=2), src).then_inc(relc_s, 1)
                pool.wait_ge(relc_s, 2 * b + i + 1)
                rot = con("rot").rearrange("p (r d) -> p r d", r=4).unsqueeze(1).broadcast_to([P, H, 4, DIST])
                nc.gpsimd.tensor_tensor(rotc[:], relc[:].unsqueeze(2).broadcast_to([P, H, 4, DIST]), rot,
                                        ALU.mult).then_inc(rel_step, 1)
                pool.wait_ge(rel_step, n + 1)
                nc.gpsimd.tensor_tensor(rotc[:, :, :, 0:2], rotc[:, :, :, 0:2], rotc[:, :, :, 2:4],
                                        ALU.add).then_inc(rel_step, 1)
                pool.wait_ge(rel_step, n + 2)
                nc.gpsimd.tensor_tensor(relr[:], rotc[:, :, :, 0], rotc[:, :, :, 1], ALU.add).then_inc(rel_step, 1)
                pool.wait_ge(rel_step, n + 3)
                nc.gpsimd.tensor_tensor(
                    dt[:].rearrange("p h (a r) -> p h a r", r=4),
                    relr[:].unsqueeze(2).broadcast_to([P, H, width // 4, 4]),
                    con(band).rearrange("p (a r) -> p a r", r=4).unsqueeze(1).broadcast_to([P, H, width // 4, 4]),
                    ALU.mult).then_inc(d_s, 1)
                pool.wait_ge(d_s, 1 + 4 * b + 2 * i + 1)
                nc.gpsimd.tensor_tensor(dt[:], dt[:], con(causal).unsqueeze(1).broadcast_to([P, H, width]),
                                        ALU.add).then_inc(d_s, 1)

    @block.scalar
    def _(act):
        for s in from_one["act"]:
            act.sem_inc(s, 1)
        act.wait_ge(w_in, 7 * 16)
        nc.scalar.activation(tg[:], gates[:], ACT.Tanh).then_inc(g_set, 1)
        nc.scalar.mul(wqh[:], wq, SCALE).then_inc(wq_set, 1)
        nc.scalar.copy(km[96:128, :, 0:PAIR].rearrange("p s (j k) -> p s j k", j=2),
                       con("head", 96, 128).rearrange("p (s j) -> p s j", j=2).unsqueeze(3)
                       .broadcast_to([32, NSTK, 2, KL])).then_inc(const_set, 1)
        nc.scalar.copy(km[96:128, :, PAIR:SW], cst[96:128, 0:1].unsqueeze(1).broadcast_to([32, NSTK, 2 * DIST]))\
            .then_inc(const_set, 1)
        act.wait_ge(rel_set, 3)
        for r, src in enumerate((relh, relh, rell)):
            nc.scalar.copy(km[32 * r:32 * r + 32, :, PAIR:SW],
                           src[0:32, :, :].rearrange("p j d -> p (j d)").unsqueeze(1).broadcast_to([32, NSTK, 2 * DIST]))\
                .then_inc(const_set, 1)
        with act.Fori(0, B) as b:
            for i in range(4):
                half, c = divmod(i, C)
                act.wait_ge(xT_ps, 1 + 4 * b + i + 1)
                if i == 0:
                    act.wait_ge(q_ps, 1 + 4 * b)
                nc.scalar.copy(xth[:, c, half * HALF:(half + 1) * HALF], W[i % 2][:]).then_inc(xT_hi, 1)
            act.wait_ge(kp_s, b + 1)
            act.wait_ge(k2_s, 1 + 2 * b)
            for j in range(2):
                nc.scalar.mul(kh[:, :, j, :], kp[:], con("odd")[:, j:j + 1]).then_inc(kh_s, 1)
            for i in range(4):
                half, c = divmod(i, C)
                act.wait_ge(q_ps, 1 + 4 * b + i + 1)
                if i == 0:
                    act.wait_ge(sm_ps, 1 + 64 * b)
                nc.scalar.copy(qh[:, c, half * HALF:(half + 1) * HALF], W[i % 2][:]).then_inc(q_hi, 1)
            act.wait_ge(st_ps, 1 + NITEM * b)
            for i in range(2):
                for s in range(NSTK):
                    act.wait_ge(sm_ps, 1 + 64 * b + 8 * i + s + 1)
                    nc.scalar.copy(sx[:, i, s, :], SM[s % 2][:, 0:SW]).then_inc(sx_s, 1)
            for half in range(2):
                for g in range(NG):
                    act.wait_ge(pv_ps, 1 + 8 * b + max(0, 4 * half + g - 1))
                    for i in range(5):
                        n = (4 * half + g) * 5 + i
                        q0 = P if half == 0 and i == 4 else 0
                        act.wait_ge(st_ps, 1 + NITEM * b + n + 1)
                        nc.scalar.activation(ex[:, (g % 2) * 5 + i, q0:HALF], ST[n % 2][:, q0:HALF],
                                             ACT.Exp).then_inc(exp_s, 1)

    @block.vector
    def _(dve):
        for s in from_one["dve"]:
            dve.sem_inc(s, 1)
        dve.wait_ge(pool_set, 4)
        nc.vector.memset(va[:, :, HD:HD + 1], 1.0)
        for j in range(4):
            nc.vector.memset(vb[32 * j:32 * j + K1, :, j, HD:HD + 1], 1.0)
        dve.wait_ge(w_in, 7 * 16)
        dve.wait_ge(wq_set, 1)
        nc.vector.scalar_tensor_tensor(wql[:], wq, SCALE, wqh[:], ALU.mult, ALU.subtract).then_inc(wq_set, 1)
        nc.vector.tensor_scalar(reld[:], rel[:, DIST:2 * DIST], rel[:, 2 * DIST:], None, ALU.subtract)\
            .then_inc(rel_set, 1)
        dve.wait_ge(rel_set, 1)
        for j in range(2):
            nc.vector.tensor_scalar(relm[:, j, :], reld[:], con("odd")[:, j:j + 1], None, ALU.mult)
            last = nc.vector.tensor_scalar(relh[:, j, :], reld[:], con("odd")[:, j:j + 1], None, ALU.mult)
        last.then_inc(rel_set, 1)
        dve.wait_ge(rel_set, 2)
        nc.vector.tensor_tensor(rell[:], relm[:], relh[:], ALU.subtract).then_inc(rel_set, 1)
        with dve.Fori(0, B) as b:
            dve.wait_ge(x_in, 16 * (b + 1))
            for i in range(NT):
                nc.vector.bn_stats(stats[:, i, :], x1[:, b * NT + i, :]).then_inc(stat_s, 1)
            dve.wait_ge(stat_s, NT * (b + 1))
            dve.nop().then_inc(waited, 1)
            for i in range(NT):
                nc.vector.bn_aggr(mv[:, i, :], stats[:, i, :]).then_inc(mv_s, 1)
            dve.wait_ge(rstd_s, b + 1)
            for i in range(NT):
                if i % 4 == 0:
                    dve.wait_ge(xT_ps, 1 + 4 * b + i // 2)
                nc.vector.tensor_scalar(xn[:, i % 4, :], x1[:, b * NT + i, :], mv[:, i, 0:1], rstd[:, i:i + 1],
                                        ALU.subtract, ALU.mult).then_inc(xn_s, 1)
                if i % 4 < 3:
                    continue
                half = i // 4
                n = slice(half * HALF, (half + 1) * HALF)
                for c in range(C):
                    dve.wait_ge(xT_hi, 4 * b + 2 * half + c + 1)
                    nc.vector.tensor_tensor(xtl[:, c, n], W[c][:], xth[:, c, n], ALU.subtract).then_inc(work_free, 1)
            dve.wait_ge(k_ps, b + 1)
            nc.vector.tensor_scalar(kp[:], W[0][:, 0:2 * KL].rearrange("p (c k) -> p c k", c=C), rel[:, 2 * DIST:],
                                    None, ALU.add).then_inc(kp_s, 1)
            dve.wait_ge(kp_s, b + 1)
            nc.vector.nop().then_inc(work_free, 1)
            for j in range(2):
                dve.wait_ge(kh_s, 2 * b + j + 1)
                nc.vector.scalar_tensor_tensor(kl[:, :, j, :], kp[:], con("odd")[:, j:j + 1], kh[:, :, j, :],
                                               ALU.mult, ALU.subtract).then_inc(kl_s, 1)
            dve.wait_ge(v_ps, b + 1)
            dve.wait_ge(pv_ps, 1 + 8 * b)
            nc.vector.tensor_copy(va[:, :, 0:HD], W[1][:, 0:D].rearrange("p (h d) -> p h d", h=H))
            for j in range(4):
                last = nc.vector.tensor_copy(vb[32 * j:32 * j + 32, :, j, 0:HD],
                                             W[1][32 * j:32 * j + 32, D:D + 64].rearrange("p (g d) -> p g d", g=NG))
            last.then_inc(work_free, 1)
            for i in range(4):
                half, c = divmod(i, C)
                n = slice(half * HALF, (half + 1) * HALF)
                dve.wait_ge(q_hi, 4 * b + i + 1)
                nc.vector.tensor_tensor(ql[:, c, n], W[i % 2][:], qh[:, c, n], ALU.subtract).then_inc(work_free, 1)
            heads0 = sx[:, 0, :, 0:PAIR].rearrange("p s (j k) -> p s j k", j=2)
            heads1 = sx[:, 1, :, 0:PAIR].rearrange("p s (j k) -> p s j k", j=2)

            def by_stack(ap):
                return ap.rearrange("p (s j) k -> p s j k", j=2)

            def over(ap, n):
                return ap.rearrange("p (s j) -> p s j", j=2).unsqueeze(3).broadcast_to([P, NSTK, 2, n])

            dve.wait_ge(d_s, 1 + 4 * b + 2)
            nc.vector.tensor_tensor(heads0[:, :, :, 0:P], heads0[:, :, :, 0:P], by_stack(d0[:]), ALU.add)\
                .then_inc(sadd_s, 1)
            dve.wait_ge(sadd_s, 1 + 4 * b + 1)
            nc.vector.reduce_max(mx[:, 0, :], heads0[:, :, :, 0:P], AX_X).then_inc(sadd_s, 1)
            dve.wait_ge(sadd_s, 1 + 4 * b + 2)
            nc.vector.tensor_tensor(heads0[:, :, :, 0:P], heads0[:, :, :, 0:P], over(mx[:, 0, :], P), ALU.subtract)\
                .then_inc(sub_s, 1)
            dve.wait_ge(d_s, 1 + 4 * b + 4)
            nc.vector.tensor_tensor(heads1[:, :, :, P - DIST:KL], heads1[:, :, :, P - DIST:KL],
                                    by_stack(d1[:, :, 0:K1 + DIST]), ALU.add).then_inc(sadd_s, 1)
            dve.wait_ge(sadd_s, 1 + 4 * b + 3)
            nc.vector.reduce_max(mx[:, 1, :], heads1, AX_X).then_inc(sadd_s, 1)
            dve.wait_ge(sadd_s, 1 + 4 * b + 4)
            nc.vector.tensor_tensor(heads1[:, :, :, 0:P], heads1[:, :, :, 0:P], over(mx[:, 1, :], P), ALU.subtract)\
                .then_inc(sub_s, 1)
            nc.vector.tensor_tensor(by_stack(tp[:, :, 0:K1]), heads1[:, :, :, P:KL], over(mx[:, 1, :], K1),
                                    ALU.subtract).then_inc(sub_s, 1)
            for i in range(2, NT):
                for s in range(NSTK):
                    dve.wait_ge(sm_ps, 1 + 64 * b + 8 * i + s + 1)
                    nc.vector.reduce_max(mx[:, i, 2 * s:2 * s + 2],
                                         SM[s % 2][:, 0:PAIR].rearrange("p (j k) -> p j k", j=2), AX_X).then_inc(mx_s, 1)
                if i in (3, 7):
                    half = i // 4
                    r = slice(2 + 2 * half, i + 1)
                    dve.wait_ge(mx_s, 1 + 48 * b + 8 * (i - 1))
                    nc.vector.tensor_scalar(nm[:, r, 0:H].bitcast(F32R), mx[:, r, :], -1.0, None, ALU.mult).then_inc(nmh_s, 1)
                    dve.wait_ge(nmh_s, 2 * b + half + 1)
                    nc.vector.scalar_tensor_tensor(nm[:, r, H:2 * H], mx[:, r, :], -1.0, nm[:, r, 0:H],
                                                   ALU.mult, ALU.subtract).then_inc(nm_s, 1)
            for half in range(2):
                q0 = HALF // 2 if half == 0 else 0
                dve.wait_ge(mT_ps, 2 * b + half + 1)
                if half == 0:
                    dve.wait_ge(st_ps, 1 + NITEM * b)
                else:
                    dve.wait_ge(ms_in[0], 16 * NSTK * (b + 1))
                nc.vector.tensor_copy(mt[:, q0:HALF], W[half][0:32, q0:HALF]).then_inc(mT_s, 1)
                dve.wait_ge(mT_s, 2 * b + half + 1)
                nc.vector.nop().then_inc(work_free, 1)

            def normalise(n):
                half, g = divmod(n, NG)
                dve.wait_ge(pv_ps, 1 + 8 * b + n + 1)
                dve.wait_ge(at_s, 1 + 8 * b + n)
                dve.nop().then_inc(waited, 1)
                nc.vector.stream_shuffle(den[:], OT[n % 2][:], [HD] * 32).then_inc(den_s, 1)
                dve.wait_ge(den_s, 8 * b + n + 1)
                nc.vector.reciprocal(den[:], den[:]).then_inc(rden_s, 1)
                dve.wait_ge(rden_s, 8 * b + n + 1)
                if g == 0:
                    dve.wait_ge(y_ps, 1 + 4 * b + 2 * half)
                nc.vector.tensor_tensor(at[:, g, :], OT[n % 2][:], den[:], ALU.mult).then_inc(at_s, 1)

            def residual(half):
                for pr in range(2):
                    u = 12 + 2 * half + pr
                    dve.wait_ge(y_ps, 1 + 4 * b + 2 * half + pr + 1)
                    dve.wait_ge(g_set, 1)
                    tile = b * NT + 4 * half + 2 * pr
                    xs = x1[:, bass.ds(tile, 2), :]
                    nc.vector.scalar_tensor_tensor(xs, W[u % 2][:].rearrange("p (t d) -> p t d", t=2), tg[:, 0:1], xs,
                                                   ALU.mult, ALU.add).then_inc(work_free, 1)

            for n in range(8):
                normalise(n)
                if n == 4:
                    residual(0)
            residual(1)

    @block.tensor
    def _(pe):
        for s in from_one["pe"]:
            pe.sem_inc(s, 1)
        pe.wait_ge(w_in, 7 * 16)
        pe.wait_ge(wq_set, 2)
        pe.wait_ge(const_set, 5)
        ident = con("ident")
        with pe.Fori(0, B) as b:
            def work(n):
                pe.wait_ge(work_free, 1 + NWORK * b + max(0, n - 1))
                return W[n % 2]

            for i in range(4):
                half, c = divmod(i, C)
                w = work(i)
                pe.wait_ge(xn_s, NT * b + 4 * (half + 1))
                for j in range(4):
                    last = nc.tensor.transpose(w[:, j * P:(j + 1) * P], xn[:, j, c * P:(c + 1) * P], ident)
                last.then_inc(xT_ps, 1)
            pe.wait_ge(c_in, 16 * (b + 1))
            w = work(4)
            for m in range(C):
                for c in range(C):
                    last = nc.tensor.matmul(w[:, m * KL:(m + 1) * KL], wk[:, c, m * P:(m + 1) * P], ctxb[:, c, 0:KL],
                                            start=(c == 0), stop=(c == C - 1))
            last.then_inc(k_ps, 1)
            w = work(5)
            for c in range(C):
                nc.tensor.matmul(w[:, 0:D], ctxb[:, c, 0:P], wv[:, c, :], start=(c == 0), stop=(c == C - 1))
            for j in range(4):
                for c in range(C):
                    last = nc.tensor.matmul(w[32 * j:32 * j + 32, D:D + 64], ctxb[:, c, P:KPAD],
                                            wv[:, c, :].rearrange("p (g j d) -> p g j d", g=NG, j=4)[:, :, j, :],
                                            start=(c == 0), stop=(c == C - 1))
            last.then_inc(v_ps, 1)
            for i in range(4):
                half, m = divmod(i, C)
                n = slice(half * HALF, (half + 1) * HALF)
                w = work(6 + i)
                pe.wait_ge(work_free, 1 + NWORK * b + 2 * (half + 1))
                steps = [(wa, xa, c) for c in range(C) for wa, xa in ((wql, xth), (wqh, xtl), (wqh, xth))]
                for k, (wa, xa, c) in enumerate(steps):
                    last = nc.tensor.matmul(w[:], wa[:, c, m * P:(m + 1) * P], xa[:, c, n],
                                            start=(k == 0), stop=(k == len(steps) - 1))
                last.then_inc(q_ps, 1)
            pe.wait_ge(ks_in, 16 * 24 * (b + 1))
            for i in range(NT):
                if i in (0, 4):
                    pe.wait_ge(qs_in[i // 4], 16 * 24 * (b + 1))
                for s in range(NSTK):
                    n = NSTK * i + s
                    width = SW if i < 2 else PAIR
                    if n < 2:
                        pe.wait_ge(mx_s, 1 + 48 * b)
                    elif n - 2 < 16:
                        pe.wait_ge(sx_s, 16 * b + n - 1)
                    else:
                        pe.wait_ge(mx_s, 1 + 48 * b + n - 17)
                    nc.tensor.matmul(SM[n % 2][:, 0:width], qs[0:96, s, i * P:(i + 1) * P], km[0:96, s, 0:width],
                                     start=True, stop=True).then_inc(sm_ps, 1)
            for half in range(2):
                w = work(10 + half)
                pe.wait_ge(nm_s, 2 * b + half + 1)
                for j in range(2 - 2 * half, 4):
                    last = nc.tensor.transpose(w[0:32, j * P:(j + 1) * P], nm[:, 4 * half + j, :], ident)
                last.then_inc(mT_ps, 1)

            def score(n, i):
                half, g = divmod(n, NG)
                item = 5 * n + i
                pe.wait_ge(exp_s, 1 + NITEM * b + max(0, item - 1))
                if i == 0 and g == 0:
                    pe.wait_ge(ms_in[half], 16 * NSTK * (b + 1))
                    if half == 0:
                        pe.wait_ge(sub_s, 3 * (b + 1))
                        pe.wait_ge(k2_s, 1 + 2 * (b + 1))
                out = ST[item % 2]
                q0 = HALF // 2 if half == 0 else 0
                q = slice(half * HALF + q0, (half + 1) * HALF)
                if i < 4:
                    s, j = divmod(4 * g + i, 2)
                    if half == 0:
                        for k in range(2):
                            nc.tensor.transpose(out[:, k * P:(k + 1) * P], sx[:, k, s, j * KL:j * KL + P], ident)
                    last = nc.tensor.matmul(out[:, q0:HALF], km[:, s, j * KL:j * KL + P], qs[:, s, q], start=True, stop=True)
                else:
                    if half == 0:
                        nc.tensor.transpose(out[:, P:2 * P], tp[:, 4 * g:4 * g + 4, :].rearrange("p h k -> p (h k)"), ident)
                    for k in range(2):
                        last = nc.tensor.matmul(out[:, q0:HALF], k2[:, 2 * g + k, :], qs[:, 2 * g + k, q],
                                                start=(k == 0), stop=(k == 1))
                last.then_inc(st_ps, 1)

            def values(n, part):
                half, g = divmod(n, NG)
                pe.wait_ge(exp_s, 1 + NITEM * b + 5 * n + (4 if part == 0 else 5))
                if part == 0:
                    pe.wait_ge(at_s, 1 + 8 * b + max(0, n - 1))
                q0 = P if half == 0 and part == 1 else 0
                for j in range(4):
                    e = (g % 2) * 5 + (j if part == 0 else 4)
                    v = va[:, 4 * g + j, :] if part == 0 else vb[:, g, j, :]
                    last = nc.tensor.matmul(OT[n % 2][32 * j:32 * j + 32, q0:HALF], v, ex[:, e, q0:HALF],
                                            start=(part == 0), stop=(part == 1))
                if part == 1:
                    last.then_inc(pv_ps, 1)

            def project(half):
                pe.wait_ge(at_s, 1 + 8 * b + 4 * (half + 1))
                for pr in range(2):
                    w = work(12 + 2 * half + pr)
                    for k in range(2):
                        j = 2 * pr + k
                        for g in range(NG):
                            last = nc.tensor.matmul(w[:, k * D:(k + 1) * D], at[:, g, j * P:(j + 1) * P], wo[:, g, :],
                                                    start=(g == 0), stop=(g == NG - 1))
                    last.then_inc(y_ps, 1)

            for n in range(8):
                for i in range(5):
                    score(n, i)
                    if n and i == 1:
                        values(n - 1, 0)
                    if n and i == 3:
                        values(n - 1, 1)
                if n == 5:
                    project(0)
            values(7, 0)
            values(7, 1)
            project(1)


def experts(nc, ctx, x1, tg, t, out):
    def sb(name, shape, dt=F32):
        return ctx.enter_context(nc.sbuf_tensor(name, shape, dt))

    def sem(name):
        return ctx.enter_context(nc.semaphore(name))

    TB = HALF // P
    NBLK = B * S // HALF
    NR = 2 * E + 1
    XW = 2 * C * I + D

    cst = sb("cst2", [P, NCONST])

    def con(name, p0=0, p1=P):
        lo, hi = CONST[name]
        return cst[p0:p1, lo:hi]

    bias = sb("bias", [P, E])
    gw = sb("gw", [P, C, E])
    gwh, gwl = sb("gwh", [P, C, E], F32R), sb("gwl", [P, C, E], F32R)
    gst = sb("gst", [P, C, P], F32R)
    wx = sb("wx", [P, NE1, XW])
    wxh, wxl = sb("wxh", [P, NE1, XW], F32R), sb("wxl", [P, NE1, XW], F32R)
    selr = sb("selr", [NR, NE1, P], F32R)
    stats, mv = sb("stats2", [P, TB, 6]), sb("mv2", [P, TB, 2])
    veps, rstd = sb("veps2", [P, TB]), sb("rstd2", [P, TB])
    xn = sb("xn2", [P, TB, D])
    xh, xl = sb("x2h", [P, 2, C, HALF], F32R), sb("x2l", [P, 2, C, HALF], F32R)
    lgT = sb("lgT", [2 * E, HALF])
    sc = sb("sc", [P, TB, E])
    scc = sb("scc", [P, TB, E])
    gs = sb("gs", [P, TB, E // 2])
    g_gt, g_eq = sb("g_gt", [P, TB, 4, 4]), sb("g_eq", [P, TB, 4, 4])
    rank_g, rank_e = sb("rank_g", [P, TB, 4]), sb("rank_e", [P, TB, E])
    vch = sb("vch", [P, TB, E])
    e_gt, e_eq = sb("e_gt", [P, TB, E, E]), sb("e_eq", [P, TB, E, E])
    wsel = sb("wsel", [P, TB, E])
    winv = sb("winv", [P, TB])
    cw = sb("cw", [P, TB, E])
    cwc = sb("cwc", [P, TB, NR])
    cwt = sb("cwt", [NR, 2, HALF], F32R)
    R = 3
    sg = sb("sg", [P, R, HALF])
    hf = sb("hf", [P, R, HALF])
    hh, hl = sb("hh", [P, R, HALF], F32R), sb("hl", [P, R, HALF], F32R)

    def bank(name):
        return ctx.enter_context(nc.psum_tensor(name, [P, HALF], F32))

    PG, PU = [bank("pg0"), bank("pg1")], [bank("pu0"), bank("pu1")]
    PC, PM = bank("pc"), bank("pm")
    PY = [bank("py0"), bank("py1")]

    w_in, c_in = [sem(f"wx_in{e}") for e in range(NE1)], sem("const_in")
    w_hi, w_lo, gst_s, tab_s = sem("wx_hi"), sem("wx_lo"), sem("router_set"), sem("tables_set")
    stat_s, mv_s, veps_s, rstd_s, xn_s = sem("stat_b"), sem("mv_b"), sem("veps_b"), sem("rstd_b"), sem("xn_b")
    t_ps, t_hi, misc_free = sem("xT_ps_b"), sem("xT_hi_b"), sem("misc_free")
    gl_ps, lgT_s, lg_ps, sc_s = sem("router_ps"), sem("router_out"), sem("logits_ps"), sem("scores_set")
    route, ct_ps = sem("route_step"), sem("cwT_ps")
    sg_s, gu_ps, gu_free, cb_ps, h_done = sem("silu_set"), sem("gate_up_ps"), sem("gate_up_free"), sem("cw_ps"), sem("hidden_done")
    waited = sem("waited_b")
    hh_s, hl_done, hid_free = sem("hidden_hi"), sem("hidden_lo_done"), sem("hidden_free")
    fin_s, out_s, y_ps = sem("fin"), sem("out_stored"), sem("y_ps_b")
    block = ctx.enter_context(nc.Block())
    RG = 2
    PER = 2 * NE1
    NROUTE = 20

    LAST = NBLK // 2 - 1

    def turns(eng, item):
        item(0, 0, False)
        item(0, 1, False)
        with eng.Fori(0, LAST) as k:
            for i in range(2, PER + 2):
                item(k, i, False)
        for i in range(2, PER):
            item(LAST, i, True)

    def place(k, i, last):
        return 2 * k + i // NE1, i % NE1, not (last and i >= NE1)

    @block.sync
    def _(sp):
        for dst, src in ((cst[:], t["cst"]), (bias[:], t["bias"]), (gw[:], t["gw"])):
            sp.dma_start(dst, src).then_inc(c_in, 16)
        for e in range(NE1):
            sp.dma_start(wx[:, e, :], t["wx"][:, e, :]).then_inc(w_in[e], 16)
        with sp.Fori(0, NBLK) as n:
            sp.wait_ge(fin_s, 2 * (n + 1))
            sp.nop().then_inc(waited, 1)
            sp.dma_start(out[n], x1[:, bass.ds(n * TB, TB), :]).then_inc(out_s, 16)
        sp.wait_ge(out_s, 16 * NBLK)

    @block.gpsimd
    def _(pool):
        nc.gpsimd.memset(gst[:].bitcast(F32), 0.0).then_inc(gst_s, 1)
        nc.gpsimd.memset(cwc[:], 1.0).then_inc(gst_s, 1)
        pool.sem_inc(hl_done, R)
        pool.wait_ge(c_in, 3 * 16)

        def rstd_of(n):
            pool.wait_ge(mv_s, TB * (n + 1))
            nc.gpsimd.tensor_tensor(veps[:], mv[:, :, 1], con("eps")[:, 0:TB], ALU.add).then_inc(veps_s, 1)
            pool.wait_ge(veps_s, n + 1)
            nc.gpsimd.tensor_tensor(rstd[:], veps[:], con("mhalf")[:, 0:TB], ALU.pow).then_inc(rstd_s, 1)

        def hidden_lo(k, i):
            m = PER * k + i
            pool.wait_ge(hh_s, m + 1)
            pool.wait_ge(hid_free, m + 1)
            nc.gpsimd.tensor_tensor(hl[:, i % R, :], hf[:, i % R, :], hh[:, i % R, :], ALU.subtract).then_inc(hl_done, 1)

        def item(k, i, last):
            n, e, ahead = place(k, i, last)
            hidden_lo(k, i)
            if ahead and e == 0:
                rstd_of(n + 1)

        rstd_of(0)
        turns(pool, item)

    @block.scalar
    def _(act):
        act.sem_inc(misc_free, 1)
        act.wait_ge(c_in, 3 * 16)
        nc.scalar.copy(gwh[:], gw[:]).then_inc(tab_s, 1)
        nc.scalar.copy(selr[:], cst[0:NR, CONST["expert"][0]:CONST["expert"][1]].unsqueeze(2)
                       .broadcast_to([NR, NE1, P])).then_inc(tab_s, 1)

        def x_hi(n, slot):
            if not (isinstance(n, int) and n == 0):
                act.wait_ge(gu_ps, 1 + NE1 * (n - 1))
            for c in range(C):
                act.wait_ge(t_ps, 2 * n + c + 1)
                nc.scalar.copy(xh[:, slot, c, :], PM[:]).then_inc(t_hi, 1)

        def scores(n):
            act.wait_ge(lg_ps, n + 1)
            act.wait_ge(route, NROUTE * n)
            nc.scalar.activation(sc[:], PM[:, 0:TB * E].rearrange("p (t e) -> p t e", t=TB), ACT.Sigmoid)\
                .then_inc(sc_s, 1)

        def silu(k, i):
            m = PER * k + i
            act.wait_ge(gu_ps, 1 + m + 1)
            act.wait_ge(h_done, m + 1)
            nc.scalar.activation(sg[:, i % R, :], PG[i % RG][:], ACT.Silu).then_inc(sg_s, 1)

        def hidden_hi(k, i):
            m = PER * k + i
            act.wait_ge(h_done, m + R + 1)
            act.wait_ge(hid_free, m + 1)
            nc.scalar.copy(hh[:, i % R, :], hf[:, i % R, :]).then_inc(hh_s, 1)

        def item(k, i, last):
            n, e, ahead = place(k, i, last)
            if not (last and i == PER - 1):
                silu(k, i + 1)
            hidden_hi(k, i)
            if ahead and e == 2:
                x_hi(n + 1, (i // NE1 + 1) % 2)
            if ahead and e == 4:
                scores(n + 1)

        x_hi(0, 0)
        for e in range(NE1):
            act.wait_ge(w_in[e], 16)
            nc.scalar.copy(wxh[:, e, :], wx[:, e, :]).then_inc(w_hi, 1)
            if e == 1:
                scores(0)
        silu(0, 0)
        turns(act, item)

    @block.vector
    def _(dve):
        dve.sem_inc(gu_free, RG)
        dve.sem_inc(h_done, R)
        dve.wait_ge(c_in, 3 * 16)
        dve.wait_ge(tab_s, 1)
        nc.vector.tensor_tensor(gwl[:], gw[:], gwh[:], ALU.subtract).then_inc(tab_s, 1)
        dve.wait_ge(tab_s, 3)
        dve.wait_ge(gst_s, 2)
        nc.vector.tensor_copy(gst[:, :, 0:E], gwh[:].bitcast(F32))
        nc.vector.tensor_copy(gst[:, :, E:2 * E], gwl[:].bitcast(F32)).then_inc(gst_s, 1)

        def norm_stats(n):
            for i in range(TB):
                nc.vector.bn_stats(stats[:, i, :], x1[:, n * TB + i, :]).then_inc(stat_s, 1)
            dve.wait_ge(stat_s, TB * (n + 1))
            dve.nop().then_inc(waited, 1)
            for i in range(TB):
                nc.vector.bn_aggr(mv[:, i, :], stats[:, i, :]).then_inc(mv_s, 1)

        def normalised(n):
            dve.wait_ge(rstd_s, n + 1)
            dve.wait_ge(t_ps, 2 * n)
            for i in range(TB):
                nc.vector.tensor_scalar(xn[:, i, :], x1[:, n * TB + i, :], mv[:, i, 0:1], rstd[:, i:i + 1],
                                        ALU.subtract, ALU.mult).then_inc(xn_s, 1)

        def x_lo(n, slot):
            for c in range(C):
                dve.wait_ge(t_hi, 2 * n + c + 1)
                nc.vector.tensor_tensor(xl[:, slot, c, :], PM[:], xh[:, slot, c, :], ALU.subtract).then_inc(misc_free, 1)

        def router_out(n):
            dve.wait_ge(gl_ps, n + 1)
            dve.wait_ge(lg_ps, n)
            nc.vector.tensor_copy(lgT[:], PM[0:2 * E, :]).then_inc(misc_free, 1)

        def routing(n, part):
            at = [0 if part == 0 else 8]

            def step(ins):
                ins.then_inc(route, 1)
                at[0] += 1
                dve.wait_ge(route, NROUTE * n + at[0])

            def along(ap, axis, shape):
                return ap.unsqueeze(axis).broadcast_to(shape)

            def lower(k):
                return con(f"lower{k}").rearrange("p (a b) -> p a b", a=k).unsqueeze(1).broadcast_to([P, TB, k, k])

            tt = nc.vector.tensor_tensor
            if part == 0:
                dve.wait_ge(sc_s, n + 1)
                step(tt(scc[:], sc[:], bias[:].unsqueeze(1).broadcast_to([P, TB, E]), ALU.add))
                step(tt(gs[:], scc[:, :, 0::2], scc[:, :, 1::2], ALU.add))
                sh = [P, TB, 4, 4]
                step(tt(g_gt[:], along(gs[:], 2, sh), along(gs[:], 3, sh), ALU.is_gt))
                step(tt(g_eq[:], along(gs[:], 2, sh), along(gs[:], 3, sh), ALU.is_equal))
                step(tt(g_eq[:], g_eq[:], lower(4), ALU.mult))
                step(tt(g_gt[:], g_gt[:], g_eq[:], ALU.add))
                step(nc.vector.reduce_sum(rank_g[:], g_gt[:], AX_X))
                step(nc.vector.scalar_tensor_tensor(
                    vch[:].rearrange("p t (g j) -> p t g j", j=2), along(rank_g[:], 3, [P, TB, 4, 2]), 2.0,
                    scc[:].rearrange("p t (g j) -> p t g j", j=2), ALU.is_lt, ALU.mult))
            else:
                sh = [P, TB, E, E]
                step(tt(e_gt[:], along(vch[:], 2, sh), along(vch[:], 3, sh), ALU.is_gt))
                step(tt(e_eq[:], along(vch[:], 2, sh), along(vch[:], 3, sh), ALU.is_equal))
                step(tt(e_eq[:], e_eq[:], lower(E), ALU.mult))
                step(tt(e_gt[:], e_gt[:], e_eq[:], ALU.add))
                step(nc.vector.reduce_sum(rank_e[:], e_gt[:], AX_X))
                step(nc.vector.scalar_tensor_tensor(wsel[:], rank_e[:], 4.0, sc[:], ALU.is_lt, ALU.mult))
                step(nc.vector.reduce_sum(winv[:], wsel[:], AX_X))
                step(nc.vector.tensor_scalar(winv[:], winv[:], 1e-20, 1.0 / ROUTE_SCALE, ALU.add, ALU.mult))
                step(nc.vector.reciprocal(winv[:], winv[:]))
                step(tt(cw[:], wsel[:], along(winv[:], 2, [P, TB, E]), ALU.mult))
                dve.wait_ge(ct_ps, n)
                step(nc.vector.tensor_scalar(cwc[:, :, 0:E].bitcast(F32R), cw[:], 1.0, None, ALU.mult))
                step(tt(cwc[:, :, E:2 * E], cw[:], cwc[:, :, 0:E], ALU.subtract))

        def weights_in(n, slot):
            dve.wait_ge(ct_ps, n + 1)
            if not (isinstance(n, int) and n == 0):
                dve.wait_ge(cb_ps, 1 + NE1 * (n - 1))
            nc.vector.tensor_copy(cwt[:, slot, :], PM[0:NR, :]).then_inc(misc_free, 1)

        def product(k, i):
            m = PER * k + i
            dve.wait_ge(sg_s, m + 1)
            nc.vector.tensor_tensor(sg[:, i % R, :], PU[i % RG][:], sg[:, i % R, :], ALU.mult).then_inc(gu_free, 1)
            dve.wait_ge(gu_free, m + RG + 1)
            dve.wait_ge(cb_ps, 1 + m + 1)
            dve.wait_ge(hl_done, m + 1)
            nc.vector.tensor_tensor(hf[:, i % R, :], PC[:], sg[:, i % R, :], ALU.mult).then_inc(h_done, 1)

        def residual(n):
            for pr in range(2):
                if pr == 0:
                    dve.wait_ge(y_ps, n + 1)
                else:
                    dve.wait_ge(hid_free, NE1 * (n + 1) + R)
                xs = x1[:, bass.ds(n * TB + 2 * pr, 2), :]
                nc.vector.scalar_tensor_tensor(xs, PY[pr][:].rearrange("p (t d) -> p t d", t=2), tg[:, 1:2], xs,
                                               ALU.mult, ALU.add).then_inc(fin_s, 1)

        def item(k, i, last):
            n, e, ahead = place(k, i, last)
            slot = (i // NE1 + 1) % 2
            product(k, i)
            if e == 1 and i >= NE1:
                residual(n - 1)
            if ahead and e == 0:
                norm_stats(n + 1)
            if ahead and e == 1:
                normalised(n + 1)
            if ahead and e == 2:
                x_lo(n + 1, slot)
            if ahead and e == 3:
                router_out(n + 1)
            if ahead and e == 4:
                routing(n + 1, 0)
            if ahead and e == 5:
                routing(n + 1, 1)
            if ahead and e == 6:
                weights_in(n + 1, slot)

        norm_stats(0)
        normalised(0)
        x_lo(0, 0)
        router_out(0)
        for e in range(NE1):
            dve.wait_ge(w_hi, e + 1)
            nc.vector.tensor_tensor(wxl[:, e, :], wx[:, e, :], wxh[:, e, :], ALU.subtract).then_inc(w_lo, 1)
            if e == 3:
                routing(0, 0)
                routing(0, 1)
                weights_in(0, 0)
        turns(dve, item)
        residual(NBLK - 1)

    @block.tensor
    def _(pe):
        pe.sem_inc(hid_free, R)
        pe.sem_inc(gu_ps, 1)
        pe.sem_inc(cb_ps, 1)
        pe.wait_ge(tab_s, 3)
        ident = con("ident")
        pe.wait_ge(gst_s, 3)

        def split3(a, b):
            return ((a[0], b[1]), (a[1], b[0]), (a[0], b[0]))

        def transposes(n):
            for c in range(C):
                pe.wait_ge(misc_free, 4 * n + c + 1)
                if c == 0:
                    pe.wait_ge(xn_s, TB * (n + 1))
                for j in range(TB):
                    last = nc.tensor.transpose(PM[:, j * P:(j + 1) * P], xn[:, j, c * P:(c + 1) * P], ident)
                last.then_inc(t_ps, 1)

        def router(n, slot):
            pe.wait_ge(misc_free, 4 * n + 3)
            for c in range(C):
                for k, xa in enumerate((xl, xh)):
                    last = nc.tensor.matmul(PM[:], gst[:, c, :], xa[:, slot, c, :], start=(c == 0 and k == 0),
                                            stop=(c == C - 1 and k == 1))
            last.then_inc(gl_ps, 1)

        def logits(n):
            pe.wait_ge(misc_free, 4 * n + 4)
            for j in range(TB):
                last = nc.tensor.matmul(PM[:, j * E:(j + 1) * E], lgT[:, j * P:(j + 1) * P],
                                        con("expert", 0, 2 * E)[:, 0:E], start=True, stop=True)
            last.then_inc(lg_ps, 1)

        def weights_T(n):
            pe.wait_ge(sc_s, n + 1)
            pe.wait_ge(route, NROUTE * (n + 1))
            for j in range(TB):
                last = nc.tensor.transpose(PM[0:NR, j * P:(j + 1) * P], cwc[:, j, :], ident)
            last.then_inc(ct_ps, 1)

        def gate_up(k, i):
            m = PER * k + i
            u, e = divmod(i % PER, NE1)
            pe.wait_ge(gu_free, m + 1)
            pe.wait_ge(w_lo, e + 1)
            for o, out_ in ((0, PG[i % RG]), (C * I, PU[i % RG])):
                first = True
                for c in range(C):
                    w = slice(o + c * I, o + (c + 1) * I)
                    for wa, xa in split3((wxh, wxl), (xh, xl)):
                        last = nc.tensor.matmul(out_[:], wa[:, e, w], xa[:, u, c, :], start=first,
                                                stop=(c == C - 1 and wa is wxh and xa is xh))
                        first = False
            last.then_inc(gu_ps, 1)

        def weight(k, i):
            m = PER * k + i
            u, e = divmod(i % PER, NE1)
            pe.wait_ge(h_done, m + R)
            if e == 0:
                pe.wait_ge(misc_free, 4 * (2 * k + i // NE1 + 1) + 1)
            nc.tensor.matmul(PC[:], selr[:, e, :], cwt[:, u, :], start=True, stop=True).then_inc(cb_ps, 1)

        def down(k, i):
            m = PER * k + i
            n, e = 2 * k + i // NE1, i % NE1
            pe.wait_ge(hl_done, m + R + 1)
            if e == 0:
                pe.wait_ge(fin_s, 2 * n)
            for j in range(TB):
                q = slice(j * P, (j + 1) * P)
                y = PY[j // 2][:, (j % 2) * D:(j % 2 + 1) * D]
                for s, (ha, wa) in enumerate(split3((hh, hl), (wxh, wxl))):
                    last = nc.tensor.matmul(y, ha[:, i % R, q], wa[:, e, 2 * C * I:XW],
                                            start=(e == 0 and s == 0 and j % 2 == 0), stop=(e == NE1 - 1 and s == 2),
                                            skip_group_check=True)
                if j == TB - 1:
                    last.then_inc(hid_free, 1)
                elif e == NE1 - 1 and j == 1:
                    last.then_inc(y_ps, 1)

        def item(k, i, last):
            n, e, ahead = place(k, i, last)
            if not (last and i + 2 >= PER):
                gate_up(k, i + 2)
                weight(k, i + 2)
            down(k, i)
            if ahead and e == 1:
                transposes(n + 1)
            if ahead and e == 2:
                router(n + 1, (i // NE1 + 1) % 2)
            if ahead and e == 3:
                logits(n + 1)
            if ahead and e == 5:
                weights_T(n + 1)

        transposes(0)
        router(0, 0)
        logits(0)
        gate_up(0, 0)
        weights_T(0)
        weight(0, 0)
        gate_up(0, 1)
        weight(0, 1)
        turns(pe, item)


def program(nc, t, out):
    with ExitStack() as outer:
        x1 = outer.enter_context(nc.sbuf_tensor("x1", [P, B * NT, D], F32))
        tg = outer.enter_context(nc.sbuf_tensor("tg", [P, 2], F32))
        with ExitStack() as ctx:
            attention(nc, ctx, x1, tg, t)
        with ExitStack() as ctx:
            experts(nc, ctx, x1, tg, t, out)


def kernel(x, ctx_1024, g_xattn, g_ffn, L0_xattn_Wk, L0_xattn_Wv, L0_xattn_Wq, L0_xattn_Wo, L0_xattn_p_params,
           L0_ffn_gate_w, L0_ffn_correction_bias, L0_ffn_Wg, L0_ffn_Wu, L0_ffn_Wd, L0_ffn_Wg_s, L0_ffn_Wu_s,
           L0_ffn_Wd_s):
    from concourse import bacc
    from concourse.bass_utils import run_bass_kernel_spmd

    def rows(w):
        return w.reshape(C, P, -1).transpose(1, 0, 2)

    f = np.float32
    ctx_t = np.zeros((B, P, C, KPAD), f)
    ctx_t[..., :KL] = np.asarray(ctx_1024).transpose(0, 2, 1).reshape(B, C, P, KL).transpose(0, 2, 1, 3)
    wo = np.zeros((NG, 4, 32, D), f)
    wo[:, :, :HD] = np.asarray(L0_xattn_Wo).T.reshape(NG, 4, HD, D)
    wx = np.zeros((P, NE1, 2 * C * I + D), f)
    for at, many, one in ((0, L0_ffn_Wg, L0_ffn_Wg_s), (C * I, L0_ffn_Wu, L0_ffn_Wu_s)):
        for e in range(NE1):
            w = np.asarray(many)[e] if e < E else np.asarray(one)
            wx[:, e, at:at + C * I] = rows(w).reshape(P, C * I)
    wx[:, :E, 2 * C * I:] = np.asarray(L0_ffn_Wd).transpose(1, 0, 2)
    wx[:, E, 2 * C * I:] = np.asarray(L0_ffn_Wd_s)
    arrays = {
        "x": np.asarray(x).reshape(B * S, D),
        "ctx": ctx_t,
        "cst": constants(),
        "rel": np.tile(np.asarray(L0_xattn_p_params), (P // HD, 1)),
        "gates": np.tile(np.concatenate([np.asarray(g_xattn), np.asarray(g_ffn)])[None], (P, 1)),
        "wq": rows(np.asarray(L0_xattn_Wq).T),
        "wk": rows(np.asarray(L0_xattn_Wk).T),
        "wv": rows(np.asarray(L0_xattn_Wv).T),
        "wo": wo.transpose(1, 2, 0, 3).reshape(P, NG, D),
        "bias": np.tile(np.asarray(L0_ffn_correction_bias)[None], (P, 1)),
        "gw": rows(np.asarray(L0_ffn_gate_w).T),
        "wx": wx,
    }
    arrays = {"in_" + name: np.ascontiguousarray(a) for name, a in arrays.items()}
    nc = bacc.Bacc("TRN2", target_bir_lowering=False, num_devices=1)
    t = {name[3:]: nc.dram_tensor(name, a.shape, F32, kind="ExternalInput").ap() for name, a in arrays.items()}
    t["x"] = t["x"].rearrange("(b t p) d -> b p t d", b=B, p=P)
    out = nc.dram_tensor("out", (B * S, D), F32, kind="ExternalOutput").ap()
    program(nc, t, out.rearrange("(n t p) d -> n p t d", n=B * S // HALF, p=P))
    result = run_bass_kernel_spmd(nc, [arrays], core_ids=[0])
    return result.results[0]["out"].reshape(B, S, D)
```

```python
from contextlib import ExitStack

import concourse.bass as bass
import numpy as np
from concourse import mybir

F32 = mybir.dt.float32
F32R = mybir.dt.float32r
ALU = mybir.AluOpType
ACT = mybir.ActivationFunctionType
AX_X = mybir.AxisListType.X

P = 128
B, S, D = 4, 1024, 256
KL = 154
K1 = KL - P
KPAD = 160
H, HD = 16, 16
DIST = 4
E, I = 8, 128
NT = S // P
C = D // P
HALF = 512
NSTK = H // 2
PAIR = 2 * KL
SW = PAIR + 2 * DIST
NG = H // 4
SCALE = HD ** -0.5
EPS = 1e-5
NEG = -1e30
NE1 = E + 1
ROUTE_SCALE = 2.5

CONST = {}
_at = 0
for _name, _width in (("odd", 2), ("rot", 16), ("band0", P), ("band1", 32), ("causal1", 32), ("head", H),
                      ("mhalf", 4), ("eps", 4), ("strip", 4), ("ident", P), ("causal0", P), ("expert", E + 1),
                      ("lower4", 16), ("lower8", E * E)):
    CONST[_name] = (_at, _at + _width)
    _at += _width
NKEPT = CONST["ident"][0]
NCONST = _at


def constants():
    c = np.zeros((P, NCONST), np.float32)
    p = np.arange(P)[:, None]

    def put(name, value):
        lo, hi = CONST[name]
        c[:, lo:hi] = value

    put("ident", np.eye(P))
    put("odd", (p // HD) % 2 == np.arange(2)[None])
    r, j = np.divmod(np.arange(16)[None], 4)
    put("rot", (p - r) % 4 == j)
    k = np.arange(P)[None]
    put("band0", (p - k >= 0) & (p - k < DIST))
    put("causal0", np.where(k > p, NEG, 0))
    k = np.arange(32)[None] - DIST
    put("band1", (p - k >= 0) & (p - k < DIST))
    put("causal1", np.where(k > p, NEG, 0))
    put("head", p % H == np.arange(H)[None])
    put("mhalf", -0.5)
    put("eps", EPS)
    e = np.arange(E + 1)[None]
    put("expert", ((p % E == e) & (p < 2 * E)) | ((e == E) & (p == 2 * E)))
    for name, n in (("lower4", 4), ("lower8", E)):
        a, b = np.divmod(np.arange(n * n)[None], n)
        put(name, b < a)
    put("strip", p // 32 == np.arange(4)[None])
    return c


def attention(nc, ctx, x1, tg, t):
    def sb(name, shape, dt=F32):
        return ctx.enter_context(nc.sbuf_tensor(name, shape, dt))

    def sem(name):
        return ctx.enter_context(nc.semaphore(name))

    cst = sb("cst", [P, NKEPT])

    def con(name, p0=0, p1=P):
        lo, hi = CONST[name]
        return cst[p0:p1, lo:hi]

    TU = NT // 2
    gates = sb("gates", [P, 2])
    wqh, wql = sb("wqh", [P, C, D], F32R), sb("wql", [P, C, D], F32R)
    wk, wv = sb("wk", [P, C, D]), sb("wv", [P, C, D])
    wo = sb("wo", [P, NG, D])
    rel = sb("rel", [P, 2 * DIST + 1])
    reld = sb("reld", [P, DIST])
    relm = sb("relm", [P, 2, DIST])
    relh, rell = sb("relh", [P, 2, DIST], F32R), sb("rell", [P, 2, DIST], F32R)
    idr, cmask = sb("idr", [P, P], F32R), sb("cmask", [P, P], F32R)
    ctxb = sb("ctxb", [P, C, KPAD])
    stats, mv = sb("stats", [P, TU, 6]), sb("mv", [P, TU, 2])
    veps, rstd = sb("veps", [P, TU]), sb("rstd", [P, TU])
    xn = sb("xn", [P, TU, D])
    xth, xtl = sb("xth", [P, C, HALF], F32R), sb("xtl", [P, C, HALF], F32R)
    qh, ql = sb("qh", [P, C, HALF], F32R), sb("ql", [P, C, HALF], F32R)
    kp = sb("kp", [P, C, KL])
    kh, kl = sb("kh", [P, C, 2, KL], F32R), sb("kl", [P, C, 2, KL], F32R)
    km = sb("km", [96, NSTK, SW], F32R)
    ks = sb("ks", [P, NSTK, PAIR], F32R)
    k2 = sb("k2", [P, NSTK, P], F32R)
    qs = sb("qs", [P, NSTK, S], F32R)
    vs = sb("vs", [P, D + 64])
    va = sb("va", [P, H, 32])
    vb = sb("vb", [P, NG, 4, 32])
    sx = sb("sx", [P, 2, NSTK, SW])
    relc, rotc, relr = sb("relc", [P, H, DIST]), sb("rotc", [P, H, 4, DIST]), sb("relr", [P, H, 4])
    d0, d1 = sb("d0", [P, H, P]), sb("d1", [P, H, 32])
    tp = sb("tp", [P, H, 32])
    mx, nm = sb("mx", [P, NT, H]), sb("nm", [P, NT, 2 * H])
    mt = sb("mt", [2 * H, HALF], F32R)
    ex = sb("ex", [P, 2, 5, HALF])
    raw = sb("raw", [P, NG, HALF])
    dent = sb("dent", [P, H * HALF // P])
    at = sb("at", [P, NG, HALF])
    wq = raw[:, 0, :].rearrange("p (c d) -> p c d", c=C)
    den_d = nc.dram_tensor("den_d", (4, NG * HALF), F32).ap()
    rden_d = nc.dram_tensor("rden_d", (4, NG * HALF), F32).ap()

    W = [ctx.enter_context(nc.psum_tensor(f"work{i}", [P, HALF], F32)) for i in range(2)]
    SM = [ctx.enter_context(nc.psum_tensor(f"smax{i}", [P, HALF], F32)) for i in range(2)]
    ST = [ctx.enter_context(nc.psum_tensor(f"sT{i}", [P, HALF], F32)) for i in range(2)]
    OT = [ctx.enter_context(nc.psum_tensor(f"oT{i}", [P, HALF], F32)) for i in range(2)]

    x_in, w_in, c_in = [sem(f"x_in{i}") for i in range(B)], sem("w_in"), sem("ctx_in")
    const_set, pool_set, wq_set, rel_set = sem("const_set"), sem("pool_set"), sem("wq_set"), sem("rel_set")
    rel_step = sem("rel_step")
    waited = sem("waited")
    g_set = sem("g_set")
    stat_s, mv_s, veps_s, rstd_s, xn_s = sem("stat"), sem("mv"), sem("veps"), sem("rstd"), sem("xn")
    xT_ps, xT_hi, work_free = sem("xT_ps"), sem("xT_hi"), sem("work_free")
    k_ps, kp_s, kh_s, kl_s, v_ps = sem("k_ps"), sem("kp"), sem("kh"), sem("kl"), sem("v_ps")
    q_ps, q_hi = sem("q_ps"), sem("q_hi")
    km_in, ks_in, k2_s, v_s = sem("km_in"), [sem(f"ks_in{g}") for g in range(NG)], sem("k2"), sem("v")
    qs_in, ms_in = [sem("qs_in0"), sem("qs_in1")], sem("ms_in")
    sm_ps, sx_s, mx_s = sem("scores_ps"), sem("sx"), sem("mx")
    relc_s, d_s, sadd_s, sub_s = sem("relc"), sem("d"), sem("sadd"), sem("sub")
    nmh_s, nm_s, mT_ps, mT_s = sem("nm_hi"), sem("nm"), sem("mT_ps"), sem("mT")
    st_ps, exp_s, pv_ps, raw_s = sem("sT_ps"), sem("exp"), sem("pv_ps"), sem("raw")
    den_out, den_in, rden_s, rden_out, rden_in = sem("den_out"), sem("den_in"), sem("rden"), sem("rden_out"), sem("rden_in")
    at_s, y_ps = sem("at"), sem("y_ps")

    NI = 20
    NW0, NWORK = 11, 16
    X_USE, K_USE, V_USE, Q_USE, M_USE, Y_USE = (0, 9), 2, 3, (4, 11), (6, 13), (7, 14)

    def m_steps(i):
        return range(3 * (i - 5), min(TU * NSTK, 3 * (i - 4))) if i >= 5 else ()

    def m_tile(h, j):
        return (0, 2, 1, 3)[j // NSTK] if h == 0 else TU + j // NSTK

    def body(unit, b, first=False, last=False):
        unit(b, 0, not first, not last)
        unit(b, 1, True, not last)

    def batches(eng, unit):
        body(unit, 0, first=True)
        with eng.Fori(0, B - 2) as k:
            body(unit, k + 1)
        body(unit, B - 1, last=True)

    block = ctx.enter_context(nc.Block())

    @block.sync
    def _(sp):
        for dst, src in ((cst[:], t["cst"][:, 0:NKEPT]), (raw[:, 1, 0:2 * P], t["cst"][:, NKEPT:NKEPT + 2 * P]),
                         (rel[:], t["rel"]), (gates[:], t["gates"]),
                         (raw[:, 0, :], t["wq"].rearrange("p c d -> p (c d)")), (wk[:], t["wk"]), (wv[:], t["wv"]),
                         (wo[:], t["wo"])):
            sp.dma_start(dst, src).then_inc(w_in, 16)

        def q_stack(b, h, heads):
            n = slice(h * HALF, (h + 1) * HALF)
            for r, src in enumerate((qh, ql, qh)):
                for i in heads:
                    sp.dma_start(qs[32 * r:32 * r + 32, i::4, n].bitcast(F32),
                                 src[32 * i:32 * i + 32, :, :].bitcast(F32)).then_inc(qs_in[h], 16)

        def k_stack(g):
            sp.dma_start(ks[0:96, 2 * g:2 * g + 2, :].bitcast(F32), km[:, 2 * g:2 * g + 2, 0:PAIR].bitcast(F32))\
                .then_inc(ks_in[g], 16)

        def m_stack(b, h):
            q0 = HALF // 2 if h == 0 else 0
            sp.wait_ge(mT_s, 2 * b + h + 1)
            sp.dma_start(qs[96:128, :, h * HALF + q0:(h + 1) * HALF].bitcast(F32),
                         mt[:, q0:HALF].unsqueeze(1).broadcast_to([32, NSTK, HALF - q0]).bitcast(F32)).then_inc(ms_in, 16)

        def divisors(u):
            sp.wait_ge(raw_s, NG * (u + 1))
            sp.dma_start(den_d.rearrange("j (g n) -> j g n", g=NG), raw[HD::32, :, :]).then_inc(den_out, 16)
            sp.wait_ge(den_out, 16 * (u + 1))
            sp.dma_start(dent[:], den_d.rearrange("j (p n) -> (j p) n", p=32)).then_inc(den_in, 16)
            sp.wait_ge(rden_s, u + 1)
            sp.dma_start(rden_d.rearrange("j (p n) -> (j p) n", p=32), dent[:]).then_inc(rden_out, 16)
            sp.wait_ge(rden_out, 16 * (u + 1))
            for j in range(4):
                sp.dma_start(at[32 * j:32 * j + 32, :, :].rearrange("p g n -> p (g n)"),
                             rden_d[j:j + 1, :].broadcast_to([32, NG * HALF])).then_inc(rden_in, 16)

        def unit(b, h, carry, ahead):
            u = 2 * b + h
            if h == 0 and ahead:
                sp.wait_ge(v_ps, b + 1)
                sp.nop().then_inc(waited, 1)
                sp.dma_start(ctxb[:], t["ctx"][b + 1]).then_inc(c_in, 16)
            if carry and (h == 0 or ahead):
                sp.wait_ge(st_ps, NI * u)
                q_stack(b + h, 1 - h, (2, 3))
            if carry:
                divisors(u - 1)
            if h == 1 and ahead:
                sp.wait_ge(km_in, 16 * 12 * (b + 2))
                sp.nop().then_inc(waited, 1)
                for g in range(NG - 1):
                    sp.wait_ge(st_ps, NI * u + 5 * (g + 1))
                    k_stack(g)
            if ahead:
                sp.wait_ge(work_free, NW0 + NWORK * b + Q_USE[h] + 2)
                sp.nop().then_inc(waited, 1)
                sp.wait_ge(st_ps, NI * u + 15)
                q_stack(b + 1, h, (0, 1))
            if h == 0:
                m_stack(b, 1)
            elif ahead:
                m_stack(b + 1, 0)
                sp.wait_ge(st_ps, NI * (u + 1))
                k_stack(NG - 1)

        sp.dma_start(ctxb[:], t["ctx"][0]).then_inc(c_in, 16)
        sp.wait_ge(work_free, 6)
        q_stack(0, 0, range(4))
        sp.wait_ge(km_in, 16 * 12)
        for g in range(NG):
            k_stack(g)
        sp.wait_ge(work_free, 10)
        q_stack(0, 1, range(4))
        m_stack(0, 0)
        batches(sp, unit)
        divisors(2 * B - 1)

    @block.gpsimd
    def _(pool):
        nc.gpsimd.memset(va[:], 0.0).then_inc(pool_set, 1)
        nc.gpsimd.memset(vb[:], 0.0).then_inc(pool_set, 1)
        nc.gpsimd.memset(tp[:], 0.0).then_inc(pool_set, 1)
        nc.gpsimd.memset(k2[:].bitcast(F32), 0.0).then_inc(pool_set, 1)
        pool.wait_ge(w_in, 8 * 16)

        def rstd_of(u):
            pool.wait_ge(mv_s, TU * (u + 1))
            nc.gpsimd.tensor_tensor(veps[:], mv[:, :, 1], con("eps"), ALU.add).then_inc(veps_s, 1)
            pool.wait_ge(veps_s, u + 1)
            nc.gpsimd.tensor_tensor(rstd[:], veps[:], con("mhalf"), ALU.pow).then_inc(rstd_s, 1)

        def short_chunk(b):
            pool.wait_ge(km_in, 16 * 12 * (b + 1))
            pool.nop().then_inc(waited, 1)
            for par in range(2):
                src = km[:, par::2, 0:PAIR].rearrange("p s (j k) -> p s j k", j=2)[:, :, :, P:KL]
                dst = k2[0:96, par::2, :].rearrange("p s (q k) -> p s q k", q=4)[:, :, 2 * par:2 * par + 2, 0:K1]
                nc.gpsimd.tensor_copy(dst, src).then_inc(k2_s, 1)

        def values(use):
            pool.wait_ge(work_free, use + 1)
            pool.nop().then_inc(waited, 1)
            nc.gpsimd.tensor_copy(va[:, :, 0:HD], vs[:, 0:D].rearrange("p (h d) -> p h d", h=H)).then_inc(v_s, 1)
            strip = con("strip").unsqueeze(1).unsqueeze(3).broadcast_to([P, NG, 4, HD])
            nc.gpsimd.tensor_tensor(vb[:, :, :, 0:HD], strip,
                                    vs[:, D:D + 64].rearrange("p (g d) -> p g d", g=NG).unsqueeze(2)
                                    .broadcast_to([P, NG, 4, HD]), ALU.mult).then_inc(v_s, 1)

        def near(b, start):
            for i, (dt, band, width) in enumerate(((d0, "band0", P), (d1, "band1", 32))):
                n = 6 * b + 3 * i
                pool.wait_ge(sx_s, 16 * b + 8 * (i + 1))
                if i == 0 and not start:
                    pool.wait_ge(sadd_s, 4 * b)
                if not (i == 0 and start):
                    pool.wait_ge(d_s, 3 * b + i)
                pool.nop().then_inc(waited, 1)
                src = sx[:, i, :, PAIR:SW].rearrange("p s (j d) -> p s j d", j=2)
                nc.gpsimd.tensor_copy(relc[:].rearrange("p (s j) d -> p s j d", j=2), src).then_inc(relc_s, 1)
                pool.wait_ge(relc_s, 2 * b + i + 1)
                rot = con("rot").rearrange("p (r d) -> p r d", r=4).unsqueeze(1).broadcast_to([P, H, 4, DIST])
                nc.gpsimd.tensor_tensor(rotc[:], relc[:].unsqueeze(2).broadcast_to([P, H, 4, DIST]), rot,
                                        ALU.mult).then_inc(rel_step, 1)
                pool.wait_ge(rel_step, n + 1)
                nc.gpsimd.tensor_tensor(rotc[:, :, :, 0:2], rotc[:, :, :, 0:2], rotc[:, :, :, 2:4],
                                        ALU.add).then_inc(rel_step, 1)
                pool.wait_ge(rel_step, n + 2)
                nc.gpsimd.tensor_tensor(relr[:], rotc[:, :, :, 0], rotc[:, :, :, 1], ALU.add).then_inc(rel_step, 1)
                pool.wait_ge(rel_step, n + 3)
                nc.gpsimd.tensor_tensor(
                    dt[:].rearrange("p h (a r) -> p h a r", r=4),
                    relr[:].unsqueeze(2).broadcast_to([P, H, width // 4, 4]),
                    con(band).rearrange("p (a r) -> p a r", r=4).unsqueeze(1).broadcast_to([P, H, width // 4, 4]),
                    ALU.mult).then_inc(d_s, 1)
            pool.wait_ge(d_s, 3 * b + 2)
            nc.gpsimd.tensor_tensor(d1[:], d1[:], con("causal1").unsqueeze(1).broadcast_to([P, H, 32]),
                                    ALU.add).then_inc(d_s, 1)

        def unit(b, h, carry, ahead):
            u = 2 * b + h
            if ahead:
                rstd_of(u + 2)
            if carry and h == 0:
                pool.wait_ge(pv_ps, NG * u)
                values(NW0 + NWORK * (b - 1) + V_USE)
            if h == 1 and ahead:
                near(b + 1, False)
                pool.wait_ge(st_ps, NI * (u + 1))
                short_chunk(b + 1)

        rstd_of(0)
        rstd_of(1)
        pool.wait_ge(const_set, 3)
        short_chunk(0)
        values(V_USE)
        near(0, True)
        batches(pool, unit)

    @block.scalar
    def _(act):
        for i in range(B):
            act.dma_start(x1[:, i * NT:(i + 1) * NT, :], t["x"][i]).then_inc(x_in[i], 16)
        act.wait_ge(w_in, 8 * 16)
        nc.scalar.activation(tg[:], gates[:], ACT.Tanh).then_inc(g_set, 1)
        nc.scalar.mul(wqh[:], wq, SCALE).then_inc(wq_set, 1)
        nc.scalar.copy(ks[96:128, :, :].rearrange("p s (j k) -> p s j k", j=2),
                       con("head", 96, 128).rearrange("p (s j) -> p s j", j=2).unsqueeze(3)
                       .broadcast_to([32, NSTK, 2, KL])).then_inc(const_set, 1)
        act.wait_ge(pool_set, 4)
        for par in range(2):
            nc.scalar.copy(k2[96:128, par::2, :].rearrange("p s (q k) -> p s q k", q=4)[:, :, 2 * par:2 * par + 2, 0:K1],
                           con("head", 96, 128).rearrange("p (s j) -> p s j", j=2)[:, par::2, :].unsqueeze(3)
                           .broadcast_to([32, NG, 2, K1])).then_inc(const_set, 1)
        nc.scalar.copy(idr[:], raw[:, 1, 0:P]).then_inc(const_set, 1)
        nc.scalar.copy(cmask[:], raw[:, 1, P:2 * P]).then_inc(const_set, 1)
        act.wait_ge(rel_set, 3)
        for r, src in enumerate((relh, relh, rell)):
            nc.scalar.copy(km[32 * r:32 * r + 32, :, PAIR:SW],
                           src[0:32, :, :].rearrange("p j d -> p (j d)").unsqueeze(1).broadcast_to([32, NSTK, 2 * DIST]))\
                .then_inc(const_set, 1)

        def x_hi(u, use):
            for c in range(C):
                act.wait_ge(xT_ps, 2 * u + c + 1)
                nc.scalar.copy(xth[:, c, :], W[(use + c) % 2][:]).then_inc(xT_hi, 1)

        def k_hi(b, start):
            act.wait_ge(kp_s, b + 1)
            if not start:
                act.wait_ge(km_in, 16 * 12 * b)
            for j in range(2):
                nc.scalar.mul(kh[:, :, j, :], kp[:], con("odd")[:, j:j + 1]).then_inc(kh_s, 1)

        def k_out(b, r, start):
            if r == 0:
                act.wait_ge(kh_s, 2 * (b + 1))
                act.wait_ge(kl_s, 2 * (b + 1))
                if not start:
                    act.wait_ge(sm_ps, 64 * b)
                    act.wait_ge(k2_s, 2 * b)
                    for g in range(NG):
                        act.wait_ge(ks_in[g], 16 * b)
            for i in range(4):
                act.dma_start(km[32 * r:32 * r + 32, i::4, 0:PAIR].bitcast(F32),
                              (kh, kh, kl)[r][32 * i:32 * i + 32, :, :, :].rearrange("p c j k -> p c (j k)").bitcast(F32))\
                    .then_inc(km_in, 16)

        def q_out(u, use):
            for c in range(C):
                act.wait_ge(q_ps, 2 * u + c + 1)
                nc.scalar.copy(qh[:, c, :], W[(use + c) % 2][:]).then_inc(q_hi, 1)

        def near(b, j):
            act.wait_ge(sm_ps, 64 * b + j + 1)
            nc.scalar.copy(sx[:, m_tile(0, j), j % NSTK, :], SM[j % 2][:, 0:SW]).then_inc(sx_s, 1)

        def raw_out(u, g, start=False):
            act.wait_ge(pv_ps, NG * u + g + 1)
            if not start:
                act.wait_ge(at_s, NG * (u - 1) + g + 1)
            nc.scalar.copy(raw[:, g, :], OT[g % 2][:]).then_inc(raw_s, 1)

        def unit(b, h, carry, ahead):
            u = 2 * b + h
            for i in range(NI):
                g = i // 5
                q0 = P if h == 0 and i % 5 == 4 else 0
                if i % 5 == 0 and not (h == 0 and not carry and g < 2):
                    act.wait_ge(pv_ps, NG * u + g - 1)
                act.wait_ge(st_ps, NI * u + i + 1)
                nc.scalar.activation(ex[:, g % 2, i % 5, q0:HALF], ST[i % 2][:, q0:HALF], ACT.Exp).then_inc(exp_s, 1)
                if i == 4 and carry:
                    raw_out(u - 1, 3, start=(h == 1 and isinstance(b, int) and b == 0))
                if i == 6 and ahead:
                    x_hi(u + 2, NW0 + X_USE[h])
                if i == 8 and ahead and h == 0:
                    k_hi(b + 1, False)
                if i == 10 and ahead:
                    act.wait_ge(qs_in[1 - h], 16 * 12 * (b + h + 1))
                    q_out(u + 2, NW0 + Q_USE[h])
                if ahead and h == 1:
                    if i == 5:
                        act.wait_ge(sub_s, 3 * (b + 1))
                    for j in m_steps(i):
                        if m_tile(0, j) < 2:
                            near(b + 1, j)
                if i in (14, 17, 19):
                    raw_out(u, (14, 17, 19).index(i), start=not carry)
                if ahead and h == 0 and i in (16, 17, 18):
                    k_out(b + 1, i - 16, False)

        x_hi(0, 0)
        k_hi(0, True)
        for r in range(3):
            k_out(0, r, True)
        q_out(0, Q_USE[0])
        x_hi(1, 6)
        act.wait_ge(qs_in[0], 16 * 12)
        q_out(1, 8)
        for j in range(TU * NSTK):
            if m_tile(0, j) < 2:
                near(0, j)
        batches(act, unit)
        raw_out(2 * B - 1, 3)

    @block.vector
    def _(dve):
        dve.wait_ge(pool_set, 4)
        nc.vector.memset(va[:, :, HD:HD + 1], 1.0)
        for j in range(4):
            last_one = nc.vector.memset(vb[32 * j:32 * j + K1, :, j, HD:HD + 1], 1.0)
        last_one.then_inc(pool_set, 1)
        dve.wait_ge(w_in, 8 * 16)
        dve.wait_ge(wq_set, 1)
        nc.vector.scalar_tensor_tensor(wql[:], wq, SCALE, wqh[:], ALU.mult, ALU.subtract).then_inc(wq_set, 1)
        nc.vector.tensor_scalar(reld[:], rel[:, DIST:2 * DIST], rel[:, 2 * DIST:], None, ALU.subtract)\
            .then_inc(rel_set, 1)
        dve.wait_ge(rel_set, 1)
        for j in range(2):
            nc.vector.tensor_scalar(relm[:, j, :], reld[:], con("odd")[:, j:j + 1], None, ALU.mult)
            last_one = nc.vector.tensor_scalar(relh[:, j, :], reld[:], con("odd")[:, j:j + 1], None, ALU.mult)
        last_one.then_inc(rel_set, 1)
        dve.wait_ge(rel_set, 2)
        nc.vector.tensor_tensor(rell[:], relm[:], relh[:], ALU.subtract).then_inc(rel_set, 1)

        def norm_stats(b, h):
            u = 2 * b + h
            for i in range(TU):
                nc.vector.bn_stats(stats[:, i, :], x1[:, b * NT + TU * h + i, :]).then_inc(stat_s, 1)
            dve.wait_ge(stat_s, TU * (u + 1))
            dve.nop().then_inc(waited, 1)
            for i in range(TU):
                nc.vector.bn_aggr(mv[:, i, :], stats[:, i, :]).then_inc(mv_s, 1)

        def normalised(b, h, start=False):
            u = 2 * b + h
            dve.wait_ge(rstd_s, u + 1)
            if not start:
                dve.wait_ge(xT_ps, 2 * u)
            for i in range(TU):
                nc.vector.tensor_scalar(xn[:, i, :], x1[:, b * NT + TU * h + i, :], mv[:, i, 0:1], rstd[:, i:i + 1],
                                        ALU.subtract, ALU.mult).then_inc(xn_s, 1)

        def x_lo(u, use):
            for c in range(C):
                dve.wait_ge(xT_hi, 2 * u + c + 1)
                nc.vector.tensor_tensor(xtl[:, c, :], W[(use + c) % 2][:], xth[:, c, :], ALU.subtract)\
                    .then_inc(work_free, 1)

        def q_lo(u, use):
            for c in range(C):
                dve.wait_ge(q_hi, 2 * u + c + 1)
                nc.vector.tensor_tensor(ql[:, c, :], W[(use + c) % 2][:], qh[:, c, :], ALU.subtract)\
                    .then_inc(work_free, 1)

        def k_v(b, use, start):
            dve.wait_ge(k_ps, b + 1)
            nc.vector.tensor_scalar(kp[:], W[use % 2][:, 0:2 * KL].rearrange("p (c k) -> p c k", c=C), rel[:, 2 * DIST:],
                                    None, ALU.add).then_inc(kp_s, 1)
            dve.wait_ge(kp_s, b + 1)
            nc.vector.nop().then_inc(work_free, 1)
            dve.wait_ge(v_ps, b + 1)
            if not start:
                dve.wait_ge(v_s, 2 * b)
            nc.vector.tensor_copy(vs[:], W[(use + 1) % 2][:, 0:D + 64]).then_inc(work_free, 1)
            for j in range(2):
                dve.wait_ge(kh_s, 2 * b + j + 1)
                nc.vector.scalar_tensor_tensor(kl[:, :, j, :], kp[:], con("odd")[:, j:j + 1], kh[:, :, j, :],
                                               ALU.mult, ALU.subtract).then_inc(kl_s, 1)

        def maximum(b, h, j):
            s, tile = j % NSTK, m_tile(h, j)
            dve.wait_ge(sm_ps, 64 * b + 32 * h + j + 1)
            nc.vector.reduce_max(mx[:, tile, 2 * s:2 * s + 2],
                                 SM[s % 2][:, 0:PAIR].rearrange("p (j k) -> p j k", j=2), AX_X).then_inc(mx_s, 1)

        def by_stack(ap):
            return ap.rearrange("p (s j) k -> p s j k", j=2)

        def over(ap, n):
            return ap.rearrange("p (s j) -> p s j", j=2).unsqueeze(3).broadcast_to([P, NSTK, 2, n])

        def tile0(b, part):
            keys = sx[:, 0, :, 0:PAIR].rearrange("p s (j k) -> p s j k", j=2)[:, :, :, 0:P]
            if part == 0:
                dve.wait_ge(d_s, 3 * b + 1)
                nc.vector.tensor_tensor(keys, keys, by_stack(d0[:]), ALU.add).then_inc(sadd_s, 1)
            elif part == 1:
                dve.wait_ge(sadd_s, 4 * b + 1)
                nc.vector.reduce_max(mx[:, 0, :], keys, AX_X).then_inc(sadd_s, 1)
            else:
                dve.wait_ge(sadd_s, 4 * b + 2)
                nc.vector.tensor_tensor(keys, keys, over(mx[:, 0, :], P), ALU.subtract).then_inc(sub_s, 1)

        def tile1(b, part):
            keys = sx[:, 1, :, 0:PAIR].rearrange("p s (j k) -> p s j k", j=2)
            if part == 0:
                dve.wait_ge(d_s, 3 * b + 3)
                nc.vector.tensor_tensor(keys[:, :, :, P - DIST:KL], keys[:, :, :, P - DIST:KL],
                                        by_stack(d1[:, :, 0:K1 + DIST]), ALU.add).then_inc(sadd_s, 1)
            elif part == 1:
                dve.wait_ge(sadd_s, 4 * b + 3)
                nc.vector.reduce_max(mx[:, 1, :], keys, AX_X).then_inc(sadd_s, 1)
            else:
                dve.wait_ge(sadd_s, 4 * b + 4)
                nc.vector.tensor_tensor(keys[:, :, :, 0:P], keys[:, :, :, 0:P], over(mx[:, 1, :], P), ALU.subtract)\
                    .then_inc(sub_s, 1)
                nc.vector.tensor_tensor(by_stack(tp[:, :, 0:K1]), keys[:, :, :, P:KL], over(mx[:, 1, :], K1),
                                        ALU.subtract).then_inc(sub_s, 1)

        def minus_max(b, h, start=False):
            r = slice(2 if h == 0 else TU, TU * (h + 1))
            dve.wait_ge(mx_s, 48 * b + (16 if h == 0 else 48))
            if not start:
                dve.wait_ge(mT_ps, 2 * b + h)
            nc.vector.tensor_scalar(nm[:, r, 0:H].bitcast(F32R), mx[:, r, :], -1.0, None, ALU.mult).then_inc(nmh_s, 1)
            dve.wait_ge(nmh_s, 2 * b + h + 1)
            nc.vector.scalar_tensor_tensor(nm[:, r, H:2 * H], mx[:, r, :], -1.0, nm[:, r, 0:H],
                                           ALU.mult, ALU.subtract).then_inc(nm_s, 1)

        def max_out(b, h, use, start=False):
            u = 2 * b + h
            q0 = HALF // 2 if h == 0 else 0
            dve.wait_ge(mT_ps, u + 1)
            if not start:
                dve.wait_ge(ms_in, 16 * u)
            nc.vector.tensor_copy(mt[:, q0:HALF], W[use % 2][0:32, q0:HALF]).then_inc(mT_s, 1)
            dve.wait_ge(mT_s, u + 1)
            nc.vector.nop().then_inc(work_free, 1)

        def reciprocals(u):
            dve.wait_ge(den_in, 16 * (u + 1))
            nc.vector.reciprocal(dent[:], dent[:]).then_inc(rden_s, 1)

        def divide(u):
            dve.wait_ge(rden_in, 64 * (u + 1))
            for g in range(NG):
                nc.vector.tensor_tensor(at[:, g, :], raw[:, g, :], at[:, g, :], ALU.mult).then_inc(at_s, 1)

        def residual(b, h, pr, use):
            dve.wait_ge(y_ps, 2 * (2 * b + h) + pr + 1)
            tile = b * NT + TU * h + 2 * pr
            xs = x1[:, bass.ds(tile, 2), :]
            nc.vector.scalar_tensor_tensor(xs, W[use % 2][:].rearrange("p (t d) -> p t d", t=2), tg[:, 0:1], xs,
                                           ALU.mult, ALU.add).then_inc(work_free, 1)

        def unused(n, b, use):
            dve.wait_ge(work_free, NW0 + NWORK * b + use)
            dve.sem_inc(work_free, n)

        def unit(b, h, carry, ahead):
            u = 2 * b + h
            mb, mh = b + h, 1 - h
            diagonal = h == 1 and ahead
            for i in range(NI):
                if i == 0 and ahead:
                    norm_stats(b + 1, h)
                if i == 3 and ahead:
                    normalised(b + 1, h)
                for j in m_steps(i):
                    if h == 0 or (ahead and m_tile(mh, j) >= 2):
                        maximum(mb, mh, j)
                if i == 6 and ahead:
                    x_lo(u + 2, NW0 + X_USE[h])
                if i == 8 and ahead and h == 0:
                    k_v(b + 1, NW0 + K_USE, False)
                if i == 9 and carry:
                    reciprocals(u - 1)
                if i == 10:
                    if ahead:
                        q_lo(u + 2, NW0 + Q_USE[h])
                    else:
                        unused(M_USE[h] - X_USE[h], b, X_USE[h])
                if diagonal and i in (11, 12, 13):
                    tile0(b + 1, i - 11)
                if i == 14 and carry:
                    divide(u - 1)
                if i == 15 and (h == 0 or ahead):
                    minus_max(mb, mh)
                if diagonal and i in (16, 17, 18):
                    tile1(b + 1, i - 16)
                if i == 17:
                    if h == 0 or ahead:
                        max_out(mb, mh, NW0 + M_USE[h])
                    else:
                        unused(1, b, M_USE[h])
                if i in (18, 19):
                    if carry:
                        residual(b - 1 + h, 1 - h, i - 18, NW0 + Y_USE[h] + i - 18)
                    elif i == 18:
                        unused(2, b, Y_USE[h])

        dve.wait_ge(x_in[0], 16)
        norm_stats(0, 0)
        normalised(0, 0, start=True)
        x_lo(0, 0)
        k_v(0, K_USE, True)
        norm_stats(0, 1)
        q_lo(0, Q_USE[0])
        normalised(0, 1)
        x_lo(1, 6)
        q_lo(1, 8)
        for j in range(TU * NSTK):
            if m_tile(0, j) >= 2:
                maximum(0, 0, j)
        minus_max(0, 0, start=True)
        max_out(0, 0, 10, start=True)
        for part in range(3):
            tile0(0, part)
        for part in range(3):
            tile1(0, part)
        for i in range(1, B):
            dve.wait_ge(x_in[i], 16)
        dve.wait_ge(g_set, 1)
        batches(dve, unit)
        reciprocals(2 * B - 1)
        divide(2 * B - 1)
        unused(Y_USE[0], B, 0)
        for pr in range(2):
            residual(B - 1, 1, pr, NW0 + Y_USE[0] + pr)

    @block.tensor
    def _(pe):
        pe.wait_ge(w_in, 8 * 16)
        pe.wait_ge(wq_set, 2)
        ident = idr[:].bitcast(F32)
        pe.wait_ge(const_set, 8)

        def work(b, use):
            pe.wait_ge(work_free, NW0 + NWORK * b + use - 1)
            return W[(NW0 + use) % 2]

        START = NWORK - NW0

        def transposes(u, b, use):
            for c in range(C):
                if not (isinstance(u, int) and u == 0):
                    pe.wait_ge(work_free, NW0 + NWORK * b + use + c - 1)
                w = W[(NW0 + use + c) % 2]
                pe.wait_ge(xn_s, TU * (u + 1))
                for j in range(TU):
                    last_one = nc.tensor.transpose(w[:, j * P:(j + 1) * P], xn[:, j, c * P:(c + 1) * P], ident)
                last_one.then_inc(xT_ps, 1)

        def keys(b, use_b, use):
            pe.wait_ge(c_in, 16 * (b + 1))
            w = work(use_b, use)
            for m in range(C):
                for c in range(C):
                    last_one = nc.tensor.matmul(w[:, m * KL:(m + 1) * KL], wk[:, c, m * P:(m + 1) * P], ctxb[:, c, 0:KL],
                                                start=(c == 0), stop=(c == C - 1))
            last_one.then_inc(k_ps, 1)

        def values_in(b, use_b, use):
            w = work(use_b, use)
            for c in range(C):
                nc.tensor.matmul(w[:, 0:D], ctxb[:, c, 0:P], wv[:, c, :], start=(c == 0), stop=(c == C - 1))
            for j in range(4):
                for c in range(C):
                    last_one = nc.tensor.matmul(w[32 * j:32 * j + 32, D:D + 64], ctxb[:, c, P:KPAD],
                                                wv[:, c, :].rearrange("p (g j d) -> p g j d", g=NG, j=4)[:, :, j, :],
                                                start=(c == 0), stop=(c == C - 1))
            last_one.then_inc(v_ps, 1)

        def queries(use_b, x_use, use):
            pe.wait_ge(work_free, NW0 + NWORK * use_b + x_use + 2)
            for m in range(C):
                w = work(use_b, use + m)
                steps = [(wa, xa, c) for c in range(C) for wa, xa in ((wql, xth), (wqh, xtl), (wqh, xth))]
                for k, (wa, xa, c) in enumerate(steps):
                    last_one = nc.tensor.matmul(w[:], wa[:, c, m * P:(m + 1) * P], xa[:, c, :],
                                                start=(k == 0), stop=(k == len(steps) - 1))
                last_one.then_inc(q_ps, 1)

        def max_scores(b, h, j, start=False):
            s, tile = j % NSTK, m_tile(h, j)
            if j == 0:
                pe.wait_ge(qs_in[h], 16 * 12 * (b + 1))
                if h == 0:
                    pe.wait_ge(km_in, 16 * 12 * (b + 1))
            if h == 1:
                pe.wait_ge(mx_s, 48 * b + 15 + j)
            elif j < 2:
                if not start:
                    pe.wait_ge(mx_s, 48 * b + j - 1)
            elif j < 10:
                pe.wait_ge(sx_s, 16 * b + j - 1)
            elif j < 18:
                pe.wait_ge(mx_s, 48 * b + j - 9)
            elif j < 26:
                pe.wait_ge(sx_s, 16 * b + j - 9)
            else:
                pe.wait_ge(mx_s, 48 * b + j - 17)
            width = SW if tile < 2 else PAIR
            last_one = nc.tensor.matmul(SM[s % 2][:, 0:width], qs[0:96, s, tile * P:(tile + 1) * P], km[:, s, 0:width],
                                        start=True, stop=True)
            if tile == 0:
                last_one = nc.tensor.matmul(SM[s % 2][:, 0:PAIR].rearrange("p (j k) -> p j k", j=2)[:, :, 0:P], idr[:],
                                            cmask[:].unsqueeze(1).broadcast_to([P, 2, P]), start=False, stop=True,
                                            skip_group_check=True)
            last_one.then_inc(sm_ps, 1)

        def max_T(b, h, use_b, use):
            w = work(use_b, use)
            pe.wait_ge(nm_s, 2 * b + h + 1)
            for j in range(2 - 2 * h, TU):
                last_one = nc.tensor.transpose(w[0:32, j * P:(j + 1) * P], nm[:, TU * h + j, :], ident)
            last_one.then_inc(mT_ps, 1)

        def score(b, h, step, start):
            u = 2 * b + h
            g, i = divmod(step, 5)
            if not (start and step < 2):
                pe.wait_ge(exp_s, NI * u + step - 1)
            if step == 0:
                pe.wait_ge(ms_in, 16 * (u + 1))
            if h == 0:
                if step == 0:
                    pe.wait_ge(sub_s, 3 * (b + 1))
                if i == 0:
                    pe.wait_ge(ks_in[g], 16 * (b + 1))
                if step == 4:
                    pe.wait_ge(k2_s, 2 * (b + 1))
            out = ST[step % 2]
            q0 = HALF // 2 if h == 0 else 0
            q = slice(h * HALF + q0, (h + 1) * HALF)
            if i < 4:
                s, j = divmod(4 * g + i, 2)
                if h == 0:
                    for k in range(2):
                        nc.tensor.transpose(out[:, k * P:(k + 1) * P], sx[:, k, s, j * KL:j * KL + P], ident)
                last_one = nc.tensor.matmul(out[:, q0:HALF], ks[:, s, j * KL:j * KL + P], qs[:, s, q], start=True,
                                            stop=True)
            else:
                if h == 0:
                    nc.tensor.transpose(out[:, P:2 * P], tp[:, 4 * g:4 * g + 4, :].rearrange("p h k -> p (h k)"), ident)
                for k in range(2):
                    last_one = nc.tensor.matmul(out[:, q0:HALF], k2[:, 2 * g + k, :], qs[:, 2 * g + k, q],
                                                start=(k == 0), stop=(k == 1))
            last_one.then_inc(st_ps, 1)

        def values(b, h, g, part, start=False):
            u = 2 * b + h
            pe.wait_ge(exp_s, NI * u + 5 * g + (4 if part == 0 else 5))
            if part == 0:
                if not (start and g < 2):
                    pe.wait_ge(raw_s, NG * u + g - 1)
                if h == 0 and g == 0:
                    pe.wait_ge(v_s, 2 * (b + 1))
            q0 = P if h == 0 and part == 1 else 0
            for j in range(4):
                e = ex[:, g % 2, j if part == 0 else 4, q0:HALF]
                v = va[:, 4 * g + j, :] if part == 0 else vb[:, g, j, :]
                last_one = nc.tensor.matmul(OT[g % 2][32 * j:32 * j + 32, q0:HALF], v, e,
                                            start=(part == 0), stop=(part == 1))
            if part == 1:
                last_one.then_inc(pv_ps, 1)

        def project(b, h, pr, use_b, use):
            pe.wait_ge(at_s, NG * (2 * b + h + 1))
            w = work(use_b, use)
            for k in range(2):
                j = 2 * pr + k
                for g in range(NG):
                    last_one = nc.tensor.matmul(w[:, k * D:(k + 1) * D], at[:, g, j * P:(j + 1) * P], wo[:, g, :],
                                                start=(g == 0), stop=(g == NG - 1))
            last_one.then_inc(y_ps, 1)

        def unit(b, h, carry, ahead):
            u = 2 * b + h
            start = h == 0 and not carry
            for i in range(NI):
                js = list(m_steps(i)) if h == 0 or ahead else []
                for j in js[:1]:
                    max_scores(b + h, 1 - h, j)
                score(b, h, i, start)
                for j in js[1:2]:
                    max_scores(b + h, 1 - h, j)
                if i in (1, 3) and carry:
                    values(b - 1 + h, 1 - h, NG - 1, i // 2)
                if i > 5 and i % 5 in (1, 3):
                    values(b, h, i // 5 - 1, i % 5 // 2, start)
                for j in js[2:]:
                    max_scores(b + h, 1 - h, j)
                if i == 5 and ahead:
                    transposes(u + 2, b, X_USE[h])
                if i == 7 and ahead and h == 0:
                    keys(b + 1, b, K_USE)
                    values_in(b + 1, b, V_USE)
                if i == 9 and ahead:
                    queries(b, X_USE[h], Q_USE[h])
                if i == 17 and (h == 0 or ahead):
                    max_T(b + h, 1 - h, b, M_USE[h])
                if i in (18, 19) and carry:
                    project(b - 1 + h, 1 - h, i - 18, b, Y_USE[h] + i - 18)

        transposes(0, -1, START)
        keys(0, -1, START + 2)
        values_in(0, -1, START + 3)
        queries(-1, START, START + 4)
        transposes(1, -1, START + 6)
        queries(-1, START + 6, START + 8)
        pe.wait_ge(pool_set, 5)
        for j in range(32):
            max_scores(0, 0, j, start=True)
        max_T(0, 0, -1, START + 10)
        batches(pe, unit)
        values(B - 1, 1, NG - 1, 0)
        values(B - 1, 1, NG - 1, 1)
        for pr in range(2):
            project(B - 1, 1, pr, B, Y_USE[0] + pr)


def experts(nc, ctx, x1, tg, t, out):
    def sb(name, shape, dt=F32):
        return ctx.enter_context(nc.sbuf_tensor(name, shape, dt))

    def sem(name):
        return ctx.enter_context(nc.semaphore(name))

    TB = HALF // P
    NBLK = B * S // HALF
    NR = 2 * E + 1
    XW = 2 * C * I + D

    cst = sb("cst2", [P, NCONST])

    def con(name, p0=0, p1=P):
        lo, hi = CONST[name]
        return cst[p0:p1, lo:hi]

    bias = sb("bias", [P, E])
    gw = sb("gw", [P, C, E])
    gwh, gwl = sb("gwh", [P, C, E], F32R), sb("gwl", [P, C, E], F32R)
    gst = sb("gst", [P, C, P], F32R)
    wx = sb("wx", [P, NE1, XW])
    wxh, wxl = sb("wxh", [P, NE1, XW], F32R), sb("wxl", [P, NE1, XW], F32R)
    selr = sb("selr", [NR, NE1, P], F32R)
    stats, mv = sb("stats2", [P, TB, 6]), sb("mv2", [P, TB, 2])
    veps, rstd = sb("veps2", [P, TB]), sb("rstd2", [P, TB])
    xn = sb("xn2", [P, TB, D])
    xh, xl = sb("x2h", [P, 2, C, HALF], F32R), sb("x2l", [P, 2, C, HALF], F32R)
    lgT = sb("lgT", [2 * E, HALF])
    sc = sb("sc", [P, TB, E])
    scc = sb("scc", [P, TB, E])
    gs = sb("gs", [P, TB, E // 2])
    g_gt, g_eq = sb("g_gt", [P, TB, 4, 4]), sb("g_eq", [P, TB, 4, 4])
    rank_g, rank_e = sb("rank_g", [P, TB, 4]), sb("rank_e", [P, TB, E])
    vch = sb("vch", [P, TB, E])
    e_gt, e_eq = sb("e_gt", [P, TB, E, E]), sb("e_eq", [P, TB, E, E])
    wsel = sb("wsel", [P, TB, E])
    winv = sb("winv", [P, TB])
    cw = sb("cw", [P, TB, E])
    cwc = sb("cwc", [P, TB, NR])
    cwt = sb("cwt", [NR, 2, HALF], F32R)
    R = 3
    sg = sb("sg", [P, R, HALF])
    hf = sb("hf", [P, R, HALF])
    hh, hl = sb("hh", [P, R, HALF], F32R), sb("hl", [P, R, HALF], F32R)

    def bank(name):
        return ctx.enter_context(nc.psum_tensor(name, [P, HALF], F32))

    PG, PU = [bank("pg0"), bank("pg1")], [bank("pu0"), bank("pu1")]
    PC, PM = bank("pc"), bank("pm")
    PY = [bank("py0"), bank("py1")]

    w_in, c_in = [sem(f"wx_in{e}") for e in range(NE1)], sem("const_in")
    w_hi, w_lo, gst_s, tab_s = sem("wx_hi"), sem("wx_lo"), sem("router_set"), sem("tables_set")
    stat_s, mv_s, veps_s, rstd_s, xn_s = sem("stat_b"), sem("mv_b"), sem("veps_b"), sem("rstd_b"), sem("xn_b")
    t_ps, t_hi, misc_free = sem("xT_ps_b"), sem("xT_hi_b"), sem("misc_free")
    gl_ps, lgT_s, lg_ps, sc_s = sem("router_ps"), sem("router_out"), sem("logits_ps"), sem("scores_set")
    route, ct_ps = sem("route_step"), sem("cwT_ps")
    sg_s, gu_ps, gu_free, cb_ps, h_done = sem("silu_set"), sem("gate_up_ps"), sem("gate_up_free"), sem("cw_ps"), sem("hidden_done")
    waited = sem("waited_b")
    hh_s, hl_done, hid_free = sem("hidden_hi"), sem("hidden_lo_done"), sem("hidden_free")
    fin_s, out_s, y_ps = sem("fin"), sem("out_stored"), sem("y_ps_b")
    block = ctx.enter_context(nc.Block())
    RG = 2
    PER = 2 * NE1
    NROUTE = 20

    LAST = NBLK // 2 - 1

    def turns(eng, item):
        item(0, 0, False)
        item(0, 1, False)
        with eng.Fori(0, LAST) as k:
            for i in range(2, PER + 2):
                item(k, i, False)
        for i in range(2, PER):
            item(LAST, i, True)

    def place(k, i, last):
        return 2 * k + i // NE1, i % NE1, not (last and i >= NE1)

    @block.sync
    def _(sp):
        for dst, src in ((cst[:], t["cst"]), (bias[:], t["bias"]), (gw[:], t["gw"])):
            sp.dma_start(dst, src).then_inc(c_in, 16)
        for e in range(NE1):
            sp.dma_start(wx[:, e, :], t["wx"][:, e, :]).then_inc(w_in[e], 16)
        with sp.Fori(0, NBLK) as n:
            sp.wait_ge(fin_s, 2 * (n + 1))
            sp.nop().then_inc(waited, 1)
            sp.dma_start(out[n], x1[:, bass.ds(n * TB, TB), :]).then_inc(out_s, 16)
        sp.wait_ge(out_s, 16 * NBLK)

    @block.gpsimd
    def _(pool):
        nc.gpsimd.memset(gst[:].bitcast(F32), 0.0).then_inc(gst_s, 1)
        nc.gpsimd.memset(cwc[:], 1.0).then_inc(gst_s, 1)
        pool.sem_inc(hl_done, R)
        pool.wait_ge(c_in, 3 * 16)

        def rstd_of(n):
            pool.wait_ge(mv_s, TB * (n + 1))
            nc.gpsimd.tensor_tensor(veps[:], mv[:, :, 1], con("eps"), ALU.add).then_inc(veps_s, 1)
            pool.wait_ge(veps_s, n + 1)
            nc.gpsimd.tensor_tensor(rstd[:], veps[:], con("mhalf"), ALU.pow).then_inc(rstd_s, 1)

        def hidden_lo(k, i):
            m = PER * k + i
            pool.wait_ge(hh_s, m + 1)
            pool.wait_ge(hid_free, m + 1)
            nc.gpsimd.tensor_tensor(hl[:, i % R, :], hf[:, i % R, :], hh[:, i % R, :], ALU.subtract).then_inc(hl_done, 1)

        def item(k, i, last):
            n, e, ahead = place(k, i, last)
            hidden_lo(k, i)
            if ahead and e == 0:
                rstd_of(n + 1)

        rstd_of(0)
        turns(pool, item)

    @block.scalar
    def _(act):
        act.sem_inc(misc_free, 1)
        act.wait_ge(c_in, 3 * 16)
        nc.scalar.copy(gwh[:], gw[:]).then_inc(tab_s, 1)
        nc.scalar.copy(selr[:], cst[0:NR, CONST["expert"][0]:CONST["expert"][1]].unsqueeze(2)
                       .broadcast_to([NR, NE1, P])).then_inc(tab_s, 1)

        def x_hi(n, slot):
            if not (isinstance(n, int) and n == 0):
                act.wait_ge(gu_ps, 1 + NE1 * (n - 1))
            for c in range(C):
                act.wait_ge(t_ps, 2 * n + c + 1)
                nc.scalar.copy(xh[:, slot, c, :], PM[:]).then_inc(t_hi, 1)

        def scores(n):
            act.wait_ge(lg_ps, n + 1)
            act.wait_ge(route, NROUTE * n)
            nc.scalar.activation(sc[:], PM[:, 0:TB * E].rearrange("p (t e) -> p t e", t=TB), ACT.Sigmoid)\
                .then_inc(sc_s, 1)

        def silu(k, i):
            m = PER * k + i
            act.wait_ge(gu_ps, 1 + m + 1)
            act.wait_ge(h_done, m + 1)
            nc.scalar.activation(sg[:, i % R, :], PG[i % RG][:], ACT.Silu).then_inc(sg_s, 1)

        def hidden_hi(k, i):
            m = PER * k + i
            act.wait_ge(h_done, m + R + 1)
            act.wait_ge(hid_free, m + 1)
            nc.scalar.copy(hh[:, i % R, :], hf[:, i % R, :]).then_inc(hh_s, 1)

        def item(k, i, last):
            n, e, ahead = place(k, i, last)
            if not (last and i == PER - 1):
                silu(k, i + 1)
            hidden_hi(k, i)
            if ahead and e == 2:
                x_hi(n + 1, (i // NE1 + 1) % 2)
            if ahead and e == 4:
                scores(n + 1)

        x_hi(0, 0)
        for e in range(NE1):
            act.wait_ge(w_in[e], 16)
            nc.scalar.copy(wxh[:, e, :], wx[:, e, :]).then_inc(w_hi, 1)
            if e == 1:
                scores(0)
        silu(0, 0)
        turns(act, item)

    @block.vector
    def _(dve):
        dve.sem_inc(gu_free, RG)
        dve.sem_inc(h_done, R)
        dve.wait_ge(c_in, 3 * 16)
        dve.wait_ge(tab_s, 1)
        nc.vector.tensor_tensor(gwl[:], gw[:], gwh[:], ALU.subtract).then_inc(tab_s, 1)
        dve.wait_ge(tab_s, 3)
        dve.wait_ge(gst_s, 2)
        nc.vector.tensor_copy(gst[:, :, 0:E], gwh[:].bitcast(F32))
        nc.vector.tensor_copy(gst[:, :, E:2 * E], gwl[:].bitcast(F32)).then_inc(gst_s, 1)

        def norm_stats(n):
            for i in range(TB):
                nc.vector.bn_stats(stats[:, i, :], x1[:, n * TB + i, :]).then_inc(stat_s, 1)
            dve.wait_ge(stat_s, TB * (n + 1))
            dve.nop().then_inc(waited, 1)
            for i in range(TB):
                nc.vector.bn_aggr(mv[:, i, :], stats[:, i, :]).then_inc(mv_s, 1)

        def normalised(n):
            dve.wait_ge(rstd_s, n + 1)
            dve.wait_ge(t_ps, 2 * n)
            for i in range(TB):
                nc.vector.tensor_scalar(xn[:, i, :], x1[:, n * TB + i, :], mv[:, i, 0:1], rstd[:, i:i + 1],
                                        ALU.subtract, ALU.mult).then_inc(xn_s, 1)

        def x_lo(n, slot):
            for c in range(C):
                dve.wait_ge(t_hi, 2 * n + c + 1)
                nc.vector.tensor_tensor(xl[:, slot, c, :], PM[:], xh[:, slot, c, :], ALU.subtract).then_inc(misc_free, 1)

        def router_out(n):
            dve.wait_ge(gl_ps, n + 1)
            dve.wait_ge(lg_ps, n)
            nc.vector.tensor_copy(lgT[:], PM[0:2 * E, :]).then_inc(misc_free, 1)

        def routing(n, part):
            at = [0 if part == 0 else 8]

            def step(ins):
                ins.then_inc(route, 1)
                at[0] += 1
                dve.wait_ge(route, NROUTE * n + at[0])

            def along(ap, axis, shape):
                return ap.unsqueeze(axis).broadcast_to(shape)

            def lower(k):
                return con(f"lower{k}").rearrange("p (a b) -> p a b", a=k).unsqueeze(1).broadcast_to([P, TB, k, k])

            tt = nc.vector.tensor_tensor
            if part == 0:
                dve.wait_ge(sc_s, n + 1)
                step(tt(scc[:], sc[:], bias[:].unsqueeze(1).broadcast_to([P, TB, E]), ALU.add))
                step(tt(gs[:], scc[:, :, 0::2], scc[:, :, 1::2], ALU.add))
                sh = [P, TB, 4, 4]
                step(tt(g_gt[:], along(gs[:], 2, sh), along(gs[:], 3, sh), ALU.is_gt))
                step(tt(g_eq[:], along(gs[:], 2, sh), along(gs[:], 3, sh), ALU.is_equal))
                step(tt(g_eq[:], g_eq[:], lower(4), ALU.mult))
                step(tt(g_gt[:], g_gt[:], g_eq[:], ALU.add))
                step(nc.vector.reduce_sum(rank_g[:], g_gt[:], AX_X))
                step(nc.vector.scalar_tensor_tensor(
                    vch[:].rearrange("p t (g j) -> p t g j", j=2), along(rank_g[:], 3, [P, TB, 4, 2]), 2.0,
                    scc[:].rearrange("p t (g j) -> p t g j", j=2), ALU.is_lt, ALU.mult))
            else:
                sh = [P, TB, E, E]
                step(tt(e_gt[:], along(vch[:], 2, sh), along(vch[:], 3, sh), ALU.is_gt))
                step(tt(e_eq[:], along(vch[:], 2, sh), along(vch[:], 3, sh), ALU.is_equal))
                step(tt(e_eq[:], e_eq[:], lower(E), ALU.mult))
                step(tt(e_gt[:], e_gt[:], e_eq[:], ALU.add))
                step(nc.vector.reduce_sum(rank_e[:], e_gt[:], AX_X))
                step(nc.vector.scalar_tensor_tensor(wsel[:], rank_e[:], 4.0, sc[:], ALU.is_lt, ALU.mult))
                step(nc.vector.reduce_sum(winv[:], wsel[:], AX_X))
                step(nc.vector.tensor_scalar(winv[:], winv[:], 1e-20, 1.0 / ROUTE_SCALE, ALU.add, ALU.mult))
                step(nc.vector.reciprocal(winv[:], winv[:]))
                step(tt(cw[:], wsel[:], along(winv[:], 2, [P, TB, E]), ALU.mult))
                dve.wait_ge(ct_ps, n)
                step(nc.vector.tensor_scalar(cwc[:, :, 0:E].bitcast(F32R), cw[:], 1.0, None, ALU.mult))
                step(tt(cwc[:, :, E:2 * E], cw[:], cwc[:, :, 0:E], ALU.subtract))

        def weights_in(n, slot):
            dve.wait_ge(ct_ps, n + 1)
            if not (isinstance(n, int) and n == 0):
                dve.wait_ge(cb_ps, 1 + NE1 * (n - 1))
            nc.vector.tensor_copy(cwt[:, slot, :], PM[0:NR, :]).then_inc(misc_free, 1)

        def product(k, i):
            m = PER * k + i
            dve.wait_ge(sg_s, m + 1)
            nc.vector.tensor_tensor(sg[:, i % R, :], PU[i % RG][:], sg[:, i % R, :], ALU.mult).then_inc(gu_free, 1)
            dve.wait_ge(gu_free, m + RG + 1)
            dve.wait_ge(cb_ps, 1 + m + 1)
            dve.wait_ge(hl_done, m + 1)
            nc.vector.tensor_tensor(hf[:, i % R, :], PC[:], sg[:, i % R, :], ALU.mult).then_inc(h_done, 1)

        def residual(n):
            for pr in range(2):
                if pr == 0:
                    dve.wait_ge(y_ps, n + 1)
                else:
                    dve.wait_ge(hid_free, NE1 * (n + 1) + R)
                xs = x1[:, bass.ds(n * TB + 2 * pr, 2), :]
                nc.vector.scalar_tensor_tensor(xs, PY[pr][:].rearrange("p (t d) -> p t d", t=2), tg[:, 1:2], xs,
                                               ALU.mult, ALU.add).then_inc(fin_s, 1)

        def item(k, i, last):
            n, e, ahead = place(k, i, last)
            slot = (i // NE1 + 1) % 2
            product(k, i)
            if e == 1 and i >= NE1:
                residual(n - 1)
            if ahead and e == 0:
                norm_stats(n + 1)
            if ahead and e == 1:
                normalised(n + 1)
            if ahead and e == 2:
                x_lo(n + 1, slot)
            if ahead and e == 3:
                router_out(n + 1)
            if ahead and e == 4:
                routing(n + 1, 0)
            if ahead and e == 5:
                routing(n + 1, 1)
            if ahead and e == 6:
                weights_in(n + 1, slot)

        norm_stats(0)
        normalised(0)
        x_lo(0, 0)
        router_out(0)
        for e in range(NE1):
            dve.wait_ge(w_hi, e + 1)
            nc.vector.tensor_tensor(wxl[:, e, :], wx[:, e, :], wxh[:, e, :], ALU.subtract).then_inc(w_lo, 1)
            if e == 3:
                routing(0, 0)
                routing(0, 1)
                weights_in(0, 0)
        turns(dve, item)
        residual(NBLK - 1)

    @block.tensor
    def _(pe):
        pe.sem_inc(hid_free, R)
        pe.sem_inc(gu_ps, 1)
        pe.sem_inc(cb_ps, 1)
        pe.wait_ge(tab_s, 3)
        ident = con("ident")
        pe.wait_ge(gst_s, 3)

        def split3(a, b):
            return ((a[0], b[1]), (a[1], b[0]), (a[0], b[0]))

        def transposes(n):
            for c in range(C):
                pe.wait_ge(misc_free, 4 * n + c + 1)
                if c == 0:
                    pe.wait_ge(xn_s, TB * (n + 1))
                for j in range(TB):
                    last = nc.tensor.transpose(PM[:, j * P:(j + 1) * P], xn[:, j, c * P:(c + 1) * P], ident)
                last.then_inc(t_ps, 1)

        def router(n, slot):
            pe.wait_ge(misc_free, 4 * n + 3)
            for c in range(C):
                for k, xa in enumerate((xl, xh)):
                    last = nc.tensor.matmul(PM[:], gst[:, c, :], xa[:, slot, c, :], start=(c == 0 and k == 0),
                                            stop=(c == C - 1 and k == 1))
            last.then_inc(gl_ps, 1)

        def logits(n):
            pe.wait_ge(misc_free, 4 * n + 4)
            for j in range(TB):
                last = nc.tensor.matmul(PM[:, j * E:(j + 1) * E], lgT[:, j * P:(j + 1) * P],
                                        con("expert", 0, 2 * E)[:, 0:E], start=True, stop=True)
            last.then_inc(lg_ps, 1)

        def weights_T(n):
            pe.wait_ge(sc_s, n + 1)
            pe.wait_ge(route, NROUTE * (n + 1))
            for j in range(TB):
                last = nc.tensor.transpose(PM[0:NR, j * P:(j + 1) * P], cwc[:, j, :], ident)
            last.then_inc(ct_ps, 1)

        def gate_up(k, i):
            m = PER * k + i
            u, e = divmod(i % PER, NE1)
            pe.wait_ge(gu_free, m + 1)
            pe.wait_ge(w_lo, e + 1)
            for o, out_ in ((0, PG[i % RG]), (C * I, PU[i % RG])):
                first = True
                for c in range(C):
                    w = slice(o + c * I, o + (c + 1) * I)
                    for wa, xa in split3((wxh, wxl), (xh, xl)):
                        last = nc.tensor.matmul(out_[:], wa[:, e, w], xa[:, u, c, :], start=first,
                                                stop=(c == C - 1 and wa is wxh and xa is xh))
                        first = False
            last.then_inc(gu_ps, 1)

        def weight(k, i):
            m = PER * k + i
            u, e = divmod(i % PER, NE1)
            pe.wait_ge(h_done, m + R)
            if e == 0:
                pe.wait_ge(misc_free, 4 * (2 * k + i // NE1 + 1) + 1)
            nc.tensor.matmul(PC[:], selr[:, e, :], cwt[:, u, :], start=True, stop=True).then_inc(cb_ps, 1)

        def down(k, i):
            m = PER * k + i
            n, e = 2 * k + i // NE1, i % NE1
            pe.wait_ge(hl_done, m + R + 1)
            if e == 0:
                pe.wait_ge(fin_s, 2 * n)
            for j in range(TB):
                q = slice(j * P, (j + 1) * P)
                y = PY[j // 2][:, (j % 2) * D:(j % 2 + 1) * D]
                for s, (ha, wa) in enumerate(split3((hh, hl), (wxh, wxl))):
                    last = nc.tensor.matmul(y, ha[:, i % R, q], wa[:, e, 2 * C * I:XW],
                                            start=(e == 0 and s == 0 and j % 2 == 0), stop=(e == NE1 - 1 and s == 2),
                                            skip_group_check=True)
                if j == TB - 1:
                    last.then_inc(hid_free, 1)
                elif e == NE1 - 1 and j == 1:
                    last.then_inc(y_ps, 1)

        def item(k, i, last):
            n, e, ahead = place(k, i, last)
            if not (last and i + 2 >= PER):
                gate_up(k, i + 2)
                weight(k, i + 2)
            down(k, i)
            if ahead and e == 1:
                transposes(n + 1)
            if ahead and e == 2:
                router(n + 1, (i // NE1 + 1) % 2)
            if ahead and e == 3:
                logits(n + 1)
            if ahead and e == 5:
                weights_T(n + 1)

        transposes(0)
        router(0, 0)
        logits(0)
        gate_up(0, 0)
        weights_T(0)
        weight(0, 0)
        gate_up(0, 1)
        weight(0, 1)
        turns(pe, item)


def program(nc, t, out):
    with ExitStack() as outer:
        x1 = outer.enter_context(nc.sbuf_tensor("x1", [P, B * NT, D], F32))
        tg = outer.enter_context(nc.sbuf_tensor("tg", [P, 2], F32))
        with ExitStack() as ctx:
            attention(nc, ctx, x1, tg, t)
        with ExitStack() as ctx:
            experts(nc, ctx, x1, tg, t, out)


def kernel(x, ctx_1024, g_xattn, g_ffn, L0_xattn_Wk, L0_xattn_Wv, L0_xattn_Wq, L0_xattn_Wo, L0_xattn_p_params,
           L0_ffn_gate_w, L0_ffn_correction_bias, L0_ffn_Wg, L0_ffn_Wu, L0_ffn_Wd, L0_ffn_Wg_s, L0_ffn_Wu_s,
           L0_ffn_Wd_s):
    from concourse import bacc
    from concourse.bass_utils import run_bass_kernel_spmd

    def rows(w):
        return w.reshape(C, P, -1).transpose(1, 0, 2)

    f = np.float32
    ctx_t = np.zeros((B, P, C, KPAD), f)
    ctx_t[..., :KL] = np.asarray(ctx_1024).transpose(0, 2, 1).reshape(B, C, P, KL).transpose(0, 2, 1, 3)
    wo = np.zeros((NG, 4, 32, D), f)
    wo[:, :, :HD] = np.asarray(L0_xattn_Wo).T.reshape(NG, 4, HD, D)
    wx = np.zeros((P, NE1, 2 * C * I + D), f)
    for at, many, one in ((0, L0_ffn_Wg, L0_ffn_Wg_s), (C * I, L0_ffn_Wu, L0_ffn_Wu_s)):
        for e in range(NE1):
            w = np.asarray(many)[e] if e < E else np.asarray(one)
            wx[:, e, at:at + C * I] = rows(w).reshape(P, C * I)
    wx[:, :E, 2 * C * I:] = np.asarray(L0_ffn_Wd).transpose(1, 0, 2)
    wx[:, E, 2 * C * I:] = np.asarray(L0_ffn_Wd_s)
    arrays = {
        "x": np.asarray(x).reshape(B * S, D),
        "ctx": ctx_t,
        "cst": constants(),
        "rel": np.tile(np.asarray(L0_xattn_p_params), (P // HD, 1)),
        "gates": np.tile(np.concatenate([np.asarray(g_xattn), np.asarray(g_ffn)])[None], (P, 1)),
        "wq": rows(np.asarray(L0_xattn_Wq).T),
        "wk": rows(np.asarray(L0_xattn_Wk).T),
        "wv": rows(np.asarray(L0_xattn_Wv).T),
        "wo": wo.transpose(1, 2, 0, 3).reshape(P, NG, D),
        "bias": np.tile(np.asarray(L0_ffn_correction_bias)[None], (P, 1)),
        "gw": rows(np.asarray(L0_ffn_gate_w).T),
        "wx": wx,
    }
    arrays = {"in_" + name: np.ascontiguousarray(a) for name, a in arrays.items()}
    nc = bacc.Bacc("TRN2", target_bir_lowering=False, num_devices=1)
    t = {name[3:]: nc.dram_tensor(name, a.shape, F32, kind="ExternalInput").ap() for name, a in arrays.items()}
    t["x"] = t["x"].rearrange("(b t p) d -> b p t d", b=B, p=P)
    out = nc.dram_tensor("out", (B * S, D), F32, kind="ExternalOutput").ap()
    program(nc, t, out.rearrange("(n t p) d -> n p t d", n=B * S // HALF, p=P))
    result = run_bass_kernel_spmd(nc, [arrays], core_ids=[0])
    return result.results[0]["out"].reshape(B, S, D)
```

```python
from contextlib import ExitStack

import concourse.bass as bass
import numpy as np
from concourse import mybir

F32 = mybir.dt.float32
F32R = mybir.dt.float32r
ALU = mybir.AluOpType
ACT = mybir.ActivationFunctionType
AX_X = mybir.AxisListType.X

P = 128
B, S, D = 4, 1024, 256
KL = 154
K1 = KL - P
KPAD = 160
H, HD = 16, 16
DIST = 4
E, I = 8, 128
NT = S // P
C = D // P
HALF = 512
NSTK = H // 2
PAIR = 2 * KL
SW = PAIR + 2 * DIST
NG = H // 4
SCALE = HD ** -0.5
EPS = 1e-5
NEG = -1e30
NE1 = E + 1
ROUTE_SCALE = 2.5

CONST = {}
_at = 0
for _name, _width in (("odd", 2), ("rot", 16), ("band0", P), ("band1", 32), ("causal1", 32), ("head", H),
                      ("mhalf", 4), ("eps", 4), ("strip", 4), ("ident", P), ("causal0", P), ("expert", E + 1),
                      ("lower4", 16), ("lower8", E * E)):
    CONST[_name] = (_at, _at + _width)
    _at += _width
NKEPT = CONST["ident"][0]
NCONST = _at


def constants():
    c = np.zeros((P, NCONST), np.float32)
    p = np.arange(P)[:, None]

    def put(name, value):
        lo, hi = CONST[name]
        c[:, lo:hi] = value

    put("ident", np.eye(P))
    put("odd", (p // HD) % 2 == np.arange(2)[None])
    r, j = np.divmod(np.arange(16)[None], 4)
    put("rot", (p - r) % 4 == j)
    k = np.arange(P)[None]
    put("band0", (p - k >= 0) & (p - k < DIST))
    put("causal0", np.where(k > p, NEG, 0))
    k = np.arange(32)[None] - DIST
    put("band1", (p - k >= 0) & (p - k < DIST))
    put("causal1", np.where(k > p, NEG, 0))
    put("head", p % H == np.arange(H)[None])
    put("mhalf", -0.5)
    put("eps", EPS)
    e = np.arange(E + 1)[None]
    put("expert", ((p % E == e) & (p < 2 * E)) | ((e == E) & (p == 2 * E)))
    for name, n in (("lower4", 4), ("lower8", E)):
        a, b = np.divmod(np.arange(n * n)[None], n)
        put(name, b < a)
    put("strip", p // 32 == np.arange(4)[None])
    return c


def attention(nc, outer, ctx, x1, tg, t):
    def sb(name, shape, dt=F32, where=ctx):
        return where.enter_context(nc.sbuf_tensor(name, shape, dt))

    def sem(name):
        return outer.enter_context(nc.semaphore(name))

    TU = NT // 2
    gates = sb("gates", [P, 2], where=outer)
    wo = sb("wo", [P, 2, D], where=outer)
    va = sb("va", [P, H, 32], where=outer)
    vb = sb("vb", [P, NG, 4, 32], where=outer)
    ex = sb("ex", [P, 2, 5, HALF], where=outer)
    raw = sb("raw", [P, NG, HALF], where=outer)
    dent = sb("dent", [P, H * HALF // P], where=outer)
    at = sb("at", [P, 2, HALF], where=outer)
    wqh, wql = sb("wqh", [P, C, D], F32R), sb("wql", [P, C, D], F32R)
    wk, wv = sb("wk", [P, C, NSTK, 96]), sb("wv", [P, C, D])
    xn = sb("xn", [P, TU, D])
    xth, xtl = sb("xth", [P, C, HALF], F32R), sb("xtl", [P, C, HALF], F32R)
    qh, ql = sb("qh", [P, C, HALF], F32R), sb("ql", [P, C, HALF], F32R)
    cst = sb("cst", [P, NKEPT])

    def con(name, p0=0, p1=P):
        lo, hi = CONST[name]
        return cst[p0:p1, lo:hi]

    rel = sb("rel", [P, 2 * DIST + 1])
    reld = sb("reld", [P, DIST])
    relm = sb("relm", [P, 2, DIST])
    relh, rell = sb("relh", [P, 2, DIST], F32R), sb("rell", [P, 2, DIST], F32R)
    idr, cmask = sb("idr", [P, P], F32R), sb("cmask", [P, P], F32R)
    ctxb = sb("ctxb", [P, C, KPAD])
    stats, mv = sb("stats", [P, TU, 6]), sb("mv", [P, TU, 2])
    veps, rstd = sb("veps", [P, TU]), sb("rstd", [P, TU])
    km = sb("km", [96, NSTK, SW], F32R)
    ks = sb("ks", [P, NSTK, PAIR], F32R)
    k2 = sb("k2", [P, NSTK, P], F32R)
    qs = sb("qs", [P, NSTK, S], F32R)
    vs = sb("vs", [P, D + 64])
    sx = sb("sx", [P, 2, NSTK, SW])
    relc, rotc, relr = sb("relc", [P, H, DIST]), sb("rotc", [P, H, 4, DIST]), sb("relr", [P, H, 4])
    d0, d1 = sb("d0", [P, H, P]), sb("d1", [P, H, 32])
    kp = d0[0:96, :, :].rearrange("p h k -> p (h k)")[:, 0:NSTK * KL].rearrange("p (s k) -> p s k", s=NSTK)
    tp = sb("tp", [P, H, 32])
    mx, nm = sb("mx", [P, NT, H]), sb("nm", [P, NT, 2 * H])
    mt = sb("mt", [2 * H, HALF], F32R)
    wq = raw[:, 0, :].rearrange("p (c d) -> p c d", c=C)
    den_d = nc.dram_tensor("den_d", (4, NG * HALF), F32).ap()
    rden_d = nc.dram_tensor("rden_d", (4, NG * HALF), F32).ap()

    W = [ctx.enter_context(nc.psum_tensor(f"work{i}", [P, HALF], F32)) for i in range(2)]
    SM = ctx.enter_context(nc.psum_tensor("smax", [P, 2, HALF], F32))
    STP = ctx.enter_context(nc.psum_tensor("sT", [P, 2, HALF], F32))
    ST = [STP[:, i, :] for i in range(2)]
    M_START = (SM, STP)
    OT = [ctx.enter_context(nc.psum_tensor(f"oT{i}", [P, HALF], F32)) for i in range(2)]

    x_in, w_in, c_in = [sem(f"x_in{i}") for i in range(B)], sem("w_in"), sem("ctx_in")
    kv_in, x_first = sem("wk_wv_wo_in"), sem("x_first_half_in")
    const_set, pool_set, wq_set, rel_set = sem("const_set"), sem("pool_set"), sem("wq_set"), sem("rel_set")
    rel_step = sem("rel_step")
    waited = sem("waited")
    g_set = sem("g_set")
    stat_s, mv_s, veps_s, rstd_s, xn_s = sem("stat"), sem("mv"), sem("veps"), sem("rstd"), sem("xn")
    xT_ps, xT_hi, work_free = sem("xT_ps"), sem("xT_hi"), sem("work_free")
    k_ps, kp_s, kh_s, kl_s, v_ps = sem("k_ps"), sem("kp"), sem("k_hi"), sem("k_lo"), sem("v_ps")
    q_ps, q_hi = sem("q_ps"), sem("q_hi")
    ks_in, k2_s, v_s = [sem(f"ks_in{g}") for g in range(NG)], sem("k2"), sem("v")
    qs_in, ms_in = [[sem(f"qs_in{h}{part}") for part in range(2)] for h in range(2)], sem("ms_in")
    sm_ps, sx_s, mx_s = sem("scores_ps"), sem("sx"), sem("mx")
    relc_s, d_s, sadd_s, sub_s = sem("relc"), sem("d"), sem("sadd"), sem("sub")
    sub0_s = sem("sub0")
    nmh_s, nm_s, mT_ps, mT_s = sem("nm_hi"), sem("nm"), sem("mT_ps"), sem("mT")
    st_ps, exp_s, pv_ps, raw_s = sem("sT_ps"), sem("exp"), sem("pv_ps"), sem("raw")
    shift_in, den_out, den_in, rden_s, rden_out, rden_in = sem("shift_in"), sem("den_out"), sem("den_in"), sem("rden"), sem("rden_out"), sem("rden_in")
    at_s, y_ps = sem("at"), sem("y_ps")

    NI = 20
    NW0, NWORK = 13, 18
    X_USE, V_USE, Q_USE, K_USE, M_USE, Y_USE = (0, 11), 2, (3, 13), 5, (8, 15), (9, 16)
    K_PARTS = (range(0, 3), range(3, 6), range(6, 8))
    K_STEP, K_READ = (12, 13, 14, 14, 15, 15, 16, 16), (15, 16, 17)
    M0, NM = 3, TU * NSTK // 2

    DIVIDE, TILE0 = ((13, 14), (12, 13)), (10, 11)

    def m_tile(h, p):
        return (0, 2, 1, 3)[p // NG] if h == 0 else TU + p // NG

    def m_stacks(p):
        s = 2 * (0, 2, 1, 3)[p % NG]
        return slice(s, s + 2)

    def body(unit, b, first=False, last=False):
        unit(b, 0, not first, not last)
        unit(b, 1, True, not last)

    def batches(eng, unit):
        body(unit, 0, first=True)
        with eng.Fori(0, B - 2) as k:
            body(unit, k + 1)
        body(unit, B - 1, last=True)

    def scores_done(eng):
        eng.wait_ge(st_ps, NI * 2 * B)

    def exp_done(eng):
        eng.wait_ge(exp_s, NI * 2 * B)

    def raw_done(eng):
        eng.wait_ge(raw_s, NG * 2 * B)

    def residual_done(eng):
        eng.wait_ge(work_free, NW0 + NWORK * B + Y_USE[0] + 2)

    def sync(sp, load_weights):
        for dst, src in ((cst[:], t["cst"][:, 0:NKEPT]), (raw[:, 1, 0:2 * P], t["cst"][:, NKEPT:NKEPT + 2 * P])):
            sp.dma_start(dst, src).then_inc(w_in, 16)
        sp.dma_start(x1[:, 0:TU, :], t["x"][0][:, 0:TU, :]).then_inc(x_first, 16)
        for dst, src in ((raw[:, 0, :], t["wq"].rearrange("p c d -> p (c d)")), (rel[:], t["rel"]), (gates[:], t["gates"])):
            sp.dma_start(dst, src).then_inc(w_in, 16)
        sp.dma_start(ctxb[:], t["ctx"][0]).then_inc(c_in, 16)
        sp.dma_start(wk[:], t["wk"]).then_inc(kv_in, 16)
        sp.dma_start(wv[:], t["wv"]).then_inc(kv_in, 16)
        sp.dma_start(x1[:, TU:NT, :], t["x"][0][:, TU:NT, :]).then_inc(x_in[0], 16)
        sp.dma_start(wo[:], t["wo"]).then_inc(kv_in, 16)
        sp.wait_ge(kv_in, 3 * 16)
        for i in range(1, B):
            sp.dma_start(x1[:, i * NT:(i + 1) * NT, :], t["x"][i]).then_inc(x_in[i], 16)

        def q_stack(h, part):
            n = slice(h * HALF, (h + 1) * HALF)
            for r, src in enumerate((qh, ql, qh)):
                for i in (2 * part, 2 * part + 1):
                    sp.dma_start(qs[32 * r:32 * r + 32, i::4, n].bitcast(F32),
                                 src[32 * i:32 * i + 32, :, :].bitcast(F32)).then_inc(qs_in[h][part], 16)

        def k_stack(g):
            sp.dma_start(ks[0:96, 2 * g:2 * g + 2, :].bitcast(F32), km[:, 2 * g:2 * g + 2, 0:PAIR].bitcast(F32))\
                .then_inc(ks_in[g], 16)

        def m_stack(b, h):
            q0 = HALF // 2 if h == 0 else 0
            sp.wait_ge(mT_s, 2 * b + h + 1)
            sp.dma_start(qs[96:128, :, h * HALF + q0:(h + 1) * HALF].bitcast(F32),
                         mt[:, q0:HALF].unsqueeze(1).broadcast_to([32, NSTK, HALF - q0]).bitcast(F32)).then_inc(ms_in, 16)

        def divisors(u):
            sp.wait_ge(raw_s, NG * (u + 1))
            sp.dma_start(den_d.rearrange("j (g n) -> j g n", g=NG), raw[HD::32, :, :]).then_inc(den_out, 16)
            sp.wait_ge(den_out, 16 * (u + 1))
            sp.dma_start(dent[:], den_d.rearrange("j (p n) -> (j p) n", p=32)).then_inc(den_in, 16)
            for j in range(4):
                sp.dma_start(raw[32 * j + HD:32 * j + 32, 0:2, :], raw[32 * j:32 * j + HD, 2:4, :]).then_inc(shift_in, 16)
            sp.wait_ge(rden_s, u + 1)
            sp.dma_start(rden_d.rearrange("j (p n) -> (j p) n", p=32), dent[:]).then_inc(rden_out, 16)
            sp.wait_ge(rden_out, 16 * (u + 1))
            for j in range(4):
                for k in range(2):
                    sp.dma_start(at[32 * j + HD * k:32 * j + HD * (k + 1), :, :].rearrange("p g n -> p (g n)"),
                                 rden_d[j:j + 1, 2 * k * HALF:2 * (k + 1) * HALF].broadcast_to([HD, 2 * HALF]))\
                        .then_inc(rden_in, 16)

        def unit(b, h, carry, ahead):
            u = 2 * b + h
            if h == 0 and ahead:
                sp.wait_ge(v_ps, b + 1)
                sp.nop().then_inc(waited, 1)
                sp.dma_start(ctxb[:], t["ctx"][b + 1]).then_inc(c_in, 16)
            if carry and (h == 0 or ahead):
                sp.wait_ge(st_ps, NI * u)
                q_stack(1 - h, 1)
            if carry:
                divisors(u - 1)
            if h == 1 and ahead:
                sp.wait_ge(kl_s, 2 * (b + 2))
                sp.nop().then_inc(waited, 1)
                for g in range(NG - 1):
                    sp.wait_ge(st_ps, NI * u + 5 * (g + 1))
                    k_stack(g)
            if ahead:
                sp.wait_ge(work_free, NW0 + NWORK * b + Q_USE[h] + 2)
                sp.nop().then_inc(waited, 1)
                sp.wait_ge(st_ps, NI * u + 15)
                q_stack(h, 0)
            if h == 0 and not ahead:
                for part in range(2):
                    sp.wait_ge(qs_in[1][part], 16 * 6 * B)
                load_weights()
            if h == 0:
                m_stack(b, 1)
            elif ahead:
                m_stack(b + 1, 0)
                sp.wait_ge(st_ps, NI * (u + 1))
                k_stack(NG - 1)

        sp.wait_ge(work_free, 4)
        for part in range(2):
            q_stack(0, part)
        sp.wait_ge(kl_s, 2)
        for g in range(NG):
            k_stack(g)
        sp.wait_ge(work_free, 12)
        for part in range(2):
            q_stack(1, part)
        m_stack(0, 0)
        batches(sp, unit)
        divisors(2 * B - 1)

    def gpsimd(pool):
        nc.gpsimd.memset(va[:], 0.0).then_inc(pool_set, 1)
        nc.gpsimd.memset(vb[:], 0.0).then_inc(pool_set, 1)
        nc.gpsimd.memset(tp[:], 0.0).then_inc(pool_set, 1)
        nc.gpsimd.memset(k2[:].bitcast(F32), 0.0).then_inc(pool_set, 1)
        pool.wait_ge(w_in, 5 * 16)

        def rstd_of(u):
            pool.wait_ge(mv_s, TU * (u + 1))
            nc.gpsimd.tensor_tensor(veps[:], mv[:, :, 1], con("eps"), ALU.add).then_inc(veps_s, 1)
            pool.wait_ge(veps_s, u + 1)
            nc.gpsimd.tensor_tensor(rstd[:], veps[:], con("mhalf"), ALU.pow).then_inc(rstd_s, 1)

        def short_chunk(b):
            pool.wait_ge(kl_s, 2 * (b + 1))
            pool.nop().then_inc(waited, 1)
            for par in range(2):
                src = km[:, par::2, 0:PAIR].rearrange("p s (j k) -> p s j k", j=2)[:, :, :, P:KL]
                dst = k2[0:96, par::2, :].rearrange("p s (q k) -> p s q k", q=4)[:, :, 2 * par:2 * par + 2, 0:K1]
                nc.gpsimd.tensor_copy(dst, src).then_inc(k2_s, 1)

        def values(use):
            pool.wait_ge(work_free, use + 1)
            pool.nop().then_inc(waited, 1)
            nc.gpsimd.tensor_copy(va[:, :, 0:HD], vs[:, 0:D].rearrange("p (h d) -> p h d", h=H)).then_inc(v_s, 1)
            strip = con("strip").unsqueeze(1).unsqueeze(3).broadcast_to([P, NG, 4, HD])
            nc.gpsimd.tensor_tensor(vb[:, :, :, 0:HD], strip,
                                    vs[:, D:D + 64].rearrange("p (g d) -> p g d", g=NG).unsqueeze(2)
                                    .broadcast_to([P, NG, 4, HD]), ALU.mult).then_inc(v_s, 1)

        def near(b, start):
            for i, (dt, band, width) in enumerate(((d0, "band0", P), (d1, "band1", 32))):
                n = 6 * b + 3 * i
                pool.wait_ge(sx_s, 16 * b + 8 * (i + 1))
                if i == 0 and not start:
                    pool.wait_ge(sadd_s, 4 * b)
                if not (i == 0 and start):
                    pool.wait_ge(d_s, 3 * b + i)
                pool.nop().then_inc(waited, 1)
                src = sx[:, i, :, PAIR:SW].rearrange("p s (j d) -> p s j d", j=2)
                nc.gpsimd.tensor_copy(relc[:].rearrange("p (s j) d -> p s j d", j=2), src).then_inc(relc_s, 1)
                pool.wait_ge(relc_s, 2 * b + i + 1)
                rot = con("rot").rearrange("p (r d) -> p r d", r=4).unsqueeze(1).broadcast_to([P, H, 4, DIST])
                nc.gpsimd.tensor_tensor(rotc[:], relc[:].unsqueeze(2).broadcast_to([P, H, 4, DIST]), rot,
                                        ALU.mult).then_inc(rel_step, 1)
                pool.wait_ge(rel_step, n + 1)
                nc.gpsimd.tensor_tensor(rotc[:, :, :, 0:2], rotc[:, :, :, 0:2], rotc[:, :, :, 2:4],
                                        ALU.add).then_inc(rel_step, 1)
                pool.wait_ge(rel_step, n + 2)
                nc.gpsimd.tensor_tensor(relr[:], rotc[:, :, :, 0], rotc[:, :, :, 1], ALU.add).then_inc(rel_step, 1)
                pool.wait_ge(rel_step, n + 3)
                nc.gpsimd.tensor_tensor(
                    dt[:].rearrange("p h (a r) -> p h a r", r=4),
                    relr[:].unsqueeze(2).broadcast_to([P, H, width // 4, 4]),
                    con(band).rearrange("p (a r) -> p a r", r=4).unsqueeze(1).broadcast_to([P, H, width // 4, 4]),
                    ALU.mult).then_inc(d_s, 1)
                if i == 0:
                    pool.wait_ge(sadd_s, 4 * b + 2)
                    keys = sx[:, 0, :, 0:PAIR].rearrange("p s (j k) -> p s j k", j=2)[:, :, :, 0:P]
                    largest = mx[:, 0, :].rearrange("p (s j) -> p s j", j=2).unsqueeze(3).broadcast_to([P, NSTK, 2, P])
                    nc.gpsimd.tensor_tensor(keys, keys, largest, ALU.subtract).then_inc(sub0_s, 1)
            pool.wait_ge(d_s, 3 * b + 2)
            nc.gpsimd.tensor_tensor(d1[:], d1[:], con("causal1").unsqueeze(1).broadcast_to([P, H, 32]),
                                    ALU.add).then_inc(d_s, 1)

        def unit(b, h, carry, ahead):
            u = 2 * b + h
            if ahead:
                rstd_of(u + 2)
            if carry and h == 0:
                pool.wait_ge(pv_ps, NG * u)
                values(NW0 + NWORK * (b - 1) + V_USE)
            if h == 1 and ahead:
                near(b + 1, False)
                pool.wait_ge(st_ps, NI * (u + 1))
                short_chunk(b + 1)

        rstd_of(0)
        rstd_of(1)
        short_chunk(0)
        values(7)
        near(0, True)
        batches(pool, unit)

    def scalar(act):
        act.wait_ge(w_in, 5 * 16)
        nc.scalar.activation(tg[:], gates[:], ACT.Tanh).then_inc(g_set, 1)
        nc.scalar.copy(idr[:], raw[:, 1, 0:P]).then_inc(const_set, 1)
        nc.scalar.mul(wqh[:], wq, SCALE).then_inc(wq_set, 1)

        def constants_late():
            nc.scalar.copy(cmask[:], raw[:, 1, P:2 * P]).then_inc(const_set, 1)
            act.wait_ge(rel_set, 3)
            for r, src in enumerate((relh, relh, rell)):
                nc.scalar.copy(km[32 * r:32 * r + 32, :, PAIR:SW],
                               src[0:32, :, :].rearrange("p j d -> p (j d)").unsqueeze(1)
                               .broadcast_to([32, NSTK, 2 * DIST])).then_inc(const_set, 1)

        def selectors():
            act.wait_ge(pool_set, 4)
            for par in range(2):
                nc.scalar.copy(k2[96:128, par::2, :].rearrange("p s (q k) -> p s q k", q=4)
                               [:, :, 2 * par:2 * par + 2, 0:K1],
                               con("head", 96, 128).rearrange("p (s j) -> p s j", j=2)[:, par::2, :].unsqueeze(3)
                               .broadcast_to([32, NG, 2, K1])).then_inc(const_set, 1)
            nc.scalar.copy(ks[96:128, :, :].rearrange("p s (j k) -> p s j k", j=2),
                           con("head", 96, 128).rearrange("p (s j) -> p s j", j=2).unsqueeze(3)
                           .broadcast_to([32, NSTK, 2, KL])).then_inc(const_set, 1)

        def x_hi(u, use):
            for c in range(C):
                act.wait_ge(xT_ps, 2 * u + c + 1)
                nc.scalar.copy(xth[:, c, :], W[(use + c) % 2][:]).then_inc(xT_hi, 1)

        def k_hi(b, start):
            act.wait_ge(kp_s, 3 * (b + 1))
            if not start:
                act.wait_ge(sm_ps, 4 * NM * b)
                act.wait_ge(k2_s, 2 * b)
                for g in range(NG):
                    act.wait_ge(ks_in[g], 16 * b)
            for j in range(2):
                nc.scalar.mul(km[:, :, j * KL:(j + 1) * KL], kp, con("odd", 0, 96)[:, j:j + 1]).then_inc(kh_s, 1)

        def q_out(u, use, chunks=range(C)):
            for c in chunks:
                act.wait_ge(q_ps, 2 * u + c + 1)
                nc.scalar.copy(qh[:, c, :], W[(use + c) % 2][:]).then_inc(q_hi, 1)

        def near(b, p, bank=SM):
            for k in range(2):
                act.wait_ge(sm_ps, 4 * NM * b + 2 * p + k + 1)
                nc.scalar.copy(sx[:, m_tile(0, p), m_stacks(p).start + k, :], bank[:, k, 0:SW]).then_inc(sx_s, 1)

        def raw_out(u, g, start=False):
            act.wait_ge(pv_ps, NG * u + g + 1)
            if not start:
                act.wait_ge(at_s, 2 * (u - 1) + g % 2 + 1)
            nc.scalar.copy(raw[:, g, :], OT[g % 2][:]).then_inc(raw_s, 1)

        def unit(b, h, carry, ahead):
            u = 2 * b + h
            for i in range(NI):
                g = i // 5
                q0 = P if h == 0 and i % 5 == 4 else 0
                if i % 5 == 0 and not (h == 0 and not carry and g < 2):
                    act.wait_ge(pv_ps, NG * u + g - 1)
                act.wait_ge(st_ps, NI * u + i + 1)
                nc.scalar.activation(ex[:, g % 2, i % 5, q0:HALF], ST[i % 2][:, q0:HALF], ACT.Exp).then_inc(exp_s, 1)
                if i == 5 and carry:
                    raw_out(u - 1, 3, start=(h == 1 and isinstance(b, int) and b == 0))
                if i == 6 and ahead:
                    x_hi(u + 2, NW0 + X_USE[h])
                if i == 11 and ahead:
                    for part in range(2):
                        act.wait_ge(qs_in[1 - h][part], 16 * 6 * (b + h + 1))
                if i in (11, 13) and ahead:
                    q_out(u + 2, NW0 + Q_USE[h], ((i - 11) // 2,))
                if ahead and h == 1:
                    if i == M0:
                        act.wait_ge(sub_s, 3 * (b + 1))
                    if i >= M0 and i - M0 < NM and m_tile(0, i - M0) < 2:
                        near(b + 1, i - M0)
                if i in (14, 17, 19):
                    raw_out(u, (14, 17, 19).index(i), start=not carry)
                if ahead and h == 0 and i == 19:
                    k_hi(b + 1, False)

        x_hi(0, 0)
        q_out(0, 2)
        constants_late()
        k_hi(0, True)
        x_hi(1, 8)
        selectors()
        for p in range(NM):
            if p == NM // 2:
                for part in range(2):
                    act.wait_ge(qs_in[0][part], 16 * 6)
                q_out(1, 10)
            if m_tile(0, p) < 2:
                near(0, p, M_START[p % 2])
        batches(act, unit)
        raw_out(2 * B - 1, 3)

    def vector(dve):
        dve.wait_ge(pool_set, 4)
        nc.vector.memset(va[:, :, HD:HD + 1], 1.0)
        for j in range(4):
            last_one = nc.vector.memset(vb[32 * j:32 * j + K1, :, j, HD:HD + 1], 1.0)
        last_one.then_inc(pool_set, 1)
        def norm_stats(b, h):
            u = 2 * b + h
            for i in range(TU):
                nc.vector.bn_stats(stats[:, i, :], x1[:, b * NT + TU * h + i, :]).then_inc(stat_s, 1)
            dve.wait_ge(stat_s, TU * (u + 1))
            dve.nop().then_inc(waited, 1)
            for i in range(TU):
                nc.vector.bn_aggr(mv[:, i, :], stats[:, i, :]).then_inc(mv_s, 1)

        def normalised(b, h, tiles=range(TU), start=False):
            u = 2 * b + h
            dve.wait_ge(rstd_s, u + 1)
            if not start:
                dve.wait_ge(xT_ps, 2 * u)
            for i in tiles:
                nc.vector.tensor_scalar(xn[:, i, :], x1[:, b * NT + TU * h + i, :], mv[:, i, 0:1], rstd[:, i:i + 1],
                                        ALU.subtract, ALU.mult).then_inc(xn_s, 1)

        def x_lo(u, use):
            for c in range(C):
                dve.wait_ge(xT_hi, 2 * u + c + 1)
                nc.vector.tensor_tensor(xtl[:, c, :], W[(use + c) % 2][:], xth[:, c, :], ALU.subtract)\
                    .then_inc(work_free, 1)

        def q_lo(u, use, chunks=range(C)):
            for c in chunks:
                dve.wait_ge(q_hi, 2 * u + c + 1)
                nc.vector.tensor_tensor(ql[:, c, :], W[(use + c) % 2][:], qh[:, c, :], ALU.subtract)\
                    .then_inc(work_free, 1)

        def k_in(b, use, part):
            stk = K_PARTS[part]
            dve.wait_ge(k_ps, 3 * b + part + 1)
            nc.vector.tensor_scalar(kp[:, stk.start:stk.stop, :],
                                    W[use % 2][0:96, 0:len(stk) * KL].rearrange("p (s k) -> p s k", s=len(stk)),
                                    rel[0:96, 2 * DIST:], None, ALU.add).then_inc(kp_s, 1)
            dve.wait_ge(kp_s, 3 * b + part + 1)
            nc.vector.nop().then_inc(work_free, 1)

        def v_in(b, use, start):
            dve.wait_ge(v_ps, b + 1)
            if not start:
                dve.wait_ge(v_s, 2 * b)
            nc.vector.tensor_copy(vs[:], W[use % 2][:, 0:D + 64]).then_inc(work_free, 1)

        def k_lo(b):
            for j in range(2):
                lo = km[64:96, :, j * KL:(j + 1) * KL]
                dve.wait_ge(kh_s, 2 * b + j + 1)
                nc.vector.scalar_tensor_tensor(lo, kp[64:96, :, :], con("odd", 64, 96)[:, j:j + 1], lo,
                                               ALU.mult, ALU.subtract).then_inc(kl_s, 1)

        def maximum(b, h, p, bank=SM):
            for k in range(2):
                stk = m_stacks(p).start + k
                dve.wait_ge(sm_ps, 2 * NM * (2 * b + h) + 2 * p + k + 1)
                nc.vector.reduce_max(mx[:, m_tile(h, p), 2 * stk:2 * stk + 2],
                                     bank[:, k, 0:PAIR].rearrange("p (j k) -> p j k", j=2), AX_X).then_inc(mx_s, 1)

        def by_stack(ap):
            return ap.rearrange("p (s j) k -> p s j k", j=2)

        def over(ap, n):
            return ap.rearrange("p (s j) -> p s j", j=2).unsqueeze(3).broadcast_to([P, NSTK, 2, n])

        def tile0(b, part):
            keys = sx[:, 0, :, 0:PAIR].rearrange("p s (j k) -> p s j k", j=2)[:, :, :, 0:P]
            if part == 0:
                dve.wait_ge(d_s, 3 * b + 1)
                nc.vector.tensor_tensor(keys, keys, by_stack(d0[:]), ALU.add).then_inc(sadd_s, 1)
            else:
                dve.wait_ge(sadd_s, 4 * b + 1)
                nc.vector.reduce_max(mx[:, 0, :], keys, AX_X).then_inc(sadd_s, 1)

        def tile1(b, part):
            keys = sx[:, 1, :, 0:PAIR].rearrange("p s (j k) -> p s j k", j=2)
            if part == 0:
                dve.wait_ge(d_s, 3 * b + 3)
                nc.vector.tensor_tensor(keys[:, :, :, P - DIST:KL], keys[:, :, :, P - DIST:KL],
                                        by_stack(d1[:, :, 0:K1 + DIST]), ALU.add).then_inc(sadd_s, 1)
            elif part == 1:
                dve.wait_ge(sadd_s, 4 * b + 3)
                nc.vector.reduce_max(mx[:, 1, :], keys, AX_X).then_inc(sadd_s, 1)
            else:
                dve.wait_ge(sadd_s, 4 * b + 4)
                for half in (slice(0, NSTK // 2), slice(NSTK // 2, NSTK)):
                    nc.vector.tensor_tensor(keys[:, half, :, 0:P], keys[:, half, :, 0:P],
                                            over(mx[:, 1, :], P)[:, half], ALU.subtract).then_inc(sub_s, 1)
                    if half.start == 0:
                        nc.vector.tensor_tensor(by_stack(tp[:, :, 0:K1]), keys[:, :, :, P:KL], over(mx[:, 1, :], K1),
                                                ALU.subtract).then_inc(sub_s, 1)

        def minus_max(b, h, start=False):
            r = slice(2 if h == 0 else TU, TU * (h + 1))
            dve.wait_ge(mx_s, 48 * b + (16 if h == 0 else 48))
            if not start:
                dve.wait_ge(mT_ps, 2 * b + h)
            nc.vector.tensor_scalar(nm[:, r, 0:H].bitcast(F32R), mx[:, r, :], -1.0, None, ALU.mult).then_inc(nmh_s, 1)
            dve.wait_ge(nmh_s, 2 * b + h + 1)
            nc.vector.scalar_tensor_tensor(nm[:, r, H:2 * H], mx[:, r, :], -1.0, nm[:, r, 0:H],
                                           ALU.mult, ALU.subtract).then_inc(nm_s, 1)

        def max_out(b, h, use, start=False):
            u = 2 * b + h
            q0 = HALF // 2 if h == 0 else 0
            dve.wait_ge(mT_ps, u + 1)
            if not start:
                dve.wait_ge(ms_in, 16 * u)
            nc.vector.tensor_copy(mt[:, q0:HALF], W[use % 2][0:32, q0:HALF]).then_inc(mT_s, 1)
            dve.wait_ge(mT_s, u + 1)
            nc.vector.nop().then_inc(work_free, 1)

        def reciprocals(u):
            dve.wait_ge(den_in, 16 * (u + 1))
            nc.vector.reciprocal(dent[:], dent[:]).then_inc(rden_s, 1)

        def divide(u, groups=range(2)):
            dve.wait_ge(rden_in, 128 * (u + 1))
            dve.wait_ge(shift_in, 64 * (u + 1))
            for g in groups:
                nc.vector.tensor_tensor(at[:, g, :], raw[:, g, :], at[:, g, :], ALU.mult).then_inc(at_s, 1)

        def residual(b, h, pr, use):
            dve.wait_ge(y_ps, 2 * (2 * b + h) + pr + 1)
            tile = b * NT + TU * h + 2 * pr
            xs = x1[:, bass.ds(tile, 2), :]
            nc.vector.scalar_tensor_tensor(xs, W[use % 2][:].rearrange("p (t d) -> p t d", t=2), tg[:, 0:1], xs,
                                           ALU.mult, ALU.add).then_inc(work_free, 1)

        def unused(n, b, use):
            dve.wait_ge(work_free, NW0 + NWORK * b + use)
            dve.sem_inc(work_free, n)

        def unit(b, h, carry, ahead):
            u = 2 * b + h
            mb, mh = b + h, 1 - h
            diagonal = h == 1 and ahead
            for i in range(NI):
                p = i - M0
                if 0 <= p < NM and (h == 0 or (ahead and m_tile(mh, p) >= 2)):
                    maximum(mb, mh, p)
                if i == 0 and ahead:
                    norm_stats(b + 1, h)
                if i in (3, 4) and ahead:
                    normalised(b + 1, h, (2 * (i - 3), 2 * (i - 3) + 1))
                if i == 6 and ahead:
                    x_lo(u + 2, NW0 + X_USE[h])
                if i in K_READ and ahead and h == 0:
                    part = K_READ.index(i)
                    k_in(b + 1, NW0 + K_USE + part, part)
                if i == 10 and ahead and h == 0:
                    v_in(b + 1, NW0 + V_USE, False)
                if i == 9 and carry:
                    reciprocals(u - 1)
                if i in DIVIDE[h] and carry:
                    divide(u - 1, (DIVIDE[h].index(i),))
                if diagonal and i in TILE0:
                    tile0(b + 1, TILE0.index(i))
                if i in (11, 13) and ahead:
                    q_lo(u + 2, NW0 + Q_USE[h], ((i - 11) // 2,))
                if i == 12 and not ahead:
                    unused(M_USE[h] - X_USE[h], b, X_USE[h])
                if i == 18:
                    if h == 0 or ahead:
                        minus_max(mb, mh)
                        if diagonal:
                            tile1(b + 1, 0)
                        max_out(mb, mh, NW0 + M_USE[h])
                    else:
                        unused(1, b, M_USE[h])
                if i == 19:
                    if diagonal:
                        tile1(b + 1, 1)
                        tile1(b + 1, 2)
                    if h == 0 and ahead:
                        k_lo(b + 1)
                    if carry:
                        for pr in range(2):
                            residual(b - 1 + h, 1 - h, pr, NW0 + Y_USE[h] + pr)
                    else:
                        unused(2, b, Y_USE[h])

        dve.wait_ge(x_first, 16)
        norm_stats(0, 0)
        dve.wait_ge(w_in, 5 * 16)
        dve.wait_ge(wq_set, 1)
        nc.vector.scalar_tensor_tensor(wql[:], wq, SCALE, wqh[:], ALU.mult, ALU.subtract).then_inc(wq_set, 1)
        nc.vector.tensor_scalar(reld[:], rel[:, DIST:2 * DIST], rel[:, 2 * DIST:], None, ALU.subtract)\
            .then_inc(rel_set, 1)
        dve.wait_ge(rel_set, 1)
        for j in range(2):
            nc.vector.tensor_scalar(relm[:, j, :], reld[:], con("odd")[:, j:j + 1], None, ALU.mult)
            last_one = nc.vector.tensor_scalar(relh[:, j, :], reld[:], con("odd")[:, j:j + 1], None, ALU.mult)
        last_one.then_inc(rel_set, 1)
        dve.wait_ge(rel_set, 2)
        nc.vector.tensor_tensor(rell[:], relm[:], relh[:], ALU.subtract).then_inc(rel_set, 1)
        normalised(0, 0, start=True)
        x_lo(0, 0)
        q_lo(0, 2)
        dve.wait_ge(x_in[0], 16)
        norm_stats(0, 1)
        normalised(0, 1)
        for part in range(3):
            k_in(0, 4 + part, part)
        v_in(0, 7, True)
        k_lo(0)
        x_lo(1, 8)
        for p in range(NM):
            if p == NM // 2:
                q_lo(1, 10)
            if m_tile(0, p) >= 2:
                maximum(0, 0, p, M_START[p % 2])
            if p == 8:
                for part in range(2):
                    tile0(0, part)
        minus_max(0, 0, start=True)
        max_out(0, 0, 12, start=True)
        for part in range(3):
            tile1(0, part)
        for i in range(1, B):
            dve.wait_ge(x_in[i], 16)
        dve.wait_ge(g_set, 1)
        batches(dve, unit)

        def last_residual():
            unused(Y_USE[0], B, 0)
            for pr in range(2):
                residual(B - 1, 1, pr, NW0 + Y_USE[0] + pr)

        return lambda: reciprocals(2 * B - 1), lambda: divide(2 * B - 1), last_residual

    def tensor(pe):
        pe.wait_ge(w_in, 5 * 16)
        pe.wait_ge(wq_set, 2)
        ident = idr[:].bitcast(F32)
        pe.wait_ge(const_set, 1)

        def work(b, use):
            pe.wait_ge(work_free, NW0 + NWORK * b + use - 1)
            return W[(NW0 + use) % 2]

        START = NWORK - NW0

        def transposes(u, b, use, chunks=range(C)):
            for c in chunks:
                if not (isinstance(u, int) and u == 0):
                    pe.wait_ge(work_free, NW0 + NWORK * b + use + c - 1)
                w = W[(NW0 + use + c) % 2]
                pe.wait_ge(xn_s, TU * (u + 1))
                for j in range(TU):
                    last_one = nc.tensor.transpose(w[:, j * P:(j + 1) * P], xn[:, j, c * P:(c + 1) * P], ident)
                last_one.then_inc(xT_ps, 1)

        def keys(b, use_b, use, stacks=range(NSTK)):
            for s in stacks:
                part, k = s // 3, s % 3
                if k == 0:
                    pe.wait_ge(c_in, 16 * (b + 1))
                    pe.wait_ge(work_free, NW0 + NWORK * use_b + use + part - 1)
                for c in range(C):
                    last_one = nc.tensor.matmul(W[(NW0 + use + part) % 2][0:96, k * KL:(k + 1) * KL], wk[:, c, s, :],
                                                ctxb[:, c, 0:KL], start=(c == 0), stop=(c == C - 1))
                if s + 1 == K_PARTS[part].stop:
                    last_one.then_inc(k_ps, 1)

        def values_in(b, use_b, use, parts=range(5)):
            for part in parts:
                if part == 0:
                    pe.wait_ge(c_in, 16 * (b + 1))
                    pe.wait_ge(work_free, NW0 + NWORK * use_b + use - 1)
                w = W[(NW0 + use) % 2]
                j = part - 1
                for c in range(C):
                    if part == 0:
                        nc.tensor.matmul(w[:, 0:D], ctxb[:, c, 0:P], wv[:, c, :], start=(c == 0), stop=(c == C - 1))
                    else:
                        last_one = nc.tensor.matmul(w[32 * j:32 * j + 32, D:D + 64], ctxb[:, c, P:KPAD],
                                                    wv[:, c, :].rearrange("p (g j d) -> p g j d", g=NG, j=4)[:, :, j, :],
                                                    start=(c == 0), stop=(c == C - 1))
                if part == 4:
                    last_one.then_inc(v_ps, 1)

        def queries(use_b, x_use, use, pieces=range(4)):
            for m, c in (divmod(piece, C) for piece in pieces):
                if c == 0:
                    pe.wait_ge(work_free, NW0 + NWORK * use_b + x_use + 2)
                    pe.wait_ge(work_free, NW0 + NWORK * use_b + use + m - 1)
                w = W[(NW0 + use + m) % 2]
                for k, (wa, xa) in enumerate(((wql, xth), (wqh, xtl), (wqh, xth))):
                    last_one = nc.tensor.matmul(w[:], wa[:, c, m * P:(m + 1) * P], xa[:, c, :],
                                                start=(c == 0 and k == 0), stop=(c == C - 1 and k == 2))
                if c == C - 1:
                    last_one.then_inc(q_ps, 1)

        def max_scores(b, h, p, k):
            if p in (0, 2) and k == 0:
                pe.wait_ge(qs_in[h][p // 2], 16 * 6 * (b + 1))
            if h == 0 and p == 0 and k == 0:
                pe.wait_ge(kl_s, 2 * (b + 1))
            if h == 1:
                pe.wait_ge(mx_s, 48 * b + 15 + 2 * p + k)
            elif p == 0:
                pe.wait_ge(mx_s, 48 * b - 1 + k)
            elif p <= 4:
                pe.wait_ge(sx_s, 16 * b + 2 * p - 1 + k)
            elif p <= 8:
                pe.wait_ge(mx_s, 48 * b + 2 * p - 9 + k)
            elif p <= 12:
                pe.wait_ge(sx_s, 16 * b + 2 * p - 9 + k)
            else:
                pe.wait_ge(mx_s, 48 * b + 2 * p - 17 + k)
            stack_scores(m_tile(h, p), p, k, SM)

        def stack_scores(tile, p, k, bank):
            width = SW if tile < 2 else PAIR
            s = m_stacks(p).start + k
            last_one = nc.tensor.matmul(bank[:, k, 0:width], qs[0:96, s, tile * P:(tile + 1) * P], km[:, s, 0:width],
                                        start=True, stop=True)
            if tile == 0:
                last_one = nc.tensor.matmul(bank[:, k, 0:PAIR].rearrange("p (j k) -> p j k", j=2)[:, :, 0:P], idr[:],
                                            cmask[:].unsqueeze(1).broadcast_to([P, 2, P]), start=False, stop=True,
                                            skip_group_check=True)
            last_one.then_inc(sm_ps, 1)

        def max_T(b, h, use_b, use):
            w = work(use_b, use)
            pe.wait_ge(nm_s, 2 * b + h + 1)
            for j in range(2 - 2 * h, TU):
                last_one = nc.tensor.transpose(w[0:32, j * P:(j + 1) * P], nm[:, TU * h + j, :], ident)
            last_one.then_inc(mT_ps, 1)

        def score(b, h, step, start):
            u = 2 * b + h
            g, i = divmod(step, 5)
            if not (start and step < 2):
                pe.wait_ge(exp_s, NI * u + step - 1)
            if step == 0:
                pe.wait_ge(ms_in, 16 * (u + 1))
            if h == 0:
                if step == 0:
                    pe.wait_ge(sub0_s, b + 1)
                    pe.wait_ge(sub_s, 3 * b + 2)
                if step == 2 * 5:
                    pe.wait_ge(sub_s, 3 * (b + 1))
                if i == 0:
                    pe.wait_ge(ks_in[g], 16 * (b + 1))
                if step == 4:
                    pe.wait_ge(k2_s, 2 * (b + 1))
            out = ST[step % 2]
            q0 = HALF // 2 if h == 0 else 0
            q = slice(h * HALF + q0, (h + 1) * HALF)
            if i < 4:
                s, j = divmod(4 * g + i, 2)
                if h == 0:
                    for k in range(2):
                        nc.tensor.transpose(out[:, k * P:(k + 1) * P], sx[:, k, s, j * KL:j * KL + P], ident)
                last_one = nc.tensor.matmul(out[:, q0:HALF], ks[:, s, j * KL:j * KL + P], qs[:, s, q], start=True,
                                            stop=True)
            else:
                if h == 0:
                    nc.tensor.transpose(out[:, P:2 * P], tp[:, 4 * g:4 * g + 4, :].rearrange("p h k -> p (h k)"), ident)
                for k in range(2):
                    last_one = nc.tensor.matmul(out[:, q0:HALF], k2[:, 2 * g + k, :], qs[:, 2 * g + k, q],
                                                start=(k == 0), stop=(k == 1))
            last_one.then_inc(st_ps, 1)

        def values(b, h, g, i, start=False):
            u = 2 * b + h
            short = i // 2
            if i % 2 == 0:
                pe.wait_ge(exp_s, NI * u + 5 * g + 4 + short)
            if i == 0:
                if not (start and g < 2):
                    pe.wait_ge(raw_s, NG * u + g - 1)
                if h == 0 and g == 0:
                    pe.wait_ge(v_s, 2 * (b + 1))
            q0 = P if h == 0 and short else 0
            for j in (2 * (i % 2), 2 * (i % 2) + 1):
                e = ex[:, g % 2, 4 if short else j, q0:HALF]
                v = vb[:, g, j, :] if short else va[:, 4 * g + j, :]
                last_one = nc.tensor.matmul(OT[g % 2][32 * j:32 * j + 32, q0:HALF], v, e, start=not short, stop=bool(short))
            if i == 3:
                last_one.then_inc(pv_ps, 1)

        def project(b, h, pr, use_b, use):
            pe.wait_ge(at_s, 2 * (2 * b + h + 1))
            w = work(use_b, use)
            for k in range(2):
                j = 2 * pr + k
                for g in range(2):
                    last_one = nc.tensor.matmul(w[:, k * D:(k + 1) * D], at[:, g, j * P:(j + 1) * P], wo[:, g, :],
                                                start=(g == 0), stop=(g == 1))
            last_one.then_inc(y_ps, 1)

        def unit(b, h, carry, ahead):
            u = 2 * b + h
            start = h == 0 and not carry
            for i in range(NI):
                seeks = 0 <= i - M0 < NM and (h == 0 or ahead)
                score(b, h, i, start)
                if seeks:
                    max_scores(b + h, 1 - h, i - M0, 0)
                if i in (1, 2, 3, 4) and carry:
                    values(b - 1 + h, 1 - h, NG - 1, i - 1)
                if i > 5 and i % 5 > 0:
                    values(b, h, i // 5 - 1, i % 5 - 1, start)
                if seeks:
                    max_scores(b + h, 1 - h, i - M0, 1)
                if i in (5, 6) and ahead:
                    transposes(u + 2, b, X_USE[h], (i - 5,))
                if i in (7, 8) and ahead and h == 0:
                    values_in(b + 1, b, V_USE, ((0, 1), (2, 3, 4))[i - 7])
                if i in (9, 10, 11, 12) and ahead:
                    queries(b, X_USE[h], Q_USE[h], (i - 9,))
                if ahead and h == 0:
                    keys(b + 1, b, K_USE, [s for s in range(NSTK) if K_STEP[s] == i])
                if i == 19:
                    if h == 0 or ahead:
                        max_T(b + h, 1 - h, b, M_USE[h])
                    if carry:
                        for pr in range(2):
                            project(b - 1 + h, 1 - h, pr, b, Y_USE[h] + pr)

        transposes(0, -1, START)
        queries(-1, START, START + 2)
        pe.wait_ge(kv_in, 3 * 16)
        keys(0, -1, START + 4)
        values_in(0, -1, START + 7)
        transposes(1, -1, START + 8)
        pe.wait_ge(pool_set, 5)
        pe.wait_ge(const_set, 5)
        for p in range(NM):
            if p == NM // 2:
                queries(-1, START + 8, START + 10)
            if p in (0, 2):
                pe.wait_ge(qs_in[0][p // 2], 16 * 6)
            if p == 0:
                pe.wait_ge(kl_s, 2)
            for k in range(2):
                if 2 <= p < 6:
                    pe.wait_ge(sx_s, 2 * p - 3 + k)
                elif 6 <= p < 10:
                    pe.wait_ge(mx_s, 2 * p - 11 + k)
                elif 10 <= p < 14:
                    pe.wait_ge(sx_s, 2 * p - 11 + k)
                elif p >= 14:
                    pe.wait_ge(mx_s, 2 * p - 19 + k)
                stack_scores(m_tile(0, p), p, k, M_START[p % 2])
        max_T(0, 0, -1, START + 12)
        pe.wait_ge(const_set, 8)
        batches(pe, unit)
        for i in range(4):
            values(B - 1, 1, NG - 1, i)

        def finish():
            for pr in range(2):
                project(B - 1, 1, pr, B, Y_USE[0] + pr)

        return finish

    return sync, gpsimd, scalar, vector, tensor, scores_done, exp_done, raw_done, residual_done


def experts(nc, ctx, x1, tg, t, out, attend):
    (attend_sync, attend_gpsimd, attend_scalar, attend_vector, attend_tensor, scores_done, exp_done, raw_done,
     residual_done) = attend

    def sb(name, shape, dt=F32):
        return ctx.enter_context(nc.sbuf_tensor(name, shape, dt))

    def sem(name):
        return ctx.enter_context(nc.semaphore(name))

    TB = HALF // P
    NBLK = B * S // HALF
    NR = 2 * E + 1
    XW = 2 * C * I + D

    wx = sb("wx", [P, NE1, XW])
    cst = sb("cst2", [P, NCONST])

    def con(name, p0=0, p1=P):
        lo, hi = CONST[name]
        return cst[p0:p1, lo:hi]

    bias = sb("bias", [P, E])
    gw = sb("gw", [P, C, E])
    gwh, gwl = sb("gwh", [P, C, E], F32R), sb("gwl", [P, C, E], F32R)
    gst = sb("gst", [P, C, P], F32R)
    wxh, wxl = sb("wxh", [P, NE1, XW], F32R), sb("wxl", [P, NE1, XW], F32R)
    selr = sb("selr", [NR, NE1, P], F32R)
    stats, mv = sb("stats2", [P, TB, 6]), sb("mv2", [P, TB, 2])
    veps, rstd = sb("veps2", [P, TB]), sb("rstd2", [P, TB])
    xn = sb("xn2", [P, TB, D])
    xh, xl = sb("x2h", [P, 2, C, HALF], F32R), sb("x2l", [P, 2, C, HALF], F32R)
    lgT = sb("lgT", [2 * E, HALF])
    sc = sb("sc", [P, TB, E])
    scc = sb("scc", [P, TB, E])
    gs = sb("gs", [P, TB, E // 2])
    g_gt, g_eq = sb("g_gt", [P, TB, 4, 4]), sb("g_eq", [P, TB, 4, 4])
    rank_g, rank_e = sb("rank_g", [P, TB, 4]), sb("rank_e", [P, TB, E])
    vch = sb("vch", [P, TB, E])
    e_gt, e_eq = sb("e_gt", [P, TB, E, E]), sb("e_eq", [P, TB, E, E])
    wsel = sb("wsel", [P, TB, E])
    winv = sb("winv", [P, TB])
    cw = sb("cw", [P, TB, E])
    cwc = sb("cwc", [P, TB, NR])
    cwt = sb("cwt", [NR, 2, HALF], F32R)
    R = 3
    sg = sb("sg", [P, R, HALF])
    hh, hl = sb("hh", [P, R, HALF], F32R), sb("hl", [P, R, HALF], F32R)

    def bank(name):
        return ctx.enter_context(nc.psum_tensor(name, [P, HALF], F32))

    PY = [bank("py0"), bank("py1")]
    PG = [bank("pg0"), bank("pg1")]
    PM, PC = bank("pm"), bank("pc")
    PU = [bank("pu0"), bank("pu1")]

    w_in, c_in = [sem(f"wx_in{e}") for e in range(NE1)], sem("const_in")
    w_hi, w_lo, gst_s, tab_s = sem("wx_hi"), sem("wx_lo"), sem("router_set"), sem("tables_set")
    stat_s, mv_s, veps_s, rstd_s, xn_s = sem("stat_b"), sem("mv_b"), sem("veps_b"), sem("rstd_b"), sem("xn_b")
    t_ps, t_hi, misc_free = sem("xT_ps_b"), sem("xT_hi_b"), sem("misc_free")
    gl_ps, lgT_s, lg_ps, sc_s = sem("router_ps"), sem("router_out"), sem("logits_ps"), sem("scores_set")
    route, ct_ps = sem("route_step"), sem("cwT_ps")
    sg_s, gu_ps, gu_free, cb_ps, h_done = sem("silu_set"), sem("gate_up_ps"), sem("gate_up_free"), sem("cw_ps"), sem("hidden_done")
    waited = sem("waited_b")
    hh_s, hl_done, hid_free = sem("hidden_hi"), sem("hidden_lo_done"), sem("hidden_free")
    fin_s, out_s, y_ps = sem("fin"), sem("out_stored"), sem("y_ps_b")
    block = ctx.enter_context(nc.Block())
    RG = 2
    PER = 2 * NE1
    NROUTE = 20

    LAST = NBLK // 2 - 1

    def turns(eng, item):
        item(0, 0, False)
        item(0, 1, False)
        with eng.Fori(0, LAST) as k:
            for i in range(2, PER + 2):
                item(k, i, False)
        for i in range(2, PER):
            item(LAST, i, True)

    def place(k, i, last):
        return 2 * k + i // NE1, i % NE1, not (last and i >= NE1)

    @block.sync
    def _(sp):
        def load_weights():
            for dst, src in ((cst[:], t["cst"]), (bias[:], t["bias"]), (gw[:], t["gw"])):
                sp.dma_start(dst, src).then_inc(c_in, 16)
            for e in range(NE1):
                sp.dma_start(wx[:, e, :], t["wx"][:, e, :]).then_inc(w_in[e], 16)

        attend_sync(sp, load_weights)
        with sp.Fori(0, NBLK) as n:
            sp.wait_ge(fin_s, 2 * (n + 1))
            sp.nop().then_inc(waited, 1)
            sp.dma_start(out[n], x1[:, bass.ds(n * TB, TB), :]).then_inc(out_s, 16)
        sp.wait_ge(out_s, 16 * NBLK)

    @block.gpsimd
    def _(pool):
        attend_gpsimd(pool)
        scores_done(pool)
        nc.gpsimd.memset(gst[:].bitcast(F32), 0.0).then_inc(gst_s, 1)
        nc.gpsimd.memset(cwc[:], 1.0).then_inc(gst_s, 1)
        pool.sem_inc(hl_done, R)
        pool.wait_ge(c_in, 3 * 16)

        def rstd_of(n):
            pool.wait_ge(mv_s, TB * (n + 1))
            nc.gpsimd.tensor_tensor(veps[:], mv[:, :, 1], con("eps"), ALU.add).then_inc(veps_s, 1)
            pool.wait_ge(veps_s, n + 1)
            nc.gpsimd.tensor_tensor(rstd[:], veps[:], con("mhalf"), ALU.pow).then_inc(rstd_s, 1)

        def hidden_lo(k, i):
            m = PER * k + i
            pool.wait_ge(hh_s, m + 1)
            pool.wait_ge(hid_free, m + 1)
            nc.gpsimd.tensor_tensor(hl[:, i % R, :], sg[:, i % R, :], hh[:, i % R, :], ALU.subtract).then_inc(hl_done, 1)

        def item(k, i, last):
            n, e, ahead = place(k, i, last)
            hidden_lo(k, i)
            if not last and e == NE1 - 1:
                rstd_of(n + 2)

        rstd_of(0)
        rstd_of(1)
        turns(pool, item)

    @block.scalar
    def _(act):
        attend_scalar(act)
        scores_done(act)
        act.sem_inc(misc_free, 1)
        act.wait_ge(c_in, 3 * 16)
        nc.scalar.copy(gwh[:], gw[:]).then_inc(tab_s, 1)
        nc.scalar.copy(selr[:], cst[0:NR, CONST["expert"][0]:CONST["expert"][1]].unsqueeze(2)
                       .broadcast_to([NR, NE1, P])).then_inc(tab_s, 1)

        def x_hi(n, slot, chunks=range(C)):
            if not (isinstance(n, int) and n == 0):
                act.wait_ge(gu_ps, 1 + NE1 * (n - 1))
            for c in chunks:
                act.wait_ge(t_ps, 2 * n + c + 1)
                nc.scalar.copy(xh[:, slot, c, :], PM[:]).then_inc(t_hi, 1)

        def scores(n):
            act.wait_ge(lg_ps, n + 1)
            act.wait_ge(route, NROUTE * n)
            nc.scalar.activation(sc[:], PM[:, 0:TB * E].rearrange("p (t e) -> p t e", t=TB), ACT.Sigmoid)\
                .then_inc(sc_s, 1)

        def silu(k, i):
            m = PER * k + i
            act.wait_ge(gu_ps, 1 + m + 1)
            act.wait_ge(hl_done, m + 1)
            nc.scalar.activation(sg[:, i % R, :], PG[i % RG][:], ACT.Silu).then_inc(sg_s, 1)

        def hidden_hi(k, i):
            m = PER * k + i
            act.wait_ge(h_done, m + R + 1)
            act.wait_ge(hid_free, m + 1)
            nc.scalar.copy(hh[:, i % R, :], sg[:, i % R, :]).then_inc(hh_s, 1)

        def item(k, i, last):
            n, e, ahead = place(k, i, last)
            if not (last and i == PER - 1):
                silu(k, i + 1)
            hidden_hi(k, i)
            if ahead and e in (1, 2):
                x_hi(n + 1, (i // NE1 + 1) % 2, (e - 1,))
            if ahead and e == 4:
                scores(n + 1)

        for e in range(NE1):
            if e == 1:
                x_hi(0, 0)
            act.wait_ge(w_in[e], 16)
            nc.scalar.copy(wxh[:, e, :], wx[:, e, :]).then_inc(w_hi, 1)
            if e == 4:
                scores(0)
        silu(0, 0)
        turns(act, item)

    @block.vector
    def _(dve):
        attend_reciprocals, attend_divide, attend_residual = attend_vector(dve)
        scores_done(dve)
        dve.sem_inc(gu_free, RG)
        dve.sem_inc(h_done, R)
        dve.wait_ge(c_in, 3 * 16)
        dve.wait_ge(tab_s, 1)
        nc.vector.tensor_tensor(gwl[:], gw[:], gwh[:], ALU.subtract).then_inc(tab_s, 1)
        dve.wait_ge(tab_s, 3)
        dve.wait_ge(gst_s, 2)
        nc.vector.tensor_copy(gst[:, :, 0:E], gwh[:].bitcast(F32))
        nc.vector.tensor_copy(gst[:, :, E:2 * E], gwl[:].bitcast(F32)).then_inc(gst_s, 1)

        def norm_stats(n):
            for i in range(TB):
                nc.vector.bn_stats(stats[:, i, :], x1[:, n * TB + i, :]).then_inc(stat_s, 1)
            dve.wait_ge(stat_s, TB * (n + 1))
            dve.nop().then_inc(waited, 1)
            for i in range(TB):
                nc.vector.bn_aggr(mv[:, i, :], stats[:, i, :]).then_inc(mv_s, 1)

        def normalised(n):
            dve.wait_ge(rstd_s, n + 1)
            dve.wait_ge(t_ps, 2 * n)
            for i in range(TB):
                nc.vector.tensor_scalar(xn[:, i, :], x1[:, n * TB + i, :], mv[:, i, 0:1], rstd[:, i:i + 1],
                                        ALU.subtract, ALU.mult).then_inc(xn_s, 1)

        def x_lo(n, slot, chunks=range(C)):
            for c in chunks:
                dve.wait_ge(t_hi, 2 * n + c + 1)
                nc.vector.tensor_tensor(xl[:, slot, c, :], PM[:], xh[:, slot, c, :], ALU.subtract).then_inc(misc_free, 1)

        def router_out(n):
            dve.wait_ge(gl_ps, n + 1)
            dve.wait_ge(lg_ps, n)
            nc.vector.tensor_copy(lgT[:], PM[0:2 * E, :]).then_inc(misc_free, 1)

        def routing(n, part):
            at = [0 if part == 0 else 8]

            def step(ins):
                ins.then_inc(route, 1)
                at[0] += 1
                dve.wait_ge(route, NROUTE * n + at[0])

            def along(ap, axis, shape):
                return ap.unsqueeze(axis).broadcast_to(shape)

            def lower(k):
                return con(f"lower{k}").rearrange("p (a b) -> p a b", a=k).unsqueeze(1).broadcast_to([P, TB, k, k])

            tt = nc.vector.tensor_tensor
            if part == 0:
                dve.wait_ge(sc_s, n + 1)
                step(tt(scc[:], sc[:], bias[:].unsqueeze(1).broadcast_to([P, TB, E]), ALU.add))
                step(tt(gs[:], scc[:, :, 0::2], scc[:, :, 1::2], ALU.add))
                sh = [P, TB, 4, 4]
                step(tt(g_gt[:], along(gs[:], 2, sh), along(gs[:], 3, sh), ALU.is_gt))
                step(tt(g_eq[:], along(gs[:], 2, sh), along(gs[:], 3, sh), ALU.is_equal))
                step(tt(g_eq[:], g_eq[:], lower(4), ALU.mult))
                step(tt(g_gt[:], g_gt[:], g_eq[:], ALU.add))
                step(nc.vector.reduce_sum(rank_g[:], g_gt[:], AX_X))
                step(nc.vector.scalar_tensor_tensor(
                    vch[:].rearrange("p t (g j) -> p t g j", j=2), along(rank_g[:], 3, [P, TB, 4, 2]), 2.0,
                    scc[:].rearrange("p t (g j) -> p t g j", j=2), ALU.is_lt, ALU.mult))
            else:
                sh = [P, TB, E, E]
                step(tt(e_gt[:], along(vch[:], 2, sh), along(vch[:], 3, sh), ALU.is_gt))
                step(tt(e_eq[:], along(vch[:], 2, sh), along(vch[:], 3, sh), ALU.is_equal))
                step(tt(e_eq[:], e_eq[:], lower(E), ALU.mult))
                step(tt(e_gt[:], e_gt[:], e_eq[:], ALU.add))
                step(nc.vector.reduce_sum(rank_e[:], e_gt[:], AX_X))
                step(nc.vector.scalar_tensor_tensor(wsel[:], rank_e[:], 4.0, sc[:], ALU.is_lt, ALU.mult))
                step(nc.vector.reduce_sum(winv[:], wsel[:], AX_X))
                step(nc.vector.tensor_scalar(winv[:], winv[:], 1e-20, 1.0 / ROUTE_SCALE, ALU.add, ALU.mult))
                step(nc.vector.reciprocal(winv[:], winv[:]))
                step(tt(cw[:], wsel[:], along(winv[:], 2, [P, TB, E]), ALU.mult))
                dve.wait_ge(ct_ps, n)
                step(nc.vector.tensor_scalar(cwc[:, :, 0:E].bitcast(F32R), cw[:], 1.0, None, ALU.mult))
                step(tt(cwc[:, :, E:2 * E], cw[:], cwc[:, :, 0:E], ALU.subtract))

        def weights_in(n, slot):
            dve.wait_ge(ct_ps, n + 1)
            if not (isinstance(n, int) and n == 0):
                dve.wait_ge(cb_ps, 1 + NE1 * (n - 1))
            nc.vector.tensor_copy(cwt[:, slot, :], PM[0:NR, :]).then_inc(misc_free, 1)

        def product(k, i):
            m = PER * k + i
            dve.wait_ge(sg_s, m + 1)
            nc.vector.tensor_tensor(sg[:, i % R, :], PU[i % RG][:], sg[:, i % R, :], ALU.mult).then_inc(gu_free, 1)
            dve.wait_ge(gu_free, m + RG + 1)
            dve.wait_ge(cb_ps, 1 + m + 1)
            dve.wait_ge(hl_done, m + 1)
            nc.vector.tensor_tensor(sg[:, i % R, :], PC[:], sg[:, i % R, :], ALU.mult).then_inc(h_done, 1)

        def residual(n):
            for pr in range(2):
                if pr == 0:
                    dve.wait_ge(y_ps, n + 1)
                else:
                    dve.wait_ge(hid_free, NE1 * (n + 1) + R)
                xs = x1[:, bass.ds(n * TB + 2 * pr, 2), :]
                nc.vector.scalar_tensor_tensor(xs, PY[pr][:].rearrange("p (t d) -> p t d", t=2), tg[:, 1:2], xs,
                                               ALU.mult, ALU.add).then_inc(fin_s, 1)

        def item(k, i, last):
            n, e, ahead = place(k, i, last)
            slot = (i // NE1 + 1) % 2
            product(k, i)
            if ahead and e == 7:
                weights_in(n + 1, slot)
            if e == 1 and i >= NE1:
                residual(n - 1)
            if not last and e == NE1 - 1:
                norm_stats(n + 2)
            if ahead and e == 0:
                normalised(n + 1)
            if ahead and e in (1, 2):
                x_lo(n + 1, slot, (e - 1,))
            if ahead and e == 3:
                router_out(n + 1)
            if ahead and e in (5, 6):
                routing(n + 1, e - 5)

        norm_stats(0)
        normalised(0)
        norm_stats(1)
        attend_reciprocals()
        for e in range(NE1):
            dve.wait_ge(w_hi, e + 1)
            nc.vector.tensor_tensor(wxl[:, e, :], wx[:, e, :], wxh[:, e, :], ALU.subtract).then_inc(w_lo, 1)
            if e == 0:
                x_lo(0, 0)
            if e == 2:
                router_out(0)
            if e == 3:
                routing(0, 0)
                routing(0, 1)
                attend_divide()
            if e == 4:
                weights_in(0, 0)
            if e == 5:
                attend_residual()
        turns(dve, item)
        residual(NBLK - 1)

    @block.tensor
    def _(pe):
        attend_finish = attend_tensor(pe)
        exp_done(pe)
        pe.sem_inc(hid_free, R)
        pe.sem_inc(gu_ps, 1)
        pe.sem_inc(cb_ps, 1)
        pe.wait_ge(tab_s, 3)
        ident = con("ident")
        pe.wait_ge(gst_s, 3)

        def split3(a, b):
            return ((a[0], b[1]), (a[1], b[0]), (a[0], b[0]))

        def transposes(n, chunks=range(C)):
            for c in chunks:
                pe.wait_ge(misc_free, 4 * n + c + 1)
                if c == 0:
                    pe.wait_ge(xn_s, TB * (n + 1))
                for j in range(TB):
                    last = nc.tensor.transpose(PM[:, j * P:(j + 1) * P], xn[:, j, c * P:(c + 1) * P], ident)
                last.then_inc(t_ps, 1)

        def router(n, slot):
            pe.wait_ge(misc_free, 4 * n + 3)
            for c in range(C):
                for k, xa in enumerate((xl, xh)):
                    last = nc.tensor.matmul(PM[:], gst[:, c, :], xa[:, slot, c, :], start=(c == 0 and k == 0),
                                            stop=(c == C - 1 and k == 1))
            last.then_inc(gl_ps, 1)

        def logits(n):
            pe.wait_ge(misc_free, 4 * n + 4)
            for j in range(TB):
                last = nc.tensor.matmul(PM[:, j * E:(j + 1) * E], lgT[:, j * P:(j + 1) * P],
                                        con("expert", 0, 2 * E)[:, 0:E], start=True, stop=True)
            last.then_inc(lg_ps, 1)

        def weights_T(n):
            pe.wait_ge(sc_s, n + 1)
            pe.wait_ge(route, NROUTE * (n + 1))
            for j in range(TB):
                last = nc.tensor.transpose(PM[0:NR, j * P:(j + 1) * P], cwc[:, j, :], ident)
            last.then_inc(ct_ps, 1)

        def gate_up(k, i):
            m = PER * k + i
            u, e = divmod(i % PER, NE1)
            pe.wait_ge(gu_free, m + 1)
            pe.wait_ge(w_lo, e + 1)
            for o, out_ in ((0, PG[i % RG]), (C * I, PU[i % RG])):
                first = True
                for c in range(C):
                    w = slice(o + c * I, o + (c + 1) * I)
                    for wa, xa in split3((wxh, wxl), (xh, xl)):
                        last = nc.tensor.matmul(out_[:], wa[:, e, w], xa[:, u, c, :], start=first,
                                                stop=(c == C - 1 and wa is wxh and xa is xh))
                        first = False
            last.then_inc(gu_ps, 1)

        def weight(k, i):
            m = PER * k + i
            u, e = divmod(i % PER, NE1)
            pe.wait_ge(h_done, m + R)
            if e == 0:
                pe.wait_ge(misc_free, 4 * (2 * k + i // NE1 + 1) + 1)
            nc.tensor.matmul(PC[:], selr[:, e, :], cwt[:, u, :], start=True, stop=True).then_inc(cb_ps, 1)

        def down(k, i):
            m = PER * k + i
            n, e = 2 * k + i // NE1, i % NE1
            pe.wait_ge(hl_done, m + R + 1)
            if e == 0:
                pe.wait_ge(fin_s, 2 * n)
            for j in range(TB):
                q = slice(j * P, (j + 1) * P)
                y = PY[j // 2][:, (j % 2) * D:(j % 2 + 1) * D]
                for s, (ha, wa) in enumerate(split3((hh, hl), (wxh, wxl))):
                    last = nc.tensor.matmul(y, ha[:, i % R, q], wa[:, e, 2 * C * I:XW],
                                            start=(e == 0 and s == 0 and j % 2 == 0), stop=(e == NE1 - 1 and s == 2),
                                            skip_group_check=True)
                if j == TB - 1:
                    last.then_inc(hid_free, 1)
                elif e == NE1 - 1 and j == 1:
                    last.then_inc(y_ps, 1)

        def item(k, i, last):
            n, e, ahead = place(k, i, last)
            if not (last and i + 2 >= PER):
                gate_up(k, i + 2)
            down(k, i)
            if not (last and i + 2 >= PER):
                weight(k, i + 2)
            if ahead and e in (0, 1):
                transposes(n + 1, (e,))
            if ahead and e == 2:
                router(n + 1, (i // NE1 + 1) % 2)
            if ahead and e == 3:
                logits(n + 1)
            if ahead and e == 6:
                weights_T(n + 1)

        transposes(0)
        router(0, 0)
        logits(0)
        raw_done(pe)
        gate_up(0, 0)
        gate_up(0, 1)
        weights_T(0)
        weight(0, 0)
        attend_finish()
        weight(0, 1)
        residual_done(pe)
        turns(pe, item)


def program(nc, t, out):
    with ExitStack() as outer:
        x1 = outer.enter_context(nc.sbuf_tensor("x1", [P, B * NT, D], F32))
        tg = outer.enter_context(nc.sbuf_tensor("tg", [P, 2], F32))
        with ExitStack() as ctx:
            attend = attention(nc, outer, ctx, x1, tg, t)
        experts(nc, outer, x1, tg, t, out, attend)


def kernel(x, ctx_1024, g_xattn, g_ffn, L0_xattn_Wk, L0_xattn_Wv, L0_xattn_Wq, L0_xattn_Wo, L0_xattn_p_params,
           L0_ffn_gate_w, L0_ffn_correction_bias, L0_ffn_Wg, L0_ffn_Wu, L0_ffn_Wd, L0_ffn_Wg_s, L0_ffn_Wu_s,
           L0_ffn_Wd_s):
    from concourse import bacc
    from concourse.bass_utils import run_bass_kernel_spmd

    def rows(w):
        return w.reshape(C, P, -1).transpose(1, 0, 2)

    f = np.float32
    ctx_t = np.zeros((B, P, C, KPAD), f)
    ctx_t[..., :KL] = np.asarray(ctx_1024).transpose(0, 2, 1).reshape(B, C, P, KL).transpose(0, 2, 1, 3)
    wo = np.asarray(L0_xattn_Wo).T.reshape(2, 2, 4, HD, D)
    wx = np.zeros((P, NE1, 2 * C * I + D), f)
    for at, many, one in ((0, L0_ffn_Wg, L0_ffn_Wg_s), (C * I, L0_ffn_Wu, L0_ffn_Wu_s)):
        for e in range(NE1):
            w = np.asarray(many)[e] if e < E else np.asarray(one)
            wx[:, e, at:at + C * I] = rows(w).reshape(P, C * I)
    wx[:, :E, 2 * C * I:] = np.asarray(L0_ffn_Wd).transpose(1, 0, 2)
    wx[:, E, 2 * C * I:] = np.asarray(L0_ffn_Wd_s)
    arrays = {
        "x": np.asarray(x).reshape(B * S, D),
        "ctx": ctx_t,
        "cst": constants(),
        "rel": np.tile(np.asarray(L0_xattn_p_params), (P // HD, 1)),
        "gates": np.tile(np.concatenate([np.asarray(g_xattn), np.asarray(g_ffn)])[None], (P, 1)),
        "wq": rows(np.asarray(L0_xattn_Wq).T),
        "wk": np.tile(rows(np.asarray(L0_xattn_Wk).T).reshape(P, C, NSTK, 1, 32), (1, 1, 1, 3, 1))
              .reshape(P, C, NSTK, 96),
        "wv": rows(np.asarray(L0_xattn_Wv).T),
        "wo": wo.transpose(2, 0, 3, 1, 4).reshape(P, 2, D),
        "bias": np.tile(np.asarray(L0_ffn_correction_bias)[None], (P, 1)),
        "gw": rows(np.asarray(L0_ffn_gate_w).T),
        "wx": wx,
    }
    arrays = {"in_" + name: np.ascontiguousarray(a) for name, a in arrays.items()}
    nc = bacc.Bacc("TRN2", target_bir_lowering=False, num_devices=1)
    t = {name[3:]: nc.dram_tensor(name, a.shape, F32, kind="ExternalInput").ap() for name, a in arrays.items()}
    t["x"] = t["x"].rearrange("(b t p) d -> b p t d", b=B, p=P)
    out = nc.dram_tensor("out", (B * S, D), F32, kind="ExternalOutput").ap()
    program(nc, t, out.rearrange("(n t p) d -> n p t d", n=B * S // HALF, p=P))
    result = run_bass_kernel_spmd(nc, [arrays], core_ids=[0])
    return result.results[0]["out"].reshape(B, S, D)
```
